# Optimizing a Trainium2 kernel written in Bass

```python
import numpy as np
import jax
import jax.numpy as jnp

def _softmax(x, axis=-1):
    return jax.nn.softmax(x, axis=axis)

def _gelu(x):
    return jax.nn.gelu(x, approximate=True)

def _silu(x):
    return jax.nn.silu(x)

def _sigmoid(x):
    return jax.nn.sigmoid(x)

def _layernorm(x, axis=-1, eps=1e-05):
    m = jnp.mean(x, axis=axis, keepdims=True)
    v = jnp.var(x, axis=axis, keepdims=True)
    return (x - m) / jnp.sqrt(v + eps)

def _scatter_add(tgt, idx, src, axis=0):
    return tgt.at[idx].add(src)

def _segment_sum(src, seg, n):
    return jax.ops.segment_sum(src, seg, n)
kernel_name = 'mk_prb_d2_jaxref_r8_2c4117'

def setup_inputs(seed: int=0):
    np.random.seed(seed)
    _w = jnp.asarray

    def _L0_attn_setup():
        import jax, jax.numpy as jnp
        import numpy as np
        DIM = 128
        STATE = 64
        KW = 4
        EXPAND = 2
        INNER = DIM * EXPAND
        BATCH = 2
        SEQ = 256
        EPS = 1e-06

        def _ssm_scan(xc, A_log, B_w, C_w, D_param, dt_w, dt_b):
            A = -jnp.exp(A_log)
            Bx = xc @ B_w.T
            Cx = xc @ C_w.T
            dt = jax.nn.softplus(xc @ dt_w.T + dt_b) + 0.0001

            def step(h, inp):
                dt_t, Bx_t, Cx_t, x_t = inp
                dA = jnp.exp(dt_t[..., None] * A)
                h = dA * h + (dt_t * x_t)[..., None] * Bx_t[:, None, :]
                y = jnp.einsum('bdn,bn->bd', h, Cx_t) + D_param * x_t
                return (h, y)
            h0 = jnp.zeros((xc.shape[0], INNER, STATE), dtype=jnp.float32)
            seq_inputs = tuple((jnp.moveaxis(a, 1, 0) for a in (dt, Bx, Cx, xc)))
            _, ys = jax.lax.scan(step, h0, seq_inputs)
            return jnp.moveaxis(ys, 0, 1)
        key = jax.random.key(seed)
        ks = jax.random.split(key, 8)
        rn = lambda k, shape, scale: jax.random.normal(k, shape, dtype=jnp.float32) * scale
        x = jax.random.normal(ks[0], (BATCH, SEQ, DIM), dtype=jnp.float32)
        in_proj_w = rn(ks[1], (2 * INNER, DIM), DIM ** (-0.5))
        conv_w = rn(ks[2], (INNER, 1, KW), 0.5)
        conv_b = jnp.zeros((INNER,), dtype=jnp.float32)
        A_log = jnp.tile(jnp.log(jnp.arange(1, STATE + 1, dtype=jnp.float32))[None, :], (INNER, 1))
        B_w = rn(ks[3], (STATE, INNER), INNER ** (-0.5))
        C_w = rn(ks[4], (STATE, INNER), INNER ** (-0.5))
        D_param = jnp.ones((INNER,), dtype=jnp.float32)
        dt_w = rn(ks[5], (INNER, INNER), 0.01 * INNER ** (-0.5))
        dt_b = jnp.full((INNER,), -3.0, dtype=jnp.float32)
        out_proj_w = rn(ks[6], (DIM, INNER), INNER ** (-0.5))
        norm_w = jnp.ones((DIM,), dtype=jnp.float32)
        return dict(x=x, in_proj_w=in_proj_w, conv_w=conv_w, conv_b=conv_b, A_log=A_log, B_w=B_w, C_w=C_w, D_param=D_param, dt_w=dt_w, dt_b=dt_b, out_proj_w=out_proj_w, norm_w=norm_w)
    _L0_attn_in = _L0_attn_setup()

    def _L0_ffn_setup():
        import jax, jax.numpy as jnp
        import numpy as np
        H = 128
        I = 512
        E = 8
        K = 2
        B, S = (2, 256)

        def _moe_linear(x, router_w, expert_w):
            n_exp = router_w.shape[0]
            logits = x @ router_w.T
            vals, idx = jax.lax.top_k(logits, K)
            probs = jax.nn.softmax(vals, axis=-1)
            onehot = jax.nn.one_hot(idx, n_exp, dtype=x.dtype)
            combine = jnp.einsum('tk,tke->te', probs, onehot)
            out = jnp.zeros((x.shape[0], expert_w.shape[1]), x.dtype)
            for e in range(n_exp):
                out = out + combine[:, e:e + 1] * (x @ expert_w[e].T)
            return out
        key = jax.random.key(seed)
        ks = jax.random.split(key, 7)
        init = lambda k, shape, fan_in: jax.random.normal(k, shape, jnp.float32) / np.float32(np.sqrt(fan_in))
        return {'x': jax.random.normal(ks[0], (B, S, H), jnp.float32), 'router_gate': init(ks[1], (E, H), H), 'w_gate': init(ks[2], (E, I, H), H), 'router_up': init(ks[3], (E, H), H), 'w_up': init(ks[4], (E, I, H), H), 'router_down': init(ks[5], (E, I), I), 'w_down': init(ks[6], (E, H, I), I)}
    _L0_ffn_in = _L0_ffn_setup()

    def _L1_attn_setup():
        import jax, jax.numpy as jnp
        import numpy as np
        N_EMBD = 128
        N_HEAD = 16
        HEAD_SIZE = 64
        LN_EPS = 0.001
        key = jax.random.key(seed)
        ks = jax.random.split(key, 7)
        B, S, D, H, E = (4, 256, N_EMBD, N_HEAD, HEAD_SIZE)
        x = jax.random.normal(ks[0], (B, S, D), dtype=jnp.float32)
        scale = 1.0 / np.sqrt(D)
        Wq = jax.random.normal(ks[1], (H, D, E), dtype=jnp.float32) * scale
        Wk = jax.random.normal(ks[2], (H, D, E), dtype=jnp.float32) * scale
        Wv = jax.random.normal(ks[3], (H, D, E), dtype=jnp.float32) * scale
        Wo = jax.random.normal(ks[4], (H * E, D), dtype=jnp.float32) * scale
        gamma = jnp.ones((D,), dtype=jnp.float32)
        beta = jnp.zeros((D,), dtype=jnp.float32)
        return {'x': x, 'Wq': Wq, 'Wk': Wk, 'Wv': Wv, 'Wo': Wo, 'gamma': gamma, 'beta': beta}
    _L1_attn_in = _L1_attn_setup()

    def _L1_ffn_setup():
        import jax, jax.numpy as jnp
        import numpy as np
        EPS = 1e-08

        def _ternary_linear(x, w):
            alpha = jnp.mean(jnp.abs(w))
            w_t = jnp.sign(w) * (jnp.abs(w) > 0.5 * alpha).astype(w.dtype)
            w_q = w + jax.lax.stop_gradient(w_t - w)
            d = x.shape[-1]
            rms = jnp.sqrt(jnp.sum(x * x, axis=-1, keepdims=True)) / jnp.sqrt(jnp.asarray(d, x.dtype))
            x_norm = x / (rms + EPS)
            return jnp.einsum('bsd,fd->bsf', x_norm, w_q)
        key = jax.random.key(seed)
        k1, k2, k3 = jax.random.split(key, 3)
        d_model, d_ff = (128, 512)
        B, S = (4, 512)
        x = jax.random.normal(k1, (B, S, d_model), dtype=jnp.float32)
        w_up = jax.random.normal(k2, (d_ff, d_model), dtype=jnp.float32) * 0.02
        w_down = jax.random.normal(k3, (d_model, d_ff), dtype=jnp.float32) * 0.02
        return {'x': x, 'w_up': w_up, 'w_down': w_down}
    _L1_ffn_in = _L1_ffn_setup()
    _d = {'L0_attn_x': _L0_attn_in['x'], 'L0_attn_in_proj_w': _L0_attn_in['in_proj_w'], 'L0_attn_conv_w': _L0_attn_in['conv_w'], 'L0_attn_conv_b': _L0_attn_in['conv_b'], 'L0_attn_A_log': _L0_attn_in['A_log'], 'L0_attn_B_w': _L0_attn_in['B_w'], 'L0_attn_C_w': _L0_attn_in['C_w'], 'L0_attn_D_param': _L0_attn_in['D_param'], 'L0_attn_dt_w': _L0_attn_in['dt_w'], 'L0_attn_dt_b': _L0_attn_in['dt_b'], 'L0_attn_out_proj_w': _L0_attn_in['out_proj_w'], 'L0_attn_norm_w': _L0_attn_in['norm_w'], 'L0_ffn_router_gate': _L0_ffn_in['router_gate'], 'L0_ffn_w_gate': _L0_ffn_in['w_gate'], 'L0_ffn_router_up': _L0_ffn_in['router_up'], 'L0_ffn_w_up': _L0_ffn_in['w_up'], 'L0_ffn_router_down': _L0_ffn_in['router_down'], 'L0_ffn_w_down': _L0_ffn_in['w_down'], 'L1_attn_Wq': _L1_attn_in['Wq'], 'L1_attn_Wk': _L1_attn_in['Wk'], 'L1_attn_Wv': _L1_attn_in['Wv'], 'L1_attn_Wo': _L1_attn_in['Wo'], 'L1_attn_gamma': _L1_attn_in['gamma'], 'L1_attn_beta': _L1_attn_in['beta'], 'L1_ffn_w_up': _L1_ffn_in['w_up'], 'L1_ffn_w_down': _L1_ffn_in['w_down']}
    _x0 = _d['L0_attn_x']
    _d['L0_attn_x'] = jax.random.normal(jax.random.fold_in(jax.random.key(seed), 1), (2, 1024, 128), dtype=_x0.dtype)
    del _x0
    return _d

def reference(L0_attn_x, L0_attn_in_proj_w, L0_attn_conv_w, L0_attn_conv_b, L0_attn_A_log, L0_attn_B_w, L0_attn_C_w, L0_attn_D_param, L0_attn_dt_w, L0_attn_dt_b, L0_attn_out_proj_w, L0_attn_norm_w, L0_ffn_router_gate, L0_ffn_w_gate, L0_ffn_router_up, L0_ffn_w_up, L0_ffn_router_down, L0_ffn_w_down, L1_attn_Wq, L1_attn_Wk, L1_attn_Wv, L1_attn_Wo, L1_attn_gamma, L1_attn_beta, L1_ffn_w_up, L1_ffn_w_down):

    def _L0_attn_ref(x, in_proj_w, conv_w, conv_b, A_log, B_w, C_w, D_param, dt_w, dt_b, out_proj_w, norm_w):
        import jax, jax.numpy as jnp
        import numpy as np
        DIM = 128
        STATE = 64
        KW = 4
        EXPAND = 2
        INNER = DIM * EXPAND
        BATCH = 2
        SEQ = 256
        EPS = 1e-06

        def _ssm_scan(xc, A_log, B_w, C_w, D_param, dt_w, dt_b):
            A = -jnp.exp(A_log)
            Bx = xc @ B_w.T
            Cx = xc @ C_w.T
            dt = jax.nn.softplus(xc @ dt_w.T + dt_b) + 0.0001

            def step(h, inp):
                dt_t, Bx_t, Cx_t, x_t = inp
                dA = jnp.exp(dt_t[..., None] * A)
                h = dA * h + (dt_t * x_t)[..., None] * Bx_t[:, None, :]
                y = jnp.einsum('bdn,bn->bd', h, Cx_t) + D_param * x_t
                return (h, y)
            h0 = jnp.zeros((xc.shape[0], INNER, STATE), dtype=jnp.float32)
            seq_inputs = tuple((jnp.moveaxis(a, 1, 0) for a in (dt, Bx, Cx, xc)))
            _, ys = jax.lax.scan(step, h0, seq_inputs)
            return jnp.moveaxis(ys, 0, 1)
        residual = x
        xn = x * jax.lax.rsqrt(jnp.mean(x * x, axis=-1, keepdims=True) + EPS) * norm_w
        xz = xn @ in_proj_w.T
        xc, z = jnp.split(xz, 2, axis=-1)
        xt = jnp.transpose(xc, (0, 2, 1))
        xt = jax.lax.conv_general_dilated(xt, conv_w, window_strides=(1,), padding=[(KW - 1, 0)], feature_group_count=INNER, dimension_numbers=('NCH', 'OIH', 'NCH'))
        xt = xt + conv_b[None, :, None]
        xc = jax.nn.silu(jnp.transpose(xt, (0, 2, 1)))
        y = _ssm_scan(xc, A_log, B_w, C_w, D_param, dt_w, dt_b)
        y = y * jax.nn.silu(z)
        return y @ out_proj_w.T + residual

    def _L0_ffn_ref(x, router_gate, w_gate, router_up, w_up, router_down, w_down):
        import jax, jax.numpy as jnp
        import numpy as np
        H = 128
        I = 512
        E = 8
        K = 2
        B, S = (2, 256)

        def _moe_linear(x, router_w, expert_w):
            n_exp = router_w.shape[0]
            logits = x @ router_w.T
            vals, idx = jax.lax.top_k(logits, K)
            probs = jax.nn.softmax(vals, axis=-1)
            onehot = jax.nn.one_hot(idx, n_exp, dtype=x.dtype)
            combine = jnp.einsum('tk,tke->te', probs, onehot)
            out = jnp.zeros((x.shape[0], expert_w.shape[1]), x.dtype)
            for e in range(n_exp):
                out = out + combine[:, e:e + 1] * (x @ expert_w[e].T)
            return out
        b, s, h = x.shape
        xt = x.reshape(b * s, h)
        g = _moe_linear(xt, router_gate, w_gate)
        u = _moe_linear(xt, router_up, w_up)
        inter = jax.nn.silu(g) * u
        d = _moe_linear(inter, router_down, w_down)
        return d.reshape(b, s, h)

    def _L1_attn_ref(x, Wq, Wk, Wv, Wo, gamma, beta):
        import jax, jax.numpy as jnp
        import numpy as np
        N_EMBD = 128
        N_HEAD = 16
        HEAD_SIZE = 64
        LN_EPS = 0.001
        B, S, D = x.shape
        H, _, E = Wq.shape
        q = jnp.einsum('bsd,hde->bhse', x, Wq)
        k = jnp.einsum('bsd,hde->bhse', x, Wk)
        v = jnp.einsum('bsd,hde->bhse', x, Wv)
        scores = jnp.einsum('bhse,bhte->bhst', q, k)
        causal = jnp.tril(jnp.ones((S, S), dtype=bool))
        scores = jnp.where(causal, scores / jnp.sqrt(jnp.float32(E)), jnp.float32(-jnp.inf))
        attn = jax.nn.softmax(scores, axis=-1)
        out = jnp.einsum('bhst,bhte->bhse', attn, v)
        heads = out.transpose(0, 2, 1, 3).reshape(B, S, H * E)
        y = x + heads @ Wo
        mu = jnp.mean(y, axis=-1, keepdims=True)
        var = jnp.mean(jnp.square(y - mu), axis=-1, keepdims=True)
        y = (y - mu) * jax.lax.rsqrt(var + LN_EPS) * gamma + beta
        return y

    def _L1_ffn_ref(x, w_up, w_down):
        import jax, jax.numpy as jnp
        import numpy as np
        EPS = 1e-08

        def _ternary_linear(x, w):
            alpha = jnp.mean(jnp.abs(w))
            w_t = jnp.sign(w) * (jnp.abs(w) > 0.5 * alpha).astype(w.dtype)
            w_q = w + jax.lax.stop_gradient(w_t - w)
            d = x.shape[-1]
            rms = jnp.sqrt(jnp.sum(x * x, axis=-1, keepdims=True)) / jnp.sqrt(jnp.asarray(d, x.dtype))
            x_norm = x / (rms + EPS)
            return jnp.einsum('bsd,fd->bsf', x_norm, w_q)
        h = jax.nn.gelu(_ternary_linear(x, w_up), approximate=False)
        return _ternary_linear(h, w_down)
    x = L0_attn_x
    xn = _layernorm(x, axis=-1)
    x = x + _L0_attn_ref(xn, L0_attn_in_proj_w, L0_attn_conv_w, L0_attn_conv_b, L0_attn_A_log, L0_attn_B_w, L0_attn_C_w, L0_attn_D_param, L0_attn_dt_w, L0_attn_dt_b, L0_attn_out_proj_w, L0_attn_norm_w) + _L0_ffn_ref(xn, L0_ffn_router_gate, L0_ffn_w_gate, L0_ffn_router_up, L0_ffn_w_up, L0_ffn_router_down, L0_ffn_w_down)
    xn = _layernorm(x, axis=-1)
    x = x + _L1_attn_ref(xn, L1_attn_Wq, L1_attn_Wk, L1_attn_Wv, L1_attn_Wo, L1_attn_gamma, L1_attn_beta) + _L1_ffn_ref(xn, L1_ffn_w_up, L1_ffn_w_down)
    return x

_drawn_inputs = setup_inputs


def setup_inputs(seed=0):
    import zlib

    import numpy as np

    out = dict(_drawn_inputs(seed))
    spreads = {'L0_attn_conv_b': (0.0, 0.368),
     'L0_attn_D_param': (1.0, 0.2),
     'L0_attn_dt_b': (-3.0, 0.6),
     'L0_attn_norm_w': (1.0, 0.2),
     'L1_attn_gamma': (1.0, 0.6),
     'L1_attn_beta': (0.0, 0.8)}
    factors = {'L0_attn_dt_w': 64.0,
     'L1_attn_Wq': 3.333,
     'L1_attn_Wk': 3.352,
     'L1_attn_Wv': 2.893,
     'L1_attn_Wo': 2.875}
    for name, (base, spread) in spreads.items():
        noise = np.random.default_rng([zlib.crc32(name.encode()), seed]).standard_normal(out[name].shape)
        drawn = base * np.exp(spread * noise) if base else spread * noise
        out[name] = jnp.asarray(drawn.astype(out[name].dtype))
    for name, factor in factors.items():
        out[name] = (out[name] * factor).astype(out[name].dtype)
    return out
```

```python
import numpy as np
import concourse.bass as bass
from concourse import mybir
from collections import namedtuple
from contextlib import ExitStack

FP32 = mybir.dt.float32
BF16 = mybir.dt.bfloat16
U32 = mybir.dt.uint32
ALU = mybir.AluOpType
ACT = mybir.ActivationFunctionType
AX = mybir.AxisListType

P = 128
B, S, D = 2, 1024, 128
T = B * S
NT = T // P
BLK = 512
INNER, STATE, KW = 256, 64, 4
DH = INNER // P
E, FF = 8, 512
KC = FF // P
H, HS = 16, 64
HP = H // 2
QT = S // P
EPS_LN, EPS_RMS, EPS_LN2, EPS_T = 1e-5, 1e-6, 1e-3, 1e-8
UN = 16
UNITS = STATE // UN
NEG = -1.0e30
V_NORM, V_CB, V_DTB, V_D = 0, 1, 1 + DH, 1 + 2 * DH
V_CW = 1 + 3 * DH
V_A = V_CW + DH * KW
VECS = V_A + DH * STATE


class Memory:
    pass


def prepare(nc, d, m, ps):
    with ExitStack() as ctx:
        sb = lambda n, s, t=FP32: ctx.enter_context(nc.sbuf_tensor(n, s, t))
        sem = lambda n: ctx.enter_context(nc.semaphore(n))
        X = sb("X", [P, NT, D])
        XR = sb("XR", [P, NT, D])
        xrT = m.dt[:, 0, :]
        cv = m.dt[:, 1, :].rearrange("p (a s) -> p a s", a=2)
        XP = m.u_mem[:, :].rearrange("p (a s) -> p a s", s=KW - 1 + S)
        bc_p = [XR[:, 8 * i:8 * i + 8, :].rearrange("p a h -> p (a h)").bitcast(BF16) for i in range(2)] + \
               [X[:, 0:8, :].rearrange("p a h -> p (a h)").bitcast(BF16)]
        xc = sb("xc", [P, DH, T])
        sz = sb("sz", [P, DH, T])
        mv = sb("mv", [P, NT, 2])
        st6 = sb("st6", [P, NT, 6])
        rr = sb("rr", [P, 2, NT])
        rstd, rms = rr[:, 0, :], rr[:, 1, :]
        w_inT = sb("w_inT", [P, 4 * P])
        w_bcT = sb("w_bcT", [P, DH, P])
        w_dtT = sb("w_dtT", [P, DH, INNER])
        w_rT = sb("w_rT", [P, 2 * E])
        vec = sb("vec", [P, VECS])
        norm_w, conv_b, dt_b = vec[:, V_NORM:V_NORM + 1], vec[:, V_CB:V_CB + DH], vec[:, V_DTB:V_DTB + DH]
        conv_w = vec[:, V_CW:V_CW + DH * KW].rearrange("p (c k) -> p c k", c=DH)
        xn = sb("xn", [P, NT, D])
        two = lambda x: x.rearrange("p a h -> p (a h)").rearrange("p (r t) -> p r t", r=2)
        ab, rl, res = two(xn[:, 0:8, :]), two(xn[:, 8:16, :]), two(X[:, 8:16, :])
        L = sb("L", [P, NT * 2, E])
        top = sb("top", [P, NT * 2, E])
        idx = sb("idx", [P, NT * 2, E], U32)
        idf = sb("idf", [P, NT * 2, 2])
        dif = sb("dif", [P, NT * 2])
        pr = sb("pr", [P, NT * 2, 2])
        oh = sb("oh", [P, 2, NT * 2, E])
        cT = sb("cT", [P, 2, P])

        ld_x, ld_w, ld_e, ld_s, ld_c = sem("ld_x"), sem("ld_w"), sem("ld_e"), sem("ld_s"), sem("ld_c")
        consts = sem("p_consts")
        rr_in, rr_sqrt = sem("rr_in"), sem("rr_sqrt")
        v = sem("p_dve")
        a = sem("p_act")
        ln_done, xn_T, tok_T = sem("ln_done"), sem("xn_T"), sem("tok_T")
        zx_mm, xc_in, xc_done, z_done = sem("zx_mm"), sem("xc_in"), sem("xc_done"), sem("z_done")
        cv_ready, mm_dt, mm_bc, sp_abs, sp_rel, sp_ln, dt_done = [sem(n) for n in (
            "cv_ready", "mm_dt", "mm_bc", "sp_abs", "sp_rel", "sp_ln", "dt_done")]
        bc_hi, bc_done, rt_mm, rt_dif, rt_exp, cb_done, cb_T, cb_cp, cb_out, pt_out, lg = [sem(n) for n in (
            "bc_hi", "bc_done", "rt_mm", "rt_dif", "rt_exp", "cb_done", "cb_T", "cb_cp", "cb_out", "pt_out", "lg")]

        block = ctx.enter_context(nc.Block())

        @block.sync
        def _(sp):
            for h in range(4):
                sp.dma_start(X[:, 4 * h:4 * h + 4, :], d.x[:, 4 * h:4 * h + 4, :]).then_inc(ld_x, 16)
            sp.dma_start(m.ident[:, :], d.ident).then_inc(ld_c, 16)
            sp.dma_start(vec[:, :], d.vec).then_inc(ld_s, 16)
            sp.dma_start(w_inT[:, :], d.w_inT).then_inc(ld_w, 16)
            sp.dma_start(w_rT[:, :], d.w_rT).then_inc(ld_w, 16)
            sp.dma_start(w_bcT[:, :, :], d.w_bcT).then_inc(ld_w, 16)
            sp.dma_start(w_dtT[:, :, :], d.w_dtT).then_inc(ld_w, 16)
            sp.dma_start(m.iota8[:, :], d.iota8).then_inc(ld_w, 16)
            sp.dma_start(m.w_rdT[:, :, :], d.w_rdT).then_inc(ld_e, 16)
            sp.dma_start(m.sel[:, :, :, :], d.sel).then_inc(ld_e, 16)
            for g in range(2):
                sp.dma_start(m.wT[g][:, :, :], (d.w_gT, d.w_uT)[g]).then_inc(ld_e, 16)
            sp.dma_start(m.w_dnT[:, :, :, :], d.w_dnT).then_inc(ld_e, 16)
            sp.wait_ge(xc_done, 4)
            sp.dma_start(m.xc_dram, xc[:, :, :]).then_inc(cb_out, 16)
            sp.wait_ge(z_done, 8)
            sp.dma_start(m.sz_dram, sz[:, :, :]).then_inc(cb_out, 16)
            sp.wait_ge(cb_cp, 1)
            sp.dma_start(m.comb_dram.rearrange("(g t) e n -> (t e) g n", g=2), cT[:, :, :]).then_inc(cb_out, 16)
            sp.wait_ge(bc_done, 4)
            for q in range(2):
                for part in range(3):
                    for ic in range(UNITS):
                        r0 = q * STATE + ic * UN
                        o0 = q * 48 + part * UN
                        sp.dma_start(m.PT[o0:o0 + UN, ic:UNITS * B * 2:UNITS, :],
                                     bc_p[part][r0:r0 + UN, :].rearrange("p (k t) -> p k t", t=BLK)).then_inc(pt_out, 16)
            sp.wait_ge(pt_out, 16 * 6 * UNITS)
            sp.wait_ge(cb_out, 48)
            sp.wait_ge(ld_e, 80)

        @block.gpsimd
        def _(pool):
            nc.gpsimd.memset(XP[:, :, 0:KW - 1], 0.0).then_inc(consts, 1)
            nc.gpsimd.memset(m.zeros[:, :], 0.0)
            nc.gpsimd.memset(m.PT[:, UNITS * B * 2, :], 0.0)

        @block.scalar
        def _(act):
            own = 0
            act.wait_ge(ld_s, 16)
            A_log = vec[:, V_A:V_A + DH * STATE].rearrange("p (c n) -> p c n", c=DH)
            nc.scalar.activation(m.A[:, :, :], A_log, ACT.Exp).then_inc(a, 1)
            act.wait_ge(a, 1)
            nc.scalar.mul(m.A[:, :, :], m.A[:, :, :], -1.0).then_inc(a, 1)
            act.wait_ge(rr_in, 1)
            nc.scalar.activation(rr[:, :, :], rr[:, :, :], ACT.Sqrt).then_inc(rr_sqrt, 1)
            for blk in range(4):
                for c in range(2):
                    act.wait_ge(zx_mm, 4 * blk + c + 1)
                    b, t0 = blk // 2, (blk % 2) * BLK
                    nc.scalar.copy(XP[:, c * B + b, KW - 1 + t0:KW - 1 + t0 + BLK], ps[4 + c][:, :]).then_inc(xc_in, 1)
                for c in range(2):
                    act.wait_ge(zx_mm, 4 * blk + 2 + c + 1)
                    nc.scalar.activation(sz[:, c, blk * BLK:(blk + 1) * BLK], ps[6 + c][:, :], ACT.Silu).then_inc(z_done, 1)
            for c in range(DH):
                for b in range(B):
                    i = c * B + b
                    act.wait_ge(cv_ready, i + 1)
                    nc.scalar.activation(xc[:, c, b * S:(b + 1) * S], cv[:, i % 2, :], ACT.Silu).then_inc(xc_done, 1)
            act.wait_ge(rt_dif, 1)
            nc.scalar.activation(dif[:, :], dif[:, :], ACT.Exp).then_inc(rt_exp, 1)
            i = 0
            for blk in range(4):
                act.wait_ge(mm_bc, blk + 1)
                nc.scalar.copy(bc_p[0][:, blk * BLK:(blk + 1) * BLK], ps[6 + blk % 2][:, :]).then_inc(bc_hi, 1)
                for o in range(DH):
                    act.wait_ge(mm_dt, i + 1)
                    if i >= 2:
                        act.wait_ge(dt_done, i - 1)
                    nc.scalar.activation(ab[:, i % 2, :], ps[4 + i % 2][:, :], ACT.Abs, bias=dt_b[:, o:o + 1]).then_inc(sp_abs, 1)
                    act.wait_ge(sp_abs, i + 1)
                    own += 1
                    nc.scalar.activation(ab[:, i % 2, :], ab[:, i % 2, :], ACT.Exp, scale=-1.0).then_inc(a, 1)
                    act.wait_ge(a, 2 + own)
                    nc.scalar.activation(ab[:, i % 2, :], ab[:, i % 2, :], ACT.Ln, bias=m.one[:, 0:1]).then_inc(sp_ln, 1)
                    i += 1

        @block.vector
        def _(dve):
            cnt = [0]

            def link(ins):
                cnt[0] += 1
                ins.then_inc(v, 1)
                dve.wait_ge(v, cnt[0])

            link(nc.vector.memset(m.one[:, :], 1.0))
            for t in range(NT):
                if t % 4 == 0:
                    dve.wait_ge(ld_x, 16 * 4)
                ins = nc.vector.bn_stats(st6[:, t, :], X[:, t, :])
            link(ins)
            for t in range(NT):
                ins = nc.vector.bn_aggr(mv[:, t, :], st6[:, t, :])
            link(ins)
            link(nc.vector.tensor_scalar(rr[:, 0, :], mv[:, :, 1], EPS_LN, None, ALU.add))
            link(nc.vector.reciprocal(rr[:, 1, :], rr[:, 0, :]))
            link(nc.vector.tensor_tensor(rr[:, 1, :], rr[:, 1, :], mv[:, :, 1], ALU.mult))
            nc.vector.tensor_scalar(rr[:, 1, :], rr[:, 1, :], EPS_RMS, None, ALU.add).then_inc(rr_in, 1)
            dve.wait_ge(rr_sqrt, 1)
            link(nc.vector.reciprocal(rr[:, :, :], rr[:, :, :]))
            for t in range(NT):
                ins = nc.vector.tensor_scalar(xn[:, t, :], X[:, t, :], mv[:, t, 0:1], rstd[:, t:t + 1], ALU.subtract, ALU.mult)
            link(ins)
            for t in range(NT):
                nc.vector.tensor_scalar(XR[:, t, :], xn[:, t, :], rms[:, t:t + 1], None, ALU.mult).then_inc(ln_done, 1)
            dve.wait_ge(ld_s, 16)
            nc.vector.tensor_copy(m.Dp[:, :], vec[:, V_D:V_D + DH])
            for q in range(4):
                dve.wait_ge(xn_T, 2 * q + 1)
                nc.vector.tensor_copy(m.xnT[:, q * BLK:(q + 1) * BLK], ps[4 + 2 * (q % 2)][:, :]).then_inc(tok_T, 1)
                dve.wait_ge(xn_T, 2 * q + 2)
                nc.vector.tensor_scalar(xrT[:, q * BLK:(q + 1) * BLK], ps[5 + 2 * (q % 2)][:, :], norm_w[:, 0:1], None, ALU.mult).then_inc(tok_T, 1)
            nc.vector.tensor_tensor(m.acc[:, :, :], X[:, :, :], xn[:, :, :], ALU.add).then_inc(lg, 1)
            dve.wait_ge(ld_w, 80)
            dve.wait_ge(rt_mm, 1)
            link(nc.vector.tensor_copy(L[:, :, :].rearrange("p a e -> p (a e)"), ps[3][:, 0:NT * 2 * E]))
            for r in range(NT * 2):
                ins = nc.vector.max(top[:, r, :], L[:, r, :])
            link(ins)
            nc.vector.tensor_tensor(dif[:, :], top[:, :, 1], top[:, :, 0], ALU.subtract).then_inc(rt_dif, 1)
            for r in range(NT * 2):
                ins = nc.vector.max_index(idx[:, r, :], top[:, r, :], L[:, r, :])
            link(ins)
            link(nc.vector.tensor_copy(idf[:, :, :], idx[:, :, 0:2]))
            for j in range(2):
                ins = nc.vector.tensor_tensor(oh[:, j, :, :], m.iota8[:, :].unsqueeze(1).to_broadcast([P, NT * 2, E]),
                                              idf[:, :, j:j + 1].to_broadcast([P, NT * 2, E]), ALU.is_equal)
            link(ins)
            n_x = 0
            for c in range(DH):
                for b in range(B):
                    i = c * B + b
                    dve.wait_ge(consts, 1)
                    dve.wait_ge(xc_in, 4 * b + 4)
                    if i >= 2:
                        dve.wait_ge(xc_done, i - 1)
                    link(nc.vector.tensor_scalar(cv[:, i % 2, :], XP[:, i, 0:S], conv_w[:, c, 0:1], conv_b[:, c:c + 1], ALU.mult, ALU.add))
                    for k in range(1, KW):
                        ins = nc.vector.scalar_tensor_tensor(cv[:, i % 2, :], XP[:, i, k:k + S], conv_w[:, c, k:k + 1], cv[:, i % 2, :], ALU.mult, ALU.add)
                        if k < KW - 1:
                            link(ins)
                    ins.then_inc(cv_ready, 1)
            dve.wait_ge(rt_exp, 1)
            link(nc.vector.tensor_scalar(pr[:, :, 0], dif[:, :], 1.0, None, ALU.add))
            link(nc.vector.reciprocal(pr[:, :, 0], pr[:, :, 0]))
            link(nc.vector.tensor_tensor(pr[:, :, 1], pr[:, :, 0], dif[:, :], ALU.mult))
            for j in range(2):
                link(nc.vector.tensor_tensor(oh[:, j, :, :], oh[:, j, :, :], pr[:, :, j:j + 1].to_broadcast([P, NT * 2, E]), ALU.mult))
            nc.vector.tensor_tensor(oh[:, 0, :, :], oh[:, 0, :, :], oh[:, 1, :, :], ALU.add).then_inc(cb_done, 1)
            dve.wait_ge(cb_T, 1)
            nc.vector.tensor_copy(cT[:, :, :].rearrange("p a n -> p (a n)"), ps[3][:, 0:2 * P]).then_inc(cb_cp, 1)
            i = 0
            for blk in range(4):
                c0 = slice(blk * BLK, (blk + 1) * BLK)
                dve.wait_ge(bc_hi, blk + 1)
                link(nc.vector.tensor_tensor(res[:, blk % 2, :], ps[6 + blk % 2][:, :], bc_p[0][:, c0], ALU.subtract))
                link(nc.vector.tensor_copy(bc_p[1][:, c0], res[:, blk % 2, :]))
                nc.vector.tensor_tensor(bc_p[2][:, c0], res[:, blk % 2, :], bc_p[1][:, c0], ALU.subtract).then_inc(bc_done, 1)
                for o in range(DH):
                    dve.wait_ge(sp_abs, i + 1)
                    link(nc.vector.tensor_scalar(rl[:, i % 2, :], ps[4 + i % 2][:, :], dt_b[:, o:o + 1], 0.0, ALU.add, ALU.max))
                    dve.wait_ge(sp_ln, i + 1)
                    nc.vector.scalar_tensor_tensor(m.dt[:, o, c0], ab[:, i % 2, :], 1e-4, rl[:, i % 2, :], ALU.add, ALU.add).then_inc(dt_done, 1)
                    dve.wait_ge(dt_done, i + 1)
                    dve.wait_ge(xc_done, 4)
                    nc.vector.tensor_tensor(m.u[:, o, c0], m.dt[:, o, c0], xc[:, o, c0], ALU.mult)
                    i += 1

        @block.tensor
        def _(pe):
            pe.wait_ge(ld_c, 16)
            for q in range(4):
                pe.wait_ge(ln_done, 4 * q + 4)
                for k, src in enumerate((xn, XR)):
                    if q >= 2:
                        pe.wait_ge(tok_T, 2 * (q - 2) + k + 1)
                    for j in range(4):
                        ins = nc.tensor.transpose(ps[4 + 2 * (q % 2) + k][:, j * P:(j + 1) * P], src[:, 4 * q + j, :], m.ident[:, :])
                    ins.then_inc(xn_T, 1)
            pe.wait_ge(ld_w, 80)
            pe.wait_ge(tok_T, 8)
            for blk in range(4):
                for c in range(4):
                    if blk:
                        pe.wait_ge(xc_in if c < 2 else z_done, 2 * (blk - 1) + c % 2 + 1)
                    nc.tensor.matmul(ps[4 + c][:, :], lhsT=w_inT[:, c * P:(c + 1) * P], rhs=xrT[:, blk * BLK:(blk + 1) * BLK],
                                     start=True, stop=True).then_inc(zx_mm, 1)
            for t in range(NT):
                ins = nc.tensor.matmul(ps[3][:, t * 2 * E:(t + 1) * 2 * E], lhsT=m.xnT[:, t * P:(t + 1) * P], rhs=w_rT[:, :],
                                       start=True, stop=True)
            ins.then_inc(rt_mm, 1)
            pe.wait_ge(cb_done, 1)
            for g in range(2):
                ins = nc.tensor.transpose(ps[3][:, g * P:(g + 1) * P],
                                          oh[:, 0, :, :].rearrange("p a e -> p (a e)")[:, g * P:(g + 1) * P], m.ident[:, :])
            ins.then_inc(cb_T, 1)
            pe.wait_ge(xc_done, 4)
            pe.wait_ge(z_done, 8)
            i = 0
            for blk in range(4):
                if blk >= 2:
                    pe.wait_ge(bc_done, blk - 1)
                for k in range(DH):
                    ins = nc.tensor.matmul(ps[6 + blk % 2][:, :], lhsT=w_bcT[:, k, :], rhs=xc[:, k, blk * BLK:(blk + 1) * BLK],
                                           start=(k == 0), stop=(k == DH - 1))
                ins.then_inc(mm_bc, 1)
                for o in range(DH):
                    if i >= 2:
                        pe.wait_ge(dt_done, i - 1)
                    for k in range(DH):
                        ins = nc.tensor.matmul(ps[4 + i % 2][:, :], lhsT=w_dtT[:, k, o * P:(o + 1) * P], rhs=xc[:, k, blk * BLK:(blk + 1) * BLK],
                                               start=(k == 0), stop=(k == DH - 1))
                    ins.then_inc(mm_dt, 1)
                    i += 1


def scan_and_experts(nc, d, m, ps):
    with ExitStack() as ctx:
        sb = lambda n, s, t=FP32: ctx.enter_context(nc.sbuf_tensor(n, s, t))
        sem = lambda n: ctx.enter_context(nc.semaphore(n))
        RA, RD, RH, RB = 4, 2, 2, 2
        Bs = sb("Bs", [P, RB, BLK])
        dA = sb("dA", [P, RA, DH, BLK])
        dBx = sb("dBx", [P, RD, DH, BLK])
        hh = sb("hh", [P, 2, DH, BLK])
        hC = sb("hC", [P, RH, DH, BLK])
        carry = sb("carry", [P, STATE, DH])
        cbb = sb("cbb", [P, 2 * E, P])
        xs = sb("xs", [P, 2 * E, P])
        yb = sb("yb", [P, 2, BLK])
        sg = sb("sg", [P, FF])
        gg = sb("gg", [P, FF])
        inter = sb("inter", [P, FF])
        interT = sb("interT", [P, KC, P])
        Ld = sb("Ld", [P, E])
        top = sb("topd", [P, E])
        idx = sb("idxd", [P, E], U32)
        idf = sb("idfd", [P, 2])
        dif = sb("difd", [P, 1])
        edif = sb("edif", [P, 1])
        pr = sb("prd", [P, 2])
        cd = sb("cd", [P, 2, E])

        psB, psC, psY, G, U = ps[0:2], ps[2:4], ps[4:6], ps[6], ps[7]
        s_psB, s_Bs, s_dA, s_dBx, s_psC, s_scan, s_hC, s_y, s_carry = [sem(n) for n in (
            "psB_full", "Bs_full", "dA_full", "dBx_full", "psC_full", "scanned", "hC_full", "y_added", "carried")]
        s_open, s_yout, s_cbb, s_xs, s_gate, s_up, s_tanh, s_gg, s_int, s_intT, s_intE, s_lg, s_lgc, s_dif, s_exp, s_dn0, s_dn1, s_cmb, s_q = [
            sem(n) for n in ("y_open", "y_out", "cbb_full", "xs_full", "gate_done", "up_done", "tanh_done", "gg_done",
                             "inter_done", "interT_mm", "interT_done", "logits_mm", "logits_out", "dif_done", "exp_done", "down0", "down1",
                             "combined", "dve_own")]
        s_zero, s_yst, s_at = sem("carry_zero"), sem("y_stored"), sem("reached")
        OFF = 4

        block = ctx.enter_context(nc.Block())

        def loops(eng, body, start_block, end_block):
            with eng.Fori(0, B, 1) as b:
                cb = b * (2 * STATE)
                with eng.Fori(0, 2, 1) as tc:
                    ct = tc * STATE
                    start_block(cb, ct)
                    with eng.Fori(0, UNITS, 1) as ic:
                        body(cb, ct, ic * UN)
                    end_block(cb, ct)

        nothing = lambda cb, ct: None

        @block.sync
        def _(sp):
            with sp.Fori(0, NT, 1) as q:
                sp.wait_ge(s_xs, OFF + q)
                sp.dma_start(cbb[:, :, :].rearrange("p e n -> p (e n)"),
                             m.comb_dram.rearrange("t e n -> t (e n)")[bass.ds(q, 1), :].to_broadcast([P, 2 * E * P])).then_inc(s_cbb, 16)

        @block.scalar
        def _(act):
            act.sem_inc(s_Bs, OFF)
            act.sem_inc(s_exp, 1)
            act.sem_inc(s_yst, 16)
            act.sem_inc(s_dA, OFF)

            def body(cb, ct, n0):
                N = cb + ct + n0
                t0 = (cb + ct) * 8
                q = N // UN
                for s in range(UN):
                    act.wait_ge(s_psB, N + (s + 1))
                    act.wait_ge(s_dBx, N + (OFF + s - RB + 1))
                    nc.scalar.copy(Bs[:, s % RB, :], psB[s % 2][:, :]).then_inc(s_Bs, 1)
                    act.wait_ge(s_scan, N + (OFF + s - RA + 1))
                    nc.scalar.activation(dA[:, s % RA, 0, :], m.dt[:, 0, bass.ds(t0, BLK)], ACT.Exp, scale=m.A[:, 0, bass.ds(n0 + s, 1)])
                    nc.scalar.activation(dA[:, s % RA, 1, :], m.dt[:, 1, bass.ds(t0, BLK)], ACT.Exp, scale=m.A[:, 1, bass.ds(n0 + s, 1)]).then_inc(s_dA, 1)
                    if s == 8:
                        act.wait_ge(s_gate, q + 1)
                        nc.scalar.activation(sg[:, :], G[:, :], ACT.Tanh, scale=0.5).then_inc(s_tanh, 1)
                    if s == 13:
                        act.wait_ge(s_intT, q + 1)
                        nc.scalar.copy(interT[:, :, :].rearrange("p k n -> p (k n)"), G[:, :]).then_inc(s_intE, 1)
                    if s == 15:
                        act.wait_ge(s_dif, q + 1)
                        nc.scalar.activation(edif[:, :], dif[:, :], ACT.Exp).then_inc(s_exp, 1)

            def end_block(cb, ct):
                blk = (cb + ct) // STATE
                act.wait_ge(s_y, cb + ct + (OFF + STATE))
                act.wait_ge(s_yst, blk * 16 + 16)
                for j in range(2):
                    ins = nc.scalar.copy(yb[:, j, :], psY[j][:, :])
                ins.then_inc(s_yout, 1)
                act.wait_ge(s_yout, blk + 1)
                act.dma_start(m.y_dram[bass.ds(blk, 1), :, :].rearrange("a p c -> p (a c)"), yb[:, :, :].rearrange("p j c -> p (j c)")).then_inc(s_yst, 16)

            loops(act, body, nothing, end_block)
            act.wait_ge(s_yst, 16 * (2 * B + 1))

        @block.gpsimd
        def _(pool):
            pool.sem_inc(s_dBx, OFF)

            def body(cb, ct, n0):
                N = cb + ct + n0
                t0 = (cb + ct) * 8
                for s in range(UN):
                    pool.wait_ge(s_Bs, N + (OFF + s + 1))
                    pool.wait_ge(s_scan, N + (OFF + s - RD + 1))
                    pool.sem_inc(s_at, 1)
                    nc.gpsimd.tensor_tensor(dBx[:, s % RD, :, :], m.u[:, :, bass.ds(t0, BLK)],
                                            Bs[:, s % RB, :].unsqueeze(1).to_broadcast([P, DH, BLK]), ALU.mult).then_inc(s_dBx, 1)

            loops(pool, body, nothing, nothing)

        @block.vector
        def _(dve):
            nc.vector.memset(edif[:, :], 0.0)
            nc.vector.memset(idf[:, :], 0.0)
            nc.vector.memset(m.accx[:, 0, :], 0.0).then_inc(s_carry, 1)
            dve.wait_ge(s_carry, 1)
            dve.sem_inc(s_scan, OFF)
            dve.sem_inc(s_hC, OFF)
            dve.sem_inc(s_xs, OFF)
            dve.sem_inc(s_cmb, OFF)
            own = [0]

            def link(ins, q):
                own[0] += 1
                ins.then_inc(s_q, 1)
                dve.wait_ge(s_q, q + own[0])

            def combine(qc, q):
                link(nc.vector.tensor_scalar(pr[:, 0:1], edif[:, :], 1.0, None, ALU.add), qc)
                link(nc.vector.reciprocal(pr[:, 0:1], pr[:, 0:1]), qc)
                link(nc.vector.tensor_tensor(pr[:, 1:2], pr[:, 0:1], edif[:, :], ALU.mult), qc)
                nc.vector.tensor_scalar(cd[:, 0, :], m.iota8[:, :], idf[:, 0:1], pr[:, 0:1], ALU.is_equal, ALU.mult)
                link(nc.vector.tensor_scalar(cd[:, 1, :], m.iota8[:, :], idf[:, 1:2], pr[:, 1:2], ALU.is_equal, ALU.mult), qc)
                link(nc.vector.tensor_tensor(cd[:, 0, :], cd[:, 0, :], cd[:, 1, :], ALU.add), qc)

            def add_half(qc, q, half):
                a = m.accx[:, bass.ds(q, 1), :].rearrange("p a h -> p (a h)") if not isinstance(q, int) else m.accx[:, q, :]
                src = (U, G)[half]
                for j in range(4):
                    ins = nc.vector.scalar_tensor_tensor(a, src[:, j * P:(j + 1) * P], cd[:, 0, 4 * half + j:4 * half + j + 1],
                                                         a, ALU.mult, ALU.add)
                    if j < 3:
                        link(ins, qc)
                ins.then_inc(s_cmb, 1)

            def scan_step(N, t0, n0, s):
                dve.wait_ge(s_dA, N + (OFF + s + 1))
                dve.wait_ge(s_dBx, N + (OFF + s + 1))
                dve.wait_ge(s_carry, N + (s + 1))
                for h in range(DH):
                    ins = nc.vector.tensor_tensor_scan(hh[:, s % 2, h, :], dA[:, s % RA, h, :], dBx[:, s % RD, h, :],
                                                       carry[:, bass.ds(n0 + s, 1), h], ALU.mult, ALU.add)
                ins.then_inc(s_scan, 1)
                dve.wait_ge(s_scan, N + (OFF + s + 1))
                nc.vector.tensor_scalar(carry[:, bass.ds(n0 + s, 1), :].rearrange("p n h -> p (n h)"), hh[:, s % 2, :, BLK - 1], 1.0, None, ALU.mult).then_inc(s_carry, 1)
                dve.wait_ge(s_psC, N + (s + 1))
                dve.wait_ge(s_y, N + (OFF + s - RH + 1))
                nc.vector.tensor_tensor(hC[:, s % RH, :, :], hh[:, s % 2, :, :],
                                        psC[s % 2][:, :].unsqueeze(1).to_broadcast([P, DH, BLK]), ALU.mult).then_inc(s_hC, 1)

            def body(cb, ct, n0):
                N = cb + ct + n0
                t0 = (cb + ct) * 8
                q = N // UN
                qc = q * 14
                own[0] = 0
                for s in range(UN):
                    scan_step(N, t0, n0, s)
                    if s == 0:
                        dve.wait_ge(s_exp, q + 1)
                        combine(qc, q)
                        dve.wait_ge(s_dn1, q + 1)
                        add_half(qc, q, 1)
                    if s == 1:
                        dve.wait_ge(s_dn0, q + 1)
                        dve.wait_ge(s_cmb, q * 2 + (OFF + 1))
                        add_half(qc, q, 0)
                    if s == 2:
                        dve.wait_ge(s_cbb, q * 16 + 16)
                        dve.wait_ge(s_up, q + 1)
                        nc.vector.tensor_tensor(xs[:, :, :], cbb[:, :, :],
                                                m.xnT[:, bass.ds(N * 8, P)].unsqueeze(1).to_broadcast([P, 2 * E, P]), ALU.mult).then_inc(s_xs, 1)
                    if s == 9:
                        dve.wait_ge(s_tanh, q + 1)
                        nc.vector.scalar_tensor_tensor(gg[:, :], sg[:, :], 1.0, G[:, :], ALU.add, ALU.mult).then_inc(s_gg, 1)
                    if s == 12:
                        dve.wait_ge(s_gg, q + 1)
                        dve.wait_ge(s_up, q + 2)
                        nc.vector.scalar_tensor_tensor(inter[:, :], gg[:, :], 0.5, U[:, :], ALU.mult, ALU.mult).then_inc(s_int, 1)
                    if s == 14:
                        dve.wait_ge(s_lg, q + 1)
                        nc.vector.tensor_copy(Ld[:, :], G[:, 0:E]).then_inc(s_lgc, 1)
                        dve.wait_ge(s_lgc, 1)
                        dve.wait_ge(s_lgc, q + 1)
                        link(nc.vector.max(top[:, :], Ld[:, :]), qc)
                        nc.vector.tensor_tensor(dif[:, :], top[:, 1:2], top[:, 0:1], ALU.subtract).then_inc(s_dif, 1)
                        link(nc.vector.max_index(idx[:, :], top[:, :], Ld[:, :]), qc)
                        link(nc.vector.tensor_copy(idf[:, :], idx[:, 0:2]), qc)

            with dve.Fori(0, B, 1) as b:
                cb = b * (2 * STATE)
                dve.wait_ge(s_carry, cb + 1)
                nc.vector.memset(carry[:, :, :], 0.0).then_inc(s_zero, 1)
                dve.wait_ge(s_zero, b + 1)
                dve.sem_inc(s_at, 1)
                with dve.Fori(0, 2, 1) as tc:
                    with dve.Fori(0, UNITS, 1) as ic:
                        body(cb, tc * STATE, ic * UN)
            own[0] = 0
            dve.wait_ge(s_exp, NT + 1)
            combine(NT * 14, NT)
            dve.wait_ge(s_dn1, NT + 1)
            add_half(NT * 14, NT, 1)
            dve.wait_ge(s_dn0, NT + 1)
            dve.wait_ge(s_cmb, NT * 2 + OFF + 1)
            add_half(NT * 14, NT, 0)

        @block.tensor
        def _(pe):
            pe.sem_inc(s_y, OFF)
            for bank, done in ((U, s_dn0), (G, s_dn1)):
                nc.tensor.matmul(bank[:, :], lhsT=m.zeros[:, 0:P], rhs=m.zeros[:, :], start=True, stop=True).then_inc(done, 1)
            gate = [(0, e) for e in range(E)]
            up = [(1, e) for e in range(E)]
            plan = {3: gate[0:2], 4: gate[2:3], 5: gate[3:5], 6: gate[5:6], 7: gate[6:8],
                    8: up[0:2], 9: up[2:4], 10: up[4:6], 11: up[6:8]}
            down = {13: [(0, 0), (0, 1)], 14: [(0, 2), (0, 3), (1, 0)], 15: [(1, 1), (1, 2), (1, 3)]}

            def units(q, s):
                return m.PT[0:96, bass.ds(q + s // UN, 1), :].rearrange("p a t -> p (a t)")

            def bcast_B(N, q, s):
                if s >= 2 or not isinstance(N, int):
                    pe.wait_ge(s_Bs, N + (OFF + s - 2 + 1))
                nc.tensor.matmul(psB[s % 2][:, :], lhsT=m.sel[:, 0, s % UN, :], rhs=units(q, s), start=True, stop=True).then_inc(s_psB, 1)

            def bcast_C(N, q, s):
                pe.wait_ge(s_hC, N + (OFF + s - 2 + 1))
                nc.tensor.matmul(psC[s % 2][:, :], lhsT=m.sel[:, 1, s % UN, :], rhs=units(q, s), start=True, stop=True).then_inc(s_psC, 1)

            def body(cb, ct, n0):
                N = cb + ct + n0
                q = N // UN
                for s in range(UN + 1):
                    if s < UN:
                        bcast_B(N, q, s + 2)
                        bcast_C(N, q, s + 1)
                    if s == 3:
                        pe.wait_ge(s_xs, q + (OFF + 1))
                        pe.wait_ge(s_cmb, q * 2 + (OFF + 2))
                    for gu, e in plan.get(s, []):
                        ins = nc.tensor.matmul((G, U)[gu][:, :], lhsT=xs[:, gu * E + e, :], rhs=m.wT[gu][:, e, :], start=(e == 0), stop=(e == E - 1))
                        if e == E - 1:
                            ins.then_inc((s_gate, s_up)[gu], 1)
                    if s == 13:
                        pe.wait_ge(s_int, q + 1)
                        for k in range(KC):
                            ins = nc.tensor.transpose(G[:, k * P:(k + 1) * P], inter[:, k * P:(k + 1) * P], m.ident[:, :])
                        ins.then_inc(s_intT, 1)
                        pe.wait_ge(s_intE, q + 1)
                        for k in range(KC):
                            ins = nc.tensor.matmul(G[:, 0:E], lhsT=interT[:, k, :], rhs=m.w_rdT[:, k, :], start=(k == 0), stop=(k == KC - 1))
                        ins.then_inc(s_lg, 1)
                    for half, k in down.get(s, []):
                        if half and k == 0:
                            pe.wait_ge(s_lgc, q + 1)
                        ins = nc.tensor.matmul((U, G)[half][:, :], lhsT=interT[:, k, :],
                                               rhs=m.w_dnT[:, k, 4 * half:4 * half + 4, :].rearrange("p e h -> p (e h)"),
                                               start=(k == 0), stop=(k == KC - 1))
                        if k == KC - 1:
                            ins.then_inc((s_dn0, s_dn1)[half], 1)
                    if s:
                        pe.wait_ge(s_hC, N + (OFF + s))
                        for t in range(4):
                            for h in range(DH):
                                j = t * DH + h
                                ins = nc.tensor.matmul(psY[j // 4][:, (j % 4) * P:(j % 4 + 1) * P], lhsT=hC[:, (s - 1) % RH, h, t * P:(t + 1) * P],
                                                       rhs=m.ident[:, :], is_transpose=True, start=False, stop=False, skip_group_check=True)
                        ins.then_inc(s_y, 1)

            def start_block(cb, ct):
                for j in range(2):
                    nc.tensor.matmul(psY[j][:, :], lhsT=m.zeros[:, 0:P], rhs=m.zeros[:, :], start=True, stop=False, skip_group_check=True)

            def end_block(cb, ct):
                pe.wait_ge(s_yout, (cb + ct) // STATE + 1)

            pe.sem_inc(s_up, 1)
            bcast_B(0, 0, 0)
            bcast_B(0, 0, 1)
            bcast_C(0, 0, 0)
            loops(pe, body, start_block, end_block)


def gate_and_project(nc, d, m, ps):
    with ExitStack() as ctx:
        sb = lambda n, s, t=FP32: ctx.enter_context(nc.sbuf_tensor(n, s, t))
        sem = lambda n: ctx.enter_context(nc.semaphore(n))
        yg = sb("yg", [P, 2, DH, BLK])
        w_oT = sb("w_oT", [P, DH, D])
        y = sb("y", [P, T // BLK, 2 * BLK])
        xc = sb("xc2", [P, DH, T])
        sz = sb("sz2", [P, DH, T])
        ld = sem("y_loaded")
        y_T, y_dx, y_gated, y_mm, y_acc = [sem(n) for n in ("y_T", "y_dx", "y_gated", "y_mm", "y_acc")]
        block = ctx.enter_context(nc.Block())
        NB4 = T // BLK

        @block.sync
        def _(sp):
            sp.dma_start(w_oT[:, :, :], d.w_oT).then_inc(ld, 16)
            sp.dma_start(y[:, :, :], m.y_dram.rearrange("k p c -> p k c")).then_inc(ld, 16)
            sp.dma_start(xc[:, :, :], m.xc_dram).then_inc(ld, 16)
            sp.dma_start(sz[:, :, :], m.sz_dram).then_inc(ld, 16)

        @block.tensor
        def _(pe):
            pe.wait_ge(ld, 64)
            for i in range(NB4 + 1):
                if i < NB4:
                    for h in range(DH):
                        if i >= 2:
                            pe.wait_ge(y_dx, 2 * (i - 2) + h + 1)
                        for t in range(4):
                            ins = nc.tensor.transpose(ps[2 * (i % 2) + h][:, t * P:(t + 1) * P], y[:, i, (t * DH + h) * P:(t * DH + h + 1) * P], m.ident[:, :])
                        ins.then_inc(y_T, 1)
                if i >= 1:
                    k = i - 1
                    pe.wait_ge(y_gated, 2 * k + 2)
                    if k >= 2:
                        pe.wait_ge(y_acc, k - 1)
                    for t in range(4):
                        for h in range(DH):
                            ins = nc.tensor.matmul(ps[4 + k % 2][:, t * P:(t + 1) * P], lhsT=yg[:, k % 2, h, t * P:(t + 1) * P], rhs=w_oT[:, h, :],
                                                   start=(h == 0), stop=(h == DH - 1))
                    ins.then_inc(y_mm, 1)

        @block.vector
        def _(dve):
            dve.wait_ge(ld, 64)
            for i in range(NB4 + 1):
                if i < NB4:
                    for h in range(DH):
                        c = slice(i * BLK, (i + 1) * BLK)
                        dve.wait_ge(y_T, 2 * i + h + 1)
                        if i >= 2:
                            dve.wait_ge(y_mm, i - 1)
                        nc.vector.scalar_tensor_tensor(yg[:, i % 2, h, :], xc[:, h, c], m.Dp[:, h:h + 1], ps[2 * (i % 2) + h][:, :],
                                                       ALU.mult, ALU.add).then_inc(y_dx, 1)
                        dve.wait_ge(y_dx, 2 * i + h + 1)
                        nc.vector.tensor_tensor(yg[:, i % 2, h, :], yg[:, i % 2, h, :], sz[:, h, c], ALU.mult).then_inc(y_gated, 1)
                if i >= 1:
                    k = i - 1
                    dve.wait_ge(y_mm, k + 1)
                    a = m.accx[:, 1 + 4 * k:5 + 4 * k, :].rearrange("p t h -> p (t h)")
                    nc.vector.tensor_tensor(a, ps[4 + k % 2][:, :], a, ALU.add).then_inc(y_acc, 1)



def second_norm(nc, d, m, ps):
    with ExitStack() as ctx:
        sb = lambda n, s, t=FP32: ctx.enter_context(nc.sbuf_tensor(n, s, t))
        sem = lambda n: ctx.enter_context(nc.semaphore(n))
        st6, mv, r1 = sb("n_st6", [P, NT, 6]), sb("n_mv", [P, NT, 2]), sb("n_r", [P, NT])
        v, n_in, n_sqrt, n_done, n_mm, n_cp = [sem(n) for n in ("n_dve", "n_in", "n_sqrt", "n_done", "n_mm", "n_cp")]
        block = ctx.enter_context(nc.Block())

        @block.vector
        def _(dve):
            cnt = [0]

            def link(ins):
                cnt[0] += 1
                ins.then_inc(v, 1)
                dve.wait_ge(v, cnt[0])

            for t in range(NT):
                ins = nc.vector.bn_stats(st6[:, t, :], m.acc[:, t, :])
            link(ins)
            for t in range(NT):
                ins = nc.vector.bn_aggr(mv[:, t, :], st6[:, t, :])
            link(ins)
            nc.vector.tensor_scalar(r1[:, :], mv[:, :, 1], EPS_LN, None, ALU.add).then_inc(n_in, 1)
            dve.wait_ge(n_sqrt, 1)
            link(nc.vector.reciprocal(r1[:, :], r1[:, :]))
            for t in range(NT):
                nc.vector.tensor_scalar(m.xn2[:, t, :], m.acc[:, t, :], mv[:, t, 0:1], r1[:, t:t + 1], ALU.subtract, ALU.mult).then_inc(n_done, 1)
            for q in range(4):
                dve.wait_ge(n_mm, q + 1)
                nc.vector.tensor_copy(m.xn2T[:, q * BLK:(q + 1) * BLK], ps[q][:, :]).then_inc(n_cp, 1)
            dve.wait_ge(n_done, NT)
            nc.vector.tensor_copy(m.yatt[:, :, :], m.xn2[:, :, :])

        @block.scalar
        def _(act):
            act.wait_ge(n_in, 1)
            nc.scalar.activation(r1[:, :], r1[:, :], ACT.Sqrt).then_inc(n_sqrt, 1)

        @block.tensor
        def _(pe):
            for q in range(4):
                pe.wait_ge(n_done, 4 * q + 4)
                for j in range(4):
                    ins = nc.tensor.transpose(ps[q][:, j * P:(j + 1) * P], m.xn2[:, 4 * q + j, :], m.ident[:, :])
                ins.then_inc(n_mm, 1)


def attention(nc, d, m, psum):
    ORDER = [7, 0, 6, 1, 5, 2, 4, 3]
    items = []
    entries = []
    for b in range(B):
        mine = [("s", b, qt, h) for qt in ORDER for h in range(2)]
        for at, w in ((3, 0), (7, 1), (11, 2)):
            mine.insert(at + w, ("p", 1 - b, w, 0))
        entries += mine
    items = [e for e in entries if e[0] == "s"]
    NE, NI, NP = len(entries), len(items), len(items) // 2
    entry_of = [i for i, e in enumerate(entries) if e[0] == "s"]
    last_w = max(i for i, e in enumerate(entries) if e[0] == "p" and e[1] == 1)
    PRO = 3

    with ExitStack() as ctx:
        sb = lambda n, s, t=FP32: ctx.enter_context(nc.sbuf_tensor(n, s, t))
        sem = lambda n: ctx.enter_context(nc.semaphore(n))
        wqkv = sb("wqkv", [P, 3, P])
        wo = sb("wo", [P, HP + 1, D])
        identb = sb("identb", [P, P], BF16)
        maskb = sb("maskb", [P, P], BF16)
        qT = sb("qT", [P, B, S])
        kT = sb("kT", [P, B, S])
        V = sb("V", [P, B, QT, P])
        Pr = sb("Pr", [P, 2, S])
        PT = sb("PTs", [P, 2, S])
        nmax = sb("nmax", [P, 2])
        rsum = sb("rsum", [P, 4])
        rinv = sb("rinv", [P, 4])
        O = sb("O", [P, 2, P])
        OT = sb("OT", [P, 2, P])

        slot = [psum[:, 0:2, :].rearrange("p a t -> p (a t)"), psum[:, 2:4, :].rearrange("p a t -> p (a t)")]
        pPT = psum[:, 4:6, :].rearrange("p a t -> p (a t)")
        pO, pW = psum[:, 6, :], psum[:, 7, :]

        a_ld, a_w, a_z = sem("a_ld"), sem("a_w"), sem("a_zero")
        s_full, s_free, s_max, s_T, s_ev, s_PV, s_norm, s_oT, s_oTs, s_Wo, s_add = [sem("a_" + n) for n in (
            "slot_full", "slot_free", "max", "PT_mm", "PT_out", "O_mm", "O_out", "OT_mm", "OT_out", "Wo_mm", "added")]
        OFF = 4
        block = ctx.enter_context(nc.Block())

        @block.sync
        def _(sp):
            sp.dma_start(wqkv[:, :, :], d.wqkv[0]).then_inc(a_w, 16)
            sp.dma_start(wo[:, 1:HP + 1, :], d.wo).then_inc(a_ld, 16)
            sp.dma_start(identb[:, :], d.identb).then_inc(a_ld, 16)
            sp.dma_start(maskb[:, :], d.maskb).then_inc(a_ld, 16)
            with sp.Fori(0, HP, 1) as hp:
                sp.wait_ge(s_full, hp * NE + (PRO + last_w + 1))
                sp.dma_start(wqkv[:, :, :].rearrange("p a e -> p (a e)"),
                             d.wqkv.rearrange("n p a e -> n p (a e)")[bass.ds(hp + 1, 1)].rearrange("n p e -> (n p) e")).then_inc(a_w, 16)

        @block.gpsimd
        def _(pool):
            nc.gpsimd.memset(wo[:, 0, :], 0.0).then_inc(a_z, 1)
            nc.gpsimd.memset(V[:, 1, :, :], 0.0).then_inc(a_z, 1)
            nc.gpsimd.memset(Pr[:, :, :], 0.0).then_inc(a_z, 1)
            nc.gpsimd.memset(PT[:, :, :], 0.0).then_inc(a_z, 1)
            nc.gpsimd.memset(rsum[:, :], 1.0)
            nc.gpsimd.memset(rinv[:, :], 1.0).then_inc(a_z, 1)
            nc.gpsimd.memset(O[:, :, :], 0.0).then_inc(a_z, 1)

        @block.tensor
        def _(pe):
            pe.sem_inc(s_T, OFF - 1)
            pe.sem_inc(s_PV, OFF - 2)
            pe.sem_inc(s_oT, OFF - 2)
            pe.sem_inc(s_Wo, OFF - 2)
            pe.wait_ge(a_ld, 48)
            pe.wait_ge(a_z, 6)

            def project(base, i, e, wbase):
                _, b, w, _ = e
                pe.wait_ge(s_free, base + (OFF + i - 1))
                pe.wait_ge(a_w, wbase)
                if w < 2:
                    for c in range(2):
                        ins = nc.tensor.matmul(slot[i % 2][:, c * BLK:(c + 1) * BLK], lhsT=wqkv[:, w, :],
                                               rhs=m.xn2T[:, b * S + c * BLK:b * S + (c + 1) * BLK], start=True, stop=True)
                else:
                    for t in range(QT):
                        ins = nc.tensor.matmul(slot[i % 2][:, t * P:(t + 1) * P], lhsT=m.xn2T[:, b * S + t * P:b * S + (t + 1) * P],
                                               rhs=wqkv[:, 2, :], start=True, stop=True)
                ins.then_inc(s_full, 1)

            def scores(base, i, e):
                _, b, qt, h = e
                n = (qt + 1) * P
                r = slice(h * HS, (h + 1) * HS)
                pe.wait_ge(s_free, base + (OFF + i - 1))
                for c in range(0, n, BLK):
                    w = min(BLK, n - c)
                    last = c + w == n
                    if last:
                        nc.tensor.matmul(slot[i % 2][:, n - P:n], lhsT=identb[:, :], rhs=maskb[:, :], start=True, stop=False, skip_group_check=True)
                    ins = nc.tensor.matmul(slot[i % 2][:, c:c + w], lhsT=qT[r, b, qt * P:(qt + 1) * P], rhs=kT[r, b, c:c + w],
                                           start=not last, stop=True, skip_group_check=True)
                ins.then_inc(s_full, 1)

            def values(base, k):
                _, b, qt, h = items[k % NI]
                pe.wait_ge(s_ev, base + (OFF + k + 1))
                pe.wait_ge(s_norm, base + (OFF + k))
                for t in range(qt + 1):
                    ins = nc.tensor.matmul(pO[:, 0:HS], lhsT=PT[:, k % 2, t * P:(t + 1) * P], rhs=V[:, b, t, h * HS:(h + 1) * HS],
                                           start=(t == 0), stop=(t == qt))
                ins.then_inc(s_PV, 1)

            def turn(base, ebase, k):
                _, b, qt, h = items[k % NI]
                if k >= 0:
                    pe.wait_ge(s_free, ebase + (OFF + entry_of[k] + PRO + 1))
                else:
                    pe.wait_ge(s_free, ebase + (OFF + PRO - 1 + 1))
                pe.wait_ge(s_ev, base + (OFF + k))
                for t in range(qt + 1):
                    ins = nc.tensor.transpose(pPT[:, t * P:(t + 1) * P], Pr[:, k % 2, t * P:(t + 1) * P], m.ident[:, :])
                ins.then_inc(s_T, 1)

            def pair_turn(pbase, kbase, p):
                pe.wait_ge(s_norm, kbase + (OFF + 2 * p + 2))
                pe.wait_ge(s_add, pbase + (OFF + p))
                nc.tensor.transpose(pW[:, 0:P], O[:, p % 2, :], m.ident[:, :]).then_inc(s_oT, 1)

            def pair_out(pbase, p, w):
                pe.wait_ge(s_oTs, pbase + (OFF + p + 1))
                nc.tensor.matmul(pW[:, 0:D], lhsT=OT[:, p % 2, :], rhs=w, start=True, stop=True).then_inc(s_Wo, 1)

            for w in range(3):
                project(0, w, ("p", 0, w, 0), 16)
            with pe.Fori(0, HP, 1) as hp:
                kb, eb, pb = hp * NI, hp * NE, hp * NP
                wo_of = lambda p: wo[:, bass.ds(hp + (0 if p < 0 else 1), 1), :].rearrange("p a e -> p (a e)")
                k = 0
                for i, e in enumerate(entries):
                    if e[0] == "p":
                        project(eb, PRO + i, e, hp * 16 + (16 if e[1] == 1 else 32))
                        continue
                    scores(eb, PRO + i, e)
                    values(kb, k - 2)
                    turn(kb, eb, k - 1)
                    if k % 2 == 0:
                        pair_turn(pb, kb, k // 2 - 2)
                    else:
                        pair_out(pb, (k - 5) // 2, wo_of((k - 5) // 2))
                    k += 1
            kb, pb = HP * NI, HP * NP
            w = wo[:, HP, :]
            values(kb, -2)
            turn(kb, HP * NE, -1)
            pair_turn(pb, kb, -2)
            values(kb, -1)
            pair_out(pb, -2, w)
            pair_turn(pb, kb, -1)
            pair_out(pb, -1, w)

        @block.scalar
        def _(act):
            act.sem_inc(s_free, OFF)
            act.sem_inc(s_oTs, OFF - 2)
            act.wait_ge(a_z, 6)

            def projected(base, kbase, i, e, k):
                _, b, w, _ = e
                act.wait_ge(s_full, base + (i + 1))
                if w == 0:
                    ins = nc.scalar.mul(qT[:, b, :], slot[i % 2], HS ** -0.5)
                elif w == 1:
                    ins = nc.scalar.copy(kT[:, b, :], slot[i % 2])
                else:
                    if k is not None:
                        act.wait_ge(s_PV, kbase + (OFF + k))
                    ins = nc.scalar.copy(V[:, b, :, :].rearrange("p t e -> p (t e)"), slot[i % 2])
                ins.then_inc(s_free, 1)

            def pair_copy(pbase, p):
                act.wait_ge(s_oT, pbase + (OFF + p + 1))
                act.wait_ge(s_Wo, pbase + (OFF + p - 1))
                nc.scalar.copy(OT[:, p % 2, :], pW[:, 0:P]).then_inc(s_oTs, 1)

            for w in range(3):
                projected(0, 0, w, ("p", 0, w, 0), None)
            with act.Fori(0, HP, 1) as hp:
                kb, eb, pb = hp * NI, hp * NE, hp * NP
                k = 0
                for i, e in enumerate(entries):
                    if e[0] == "p":
                        projected(eb, kb, PRO + i, e, 0 if e[1] == 1 else NI // 2)
                        continue
                    n = (e[2] + 1) * P
                    act.wait_ge(s_max, kb + (OFF + k + 1))
                    act.wait_ge(s_T, kb + (OFF + k - 1))
                    nc.scalar.activation(Pr[:, k % 2, 0:n], slot[(PRO + i) % 2][:, 0:n], ACT.Exp, bias=nmax[:, k % 2:k % 2 + 1],
                                         accum_out=rsum[:, k % 4:k % 4 + 1]).then_inc(s_free, 1)
                    if k % 2 == 0:
                        pair_copy(pb, k // 2 - 2)
                    k += 1
            pair_copy(HP * NP, -2)
            pair_copy(HP * NP, -1)

        @block.vector
        def _(dve):
            dve.sem_inc(s_max, OFF)
            dve.sem_inc(s_ev, OFF - 1)
            dve.sem_inc(s_norm, OFF - 2)
            dve.sem_inc(s_add, OFF - 2)
            dve.wait_ge(a_z, 6)

            def normalise(base, pbase, k):
                _, b, qt, h = items[k % NI]
                p = k // 2
                dve.wait_ge(s_PV, base + (OFF + k + 1))
                dve.wait_ge(s_ev, base + (OFF + k + 1))
                if h == 0:
                    dve.wait_ge(s_oT, pbase + (OFF + p - 1))
                nc.vector.tensor_scalar(O[:, p % 2, h * HS:(h + 1) * HS], pO[:, 0:HS], rinv[:, k % 4:k % 4 + 1], None, ALU.mult).then_inc(s_norm, 1)

            def evacuate(base, k):
                n = (items[k % NI][2] + 1) * P
                dve.wait_ge(s_T, base + (OFF + k + 1))
                dve.wait_ge(s_PV, base + (OFF + k - 1))
                nc.vector.reciprocal(rinv[:, k % 4:k % 4 + 1], rsum[:, k % 4:k % 4 + 1])
                nc.vector.tensor_copy(PT[:, k % 2, 0:n], pPT[:, 0:n]).then_inc(s_ev, 1)

            def add(pbase, p):
                _, b, qt, _ = items[(2 * p) % NI]
                dve.wait_ge(s_Wo, pbase + (OFF + p + 1))
                y = m.yatt[:, b * QT + qt, :]
                nc.vector.tensor_tensor(y, y, pW[:, 0:D], ALU.add).then_inc(s_add, 1)

            with dve.Fori(0, HP, 1) as hp:
                kb, eb, pb = hp * NI, hp * NE, hp * NP
                k = 0
                for i, e in enumerate(entries):
                    if e[0] == "p":
                        continue
                    n = (e[2] + 1) * P
                    dve.wait_ge(s_full, eb + (PRO + i + 1))
                    dve.wait_ge(s_free, eb + (OFF + PRO + (entry_of[k - 2] if k >= 2 else entry_of[k - 2 + NI] - NE) + 1))
                    nc.vector.tensor_reduce(nmax[:, k % 2:k % 2 + 1], slot[(PRO + i) % 2][:, 0:n], AX.X, ALU.max, negate=True).then_inc(s_max, 1)
                    normalise(kb, pb, k - 2)
                    evacuate(kb, k - 1)
                    if k % 2:
                        add(pb, (k - 5) // 2)
                    k += 1
            kb, pb = HP * NI, HP * NP
            normalise(kb, pb, -2)
            evacuate(kb, -1)
            normalise(kb, pb, -1)
            add(pb, -2)
            add(pb, -1)


def ternary_and_last(nc, d, m, psum):
    with ExitStack() as ctx:
        sb = lambda n, s, t=FP32: ctx.enter_context(nc.sbuf_tensor(n, s, t))
        sem = lambda n: ctx.enter_context(nc.semaphore(n))
        w = [sb("t_wu", [P, FF]), sb("t_wd", [P, FF])]
        wt = [sb("t_tu", [P, FF]), sb("t_td", [P, FF])]
        asum = sb("t_as", [P, 2])
        thr = sb("t_thr", [P, 4])
        cst = sb("t_cst", [P, P])
        gb = sb("t_gb", [P, 2, D])
        hh = sb("t_h", [P, 3, FF])
        hT = sb("t_hT", [P, 2, KC, P])
        sq = sb("t_sq", [P, FF])
        sqx = sb("t_sqx", [P, NT, D])
        ssx = sb("t_ssx", [P, NT])
        ssh = sb("t_ssh", [P, NT])
        rx = sb("t_rx", [P, NT])
        rh = sb("t_rh", [P, NT])
        st6, mv, r1 = sb("l_st6", [P, NT, 6]), sb("l_mv", [P, NT, 2]), sb("l_r", [P, NT])
        dn = sb("t_dn", [P, NT, D])
        t_ld, t_v, t_as, t_sgn, t_thr, t_wq, t_x, t_xs, t_up, t_gelu, t_hT, t_hTs, t_dn, t_dns, t_sq, t_sqr, l_in, l_sqrt, t_out, t_f = [sem("t_" + n) for n in (
            "ld", "v", "as", "sgn", "thr", "wq", "x", "xs", "up", "gelu", "hT", "hTs", "dn", "dns", "sq", "sqr", "lin", "lsq", "out", "fin")]
        ps = [psum[:, i, :] for i in range(8)]
        block = ctx.enter_context(nc.Block())

        @block.sync
        def _(sp):
            sp.dma_start(w[0][:, :], d.t_upT).then_inc(t_ld, 16)
            sp.dma_start(w[1][:, :], d.t_dnT).then_inc(t_ld, 16)
            sp.dma_start(cst[:, :], d.half_mean).then_inc(t_ld, 16)
            sp.dma_start(gb[:, 0, :], d.gamma.to_broadcast([P, D])).then_inc(t_ld, 16)
            sp.dma_start(gb[:, 1, :], d.beta.to_broadcast([P, D])).then_inc(t_ld, 16)
            sp.wait_ge(t_f, 1)
            sp.dma_start(m.out, m.acc).then_inc(t_out, 16)
            sp.wait_ge(t_out, 16)

        @block.tensor
        def _(pe):
            pe.wait_ge(t_as, 1)
            nc.tensor.matmul(ps[7][:, 0:2], lhsT=cst[:, :], rhs=asum[:, :], start=True, stop=True).then_inc(t_thr, 1)
            pe.wait_ge(t_wq, 1)
            for t in range(NT + 2):
                if t < NT:
                    if t >= 2:
                        pe.wait_ge(t_gelu, t - 1)
                    nc.tensor.matmul(ps[t % 2], lhsT=m.xn2T[:, t * P:(t + 1) * P], rhs=w[0][:, :], start=True, stop=True).then_inc(t_up, 1)
                if 1 <= t <= NT:
                    j = t - 1
                    pe.wait_ge(t_gelu, j + 1)
                    if j >= 2:
                        pe.wait_ge(t_hTs, j - 1)
                    for k in range(KC):
                        ins = nc.tensor.transpose(ps[2 + j % 2][:, k * P:(k + 1) * P], hh[:, j % 3, k * P:(k + 1) * P], m.ident[:, :])
                    ins.then_inc(t_hT, 1)
                if t >= 2:
                    j = t - 2
                    pe.wait_ge(t_hTs, j + 1)
                    if j >= 2:
                        pe.wait_ge(t_dns, j - 1)
                    for k in range(KC):
                        ins = nc.tensor.matmul(ps[4 + j % 2][:, 0:D], lhsT=hT[:, j % 2, k, :], rhs=w[1][:, k * P:(k + 1) * P], start=(k == 0), stop=(k == KC - 1))
                    ins.then_inc(t_dn, 1)

        @block.scalar
        def _(act):
            act.wait_ge(t_x, 1)
            nc.scalar.activation(rx[:, :], ssx[:, :], ACT.Sqrt, scale=1.0 / D).then_inc(t_xs, 1)
            act.wait_ge(l_in, 1)
            nc.scalar.activation(r1[:, :], r1[:, :], ACT.Sqrt).then_inc(l_sqrt, 1)
            act.wait_ge(t_xs, 2)
            for t in range(NT):
                act.wait_ge(t_up, t + 1)
                if t >= 3:
                    act.wait_ge(t_hT, t - 2)
                    act.wait_ge(t_sq, t - 2)
                nc.scalar.activation(hh[:, t % 3, :], ps[t % 2], ACT.Gelu, scale=rx[:, t:t + 1]).then_inc(t_gelu, 1)
            act.wait_ge(t_sq, NT)
            nc.scalar.activation(rh[:, :], ssh[:, :], ACT.Sqrt, scale=1.0 / FF).then_inc(t_sqr, 1)

        @block.vector
        def _(dve):
            cnt = [0]

            def link(ins):
                cnt[0] += 1
                ins.then_inc(t_v, 1)
                dve.wait_ge(t_v, cnt[0])

            dve.wait_ge(t_ld, 80)
            nc.vector.tensor_reduce(asum[:, 0:1], w[0][:, :], AX.X, ALU.add, apply_absolute_value=True)
            nc.vector.tensor_reduce(asum[:, 1:2], w[1][:, :], AX.X, ALU.add, apply_absolute_value=True).then_inc(t_as, 1)
            for t in range(NT):
                ins = nc.vector.tensor_tensor_reduce(out=sqx[:, t, :], in0=m.xn2[:, t, :], in1=m.xn2[:, t, :], scale=1.0, scalar=0.0,
                                                     op0=ALU.mult, op1=ALU.add, accum_out=ssx[:, t:t + 1])
            ins.then_inc(t_x, 1)
            dve.wait_ge(t_thr, 1)
            nc.vector.tensor_scalar(thr[:, 0:2], ps[7][:, 0:2], 1.0, None, ALU.mult)
            link(nc.vector.tensor_scalar(thr[:, 2:4], ps[7][:, 0:2], -1.0, None, ALU.mult))
            for i in range(2):
                link(nc.vector.tensor_scalar(wt[i][:, :], w[i][:, :], thr[:, i:i + 1], None, ALU.is_gt))
                link(nc.vector.scalar_tensor_tensor(wt[i][:, :], w[i][:, :], thr[:, 2 + i:3 + i], wt[i][:, :], ALU.is_lt, ALU.subtract))
                link(nc.vector.tensor_tensor(wt[i][:, :], wt[i][:, :], w[i][:, :], ALU.add))
                ins = nc.vector.tensor_tensor(w[i][:, :], w[i][:, :], wt[i][:, :], ALU.subtract)
            ins.then_inc(t_wq, 1)
            for t in range(NT):
                ins = nc.vector.bn_stats(st6[:, t, :], m.yatt[:, t, :])
            link(ins)
            for t in range(NT):
                ins = nc.vector.bn_aggr(mv[:, t, :], st6[:, t, :])
            link(ins)
            nc.vector.tensor_scalar(r1[:, :], mv[:, :, 1], EPS_LN2, None, ALU.add).then_inc(l_in, 1)
            dve.wait_ge(t_xs, 1)
            link(nc.vector.tensor_scalar(rx[:, :], rx[:, :], EPS_T, None, ALU.add))
            nc.vector.reciprocal(rx[:, :], rx[:, :]).then_inc(t_xs, 1)
            dve.wait_ge(l_sqrt, 1)
            link(nc.vector.reciprocal(r1[:, :], r1[:, :]))
            for t in range(NT):
                ins = nc.vector.tensor_scalar(m.yatt[:, t, :], m.yatt[:, t, :], mv[:, t, 0:1], r1[:, t:t + 1], ALU.subtract, ALU.mult)
            link(ins)
            gam, bet = [gb[:, i, :].unsqueeze(1).to_broadcast([P, NT, D]) for i in range(2)]
            for t in range(NT + 1):
                if t == 1:
                    link(nc.vector.tensor_tensor(m.yatt[:, :, :], m.yatt[:, :, :], gam, ALU.mult))
                if t == 3:
                    link(nc.vector.tensor_tensor(m.yatt[:, :, :], m.yatt[:, :, :], bet, ALU.add))
                if t == 5:
                    link(nc.vector.tensor_tensor(m.acc, m.acc, m.yatt[:, :, :], ALU.add))
                if t < NT:
                    dve.wait_ge(t_gelu, t + 1)
                    if t:
                        dve.wait_ge(t_sq, t)
                    nc.vector.tensor_tensor_reduce(out=sq[:, :], in0=hh[:, t % 3, :], in1=hh[:, t % 3, :], scale=1.0, scalar=0.0,
                                                   op0=ALU.mult, op1=ALU.add, accum_out=ssh[:, t:t + 1]).then_inc(t_sq, 1)
                    dve.wait_ge(t_hT, t + 1)
                    if t >= 2:
                        dve.wait_ge(t_dn, t - 1)
                    nc.vector.tensor_copy(hT[:, t % 2, :, :].rearrange("p k n -> p (k n)"), ps[2 + t % 2]).then_inc(t_hTs, 1)
                if t:
                    dve.wait_ge(t_dn, t)
                    nc.vector.tensor_copy(dn[:, t - 1, :], ps[4 + (t - 1) % 2][:, 0:D]).then_inc(t_dns, 1)
            dve.wait_ge(t_dns, NT)
            dve.wait_ge(t_sqr, 1)
            link(nc.vector.tensor_scalar(rh[:, :], rh[:, :], EPS_T, None, ALU.add))
            link(nc.vector.reciprocal(rh[:, :], rh[:, :]))
            for t in range(NT):
                ins = nc.vector.scalar_tensor_tensor(m.acc[:, t, :], dn[:, t, :], rh[:, t:t + 1], m.acc[:, t, :], ALU.mult, ALU.add)
            ins.then_inc(t_f, 1)


def both_layers(nc, d, out, stage=3):
    with ExitStack() as ctx:
        sb = lambda n, s, t=FP32: ctx.enter_context(nc.sbuf_tensor(n, s, t))
        psum = ctx.enter_context(nc.psum_tensor("psum", [P, 8, BLK], FP32))
        ps = [psum[:, i, :] for i in range(8)]
        m = Memory()
        m.out = out
        m.ident = sb("ident", [P, P])
        m.accx = sb("accx", [P, NT + 1, D])
        m.acc = m.accx[:, 1:NT + 1, :]
        m.one = sb("one", [P, 1])
        m.iota8 = sb("iota8", [P, E])
        with ExitStack() as c1:
            sb = lambda n, s, t=FP32: c1.enter_context(nc.sbuf_tensor(n, s, t))
            dram = lambda n, s: nc.dram_tensor(n, s, FP32, kind="Internal").ap()
            m.Dp = sb("Dp", [P, DH])
            with ExitStack() as c2:
                sb = lambda n, s, t=FP32: c2.enter_context(nc.sbuf_tensor(n, s, t))
                m.A = sb("A", [P, DH, STATE])
                m.dt = sb("dt", [P, DH, T])
                m.u_mem = sb("u", [P, DH * B * (KW - 1 + S)])
                m.u = m.u_mem[:, 0:DH * T].rearrange("p (h t) -> p h t", h=DH)
                m.PT = sb("PT", [P, UNITS * B * 2 + 1, BLK], BF16)
                m.sel = sb("sel", [96, 2, UN, P], BF16)
                m.zeros = sb("zeros", [P, BLK], BF16)
                m.xnT = sb("xnT", [P, T])
                m.wT = [sb("w_gT", [P, E, FF]), sb("w_uT", [P, E, FF])]
                m.w_dnT = sb("w_dnT", [P, KC, E, D])
                m.w_rdT = sb("w_rdT", [P, KC, E])
                m.xc_dram, m.sz_dram = dram("xc_dram", (P, DH, T)), dram("sz_dram", (P, DH, T))
                m.y_dram = dram("y_dram", (T // BLK, P, 2 * BLK))
                m.comb_dram = dram("comb_dram", (NT, 2 * E, P))
                prepare(nc, d, m, ps)
                scan_and_experts(nc, d, m, ps)
            gate_and_project(nc, d, m, ps)
        m.xn2 = ctx.enter_context(nc.sbuf_tensor("xn2", [P, NT, D], FP32))
        m.xn2T = ctx.enter_context(nc.sbuf_tensor("xn2T", [P, T], FP32))
        m.yatt = ctx.enter_context(nc.sbuf_tensor("yatt", [P, NT, D], FP32))
        second_norm(nc, d, m, ps)
        attention(nc, d, m, psum)
        ternary_and_last(nc, d, m, psum)


def layout(i):
    bf16 = mybir.dt.np(BF16)
    c = np.ascontiguousarray
    half = lambda w: w.reshape(DH, P, -1).transpose(1, 0, 2)
    o = {}
    o["x"] = c(i["L0_attn_x"].reshape(NT, P, D).transpose(1, 0, 2))
    o["vec"] = c(np.concatenate([i["L0_attn_norm_w"].reshape(P, 1), half(i["L0_attn_conv_b"].reshape(INNER, 1)).reshape(P, -1),
                                 half(i["L0_attn_dt_b"].reshape(INNER, 1)).reshape(P, -1), half(i["L0_attn_D_param"].reshape(INNER, 1)).reshape(P, -1),
                                 half(i["L0_attn_conv_w"].reshape(INNER, KW)).reshape(P, -1), half(i["L0_attn_A_log"]).reshape(P, -1)], axis=1))
    o["w_inT"] = c(i["L0_attn_in_proj_w"].T)
    o["w_bcT"] = c(half(np.concatenate([i["L0_attn_B_w"], i["L0_attn_C_w"]], axis=0).T))
    o["w_dtT"] = c(half(i["L0_attn_dt_w"].T))
    o["w_oT"] = c(half(i["L0_attn_out_proj_w"].T))
    o["w_rT"] = c(np.concatenate([i["L0_ffn_router_gate"], i["L0_ffn_router_up"]], axis=0).T)
    o["w_rdT"] = c(i["L0_ffn_router_down"].T.reshape(KC, P, E).transpose(1, 0, 2))
    o["w_gT"] = c(i["L0_ffn_w_gate"].transpose(2, 0, 1))
    o["w_uT"] = c(i["L0_ffn_w_up"].transpose(2, 0, 1))
    o["w_dnT"] = c(i["L0_ffn_w_down"].transpose(2, 0, 1).reshape(KC, P, E, D).transpose(1, 0, 2, 3))
    pairs = lambda w: w.reshape(HP, 2, D, HS).transpose(0, 2, 1, 3).reshape(HP, D, P)
    w = np.stack([pairs(i["L1_attn_" + n]) for n in ("Wq", "Wk", "Wv")], axis=2)
    o["wqkv"] = c(np.concatenate([w, np.zeros_like(w[:1])], axis=0))
    o["wo"] = c(i["L1_attn_Wo"].reshape(HP, P, D).transpose(1, 0, 2))
    o["gamma"], o["beta"] = i["L1_attn_gamma"].reshape(1, D), i["L1_attn_beta"].reshape(1, D)
    o["t_upT"] = c(i["L1_ffn_w_up"].T)
    o["t_dnT"] = c(i["L1_ffn_w_down"].T.reshape(KC, P, D).transpose(1, 0, 2).reshape(P, FF))
    o["half_mean"] = np.full((P, P), 0.5 / (FF * D), np.float32)
    o["identb"] = np.eye(P).astype(bf16)
    o["maskb"] = np.where(np.tril(np.ones((P, P))) > 0, 0.0, NEG).astype(bf16)
    o["ident"] = np.eye(P, dtype=np.float32)
    o["iota8"] = c(np.broadcast_to(np.arange(E, dtype=np.float32), (P, E)))
    sel = np.zeros((2, 3, UN, 2, UN, P), np.float32)
    for q in range(2):
        for s in range(UN):
            sel[q, :, s, q, s, :] = 1.0
    o["sel"] = sel.reshape(96, 2, UN, P).astype(bf16)
    return o


INPUTS = ["x", "vec", "w_inT", "w_bcT", "w_dtT", "w_oT", "w_rT", "w_rdT", "w_gT", "w_uT", "w_dnT", "wqkv", "wo", "gamma", "beta",
          "t_upT", "t_dnT", "half_mean", "identb", "maskb", "ident", "iota8", "sel"]


def kernel(**inputs):
    import concourse.bacc as bacc
    from concourse.bass_utils import run_bass_kernel_spmd

    arrays = layout({k: np.asarray(v) for k, v in inputs.items()})
    nc = bacc.Bacc("TRN2", target_bir_lowering=False, num_devices=1)
    d = namedtuple("Inputs", INPUTS)(*[nc.dram_tensor("in_" + n, arrays[n].shape, mybir.dt.from_np(arrays[n].dtype), kind="ExternalInput").ap()
                                       for n in INPUTS])
    out = nc.dram_tensor("out", (P, NT, D), FP32, kind="ExternalOutput").ap()
    both_layers(nc, d, out)
    r = run_bass_kernel_spmd(nc, [{"in_" + n: arrays[n] for n in INPUTS}], core_ids=[0])
    return r.results[0]["out"].transpose(1, 0, 2).reshape(B, S, D)
```

```python
import numpy as np
import concourse.bass as bass
from concourse import mybir
from collections import namedtuple
from contextlib import ExitStack

FP32 = mybir.dt.float32
BF16 = mybir.dt.bfloat16
U32 = mybir.dt.uint32
ALU = mybir.AluOpType
ACT = mybir.ActivationFunctionType
AX = mybir.AxisListType

P = 128
B, S, D = 2, 1024, 128
T = B * S
NT = T // P
BLK = 512
INNER, STATE, KW = 256, 64, 4
DH = INNER // P
E, FF = 8, 512
KC = FF // P
H, HS = 16, 64
HP = H // 2
QT = S // P
EPS_LN, EPS_RMS, EPS_LN2, EPS_T = 1e-5, 1e-6, 1e-3, 1e-8
UN = 16
UNITS = STATE // UN
NEG = -1.0e30
V_NORM, V_CB, V_DTB, V_D = 0, 1, 1 + DH, 1 + 2 * DH
V_CW = 1 + 3 * DH
V_A = V_CW + DH * KW
VECS = V_A + DH * STATE


class Memory:
    pass


def prepare(nc, d, m, ps):
    with ExitStack() as ctx:
        sb = lambda n, s, t=FP32: ctx.enter_context(nc.sbuf_tensor(n, s, t))
        sem = lambda n: ctx.enter_context(nc.semaphore(n))
        X = sb("X", [P, NT, D])
        XR = sb("XR", [P, NT, D])
        xrT = m.dt[:, 0, :]
        cv = m.dt[:, 1, :].rearrange("p (a s) -> p a s", a=2)
        XP = m.u_mem[:, :].rearrange("p (a s) -> p a s", s=KW - 1 + S)
        bc_p = [XR[:, 8 * i:8 * i + 8, :].rearrange("p a h -> p (a h)").bitcast(BF16) for i in range(2)] + \
               [X[:, 0:8, :].rearrange("p a h -> p (a h)").bitcast(BF16)]
        xc = sb("xc", [P, DH, T])
        sz = sb("sz", [P, DH, T])
        mv = sb("mv", [P, NT, 2])
        st6 = sb("st6", [P, NT, 6])
        rr = sb("rr", [P, 2, NT])
        rstd, rms = rr[:, 0, :], rr[:, 1, :]
        w_inT = sb("w_inT", [P, 4 * P])
        w_bcT = sb("w_bcT", [P, DH, P])
        w_dtT = sb("w_dtT", [P, DH, INNER])
        w_rT = sb("w_rT", [P, 2 * E])
        vec = sb("vec", [P, VECS])
        norm_w, conv_b, dt_b = vec[:, V_NORM:V_NORM + 1], vec[:, V_CB:V_CB + DH], vec[:, V_DTB:V_DTB + DH]
        conv_w = vec[:, V_CW:V_CW + DH * KW].rearrange("p (c k) -> p c k", c=DH)
        xn = sb("xn", [P, NT, D])
        two = lambda x: x.rearrange("p a h -> p (a h)").rearrange("p (r t) -> p r t", r=2)
        ab, rl, res = two(xn[:, 0:8, :]), two(xn[:, 8:16, :]), two(X[:, 8:16, :])
        L = sb("L", [P, NT * 2, E])
        top = sb("top", [P, NT * 2, E])
        idx = sb("idx", [P, NT * 2, E], U32)
        idf = sb("idf", [P, NT * 2, 2])
        dif = sb("dif", [P, NT * 2])
        pr = sb("pr", [P, NT * 2, 2])
        oh = sb("oh", [P, 2, NT * 2, E])
        cT = sb("cT", [P, 2, P])

        ld_x, ld_w, ld_e, ld_s, ld_c = sem("ld_x"), sem("ld_w"), sem("ld_e"), sem("ld_s"), sem("ld_c")
        consts = sem("p_consts")
        rr_in, rr_sqrt = sem("rr_in"), sem("rr_sqrt")
        v = sem("p_dve")
        a = sem("p_act")
        ln_done, xn_T, tok_T = sem("ln_done"), sem("xn_T"), sem("tok_T")
        zx_mm, xc_in, xc_done, z_done = sem("zx_mm"), sem("xc_in"), sem("xc_done"), sem("z_done")
        cv_ready, mm_dt, mm_bc, sp_abs, sp_rel, sp_ln, dt_done = [sem(n) for n in (
            "cv_ready", "mm_dt", "mm_bc", "sp_abs", "sp_rel", "sp_ln", "dt_done")]
        bc_hi, bc_done, rt_mm, rt_dif, rt_exp, cb_done, cb_T, cb_cp, cb_out, pt_out, lg = [sem(n) for n in (
            "bc_hi", "bc_done", "rt_mm", "rt_dif", "rt_exp", "cb_done", "cb_T", "cb_cp", "cb_out", "pt_out", "lg")]

        block = ctx.enter_context(nc.Block())

        @block.sync
        def _(sp):
            for h in range(4):
                sp.dma_start(X[:, 4 * h:4 * h + 4, :], d.x[:, 4 * h:4 * h + 4, :]).then_inc(ld_x, 16)
            sp.dma_start(m.ident[:, :], d.ident).then_inc(ld_c, 16)
            sp.dma_start(vec[:, :], d.vec).then_inc(ld_s, 16)
            sp.dma_start(w_inT[:, :], d.w_inT).then_inc(ld_w, 16)
            sp.dma_start(w_rT[:, :], d.w_rT).then_inc(ld_w, 16)
            sp.dma_start(w_bcT[:, :, :], d.w_bcT).then_inc(ld_w, 16)
            sp.dma_start(w_dtT[:, :, :], d.w_dtT).then_inc(ld_w, 16)
            sp.dma_start(m.iota8[:, :], d.iota8).then_inc(ld_w, 16)
            sp.dma_start(m.w_rdT[:, :, :], d.w_rdT).then_inc(ld_e, 16)
            sp.dma_start(m.sel[:, :, :, :], d.sel).then_inc(ld_e, 16)
            for g in range(2):
                sp.dma_start(m.wT[g][:, :, :], (d.w_gT, d.w_uT)[g]).then_inc(ld_e, 16)
            sp.dma_start(m.w_dnT[:, :, :, :], d.w_dnT).then_inc(ld_e, 16)
            sp.wait_ge(xc_done, 4)
            sp.dma_start(m.xc_dram, xc[:, :, :]).then_inc(cb_out, 16)
            sp.wait_ge(z_done, 8)
            sp.dma_start(m.sz_dram, sz[:, :, :]).then_inc(cb_out, 16)
            sp.wait_ge(cb_cp, 1)
            sp.dma_start(m.comb_dram[0:NT].rearrange("(g t) e n -> (t e) g n", g=2), cT[:, :, :]).then_inc(cb_out, 16)
            sp.dma_start(m.comb_dram[NT], cT[0:2 * E, 0, :]).then_inc(cb_out, 16)
            sp.wait_ge(bc_done, 4)
            for q in range(2):
                for part in range(3):
                    for ic in range(UNITS):
                        r0 = q * STATE + ic * UN
                        o0 = q * 48 + part * UN
                        sp.dma_start(m.PT[o0:o0 + UN, ic:UNITS * B * 2:UNITS, :],
                                     bc_p[part][r0:r0 + UN, :].rearrange("p (k t) -> p k t", t=BLK)).then_inc(pt_out, 16)
            sp.wait_ge(pt_out, 16 * 6 * UNITS)
            sp.wait_ge(cb_out, 64)
            sp.wait_ge(ld_e, 80)

        @block.gpsimd
        def _(pool):
            nc.gpsimd.memset(XP[:, :, 0:KW - 1], 0.0).then_inc(consts, 1)
            nc.gpsimd.memset(m.zeros[:, :], 0.0)
            nc.gpsimd.memset(m.PT[:, UNITS * B * 2, :], 0.0)

        @block.scalar
        def _(act):
            own = 0
            act.wait_ge(ld_s, 16)
            A_log = vec[:, V_A:V_A + DH * STATE].rearrange("p (c n) -> p c n", c=DH)
            nc.scalar.activation(m.A[:, :, :], A_log, ACT.Exp).then_inc(a, 1)
            act.wait_ge(a, 1)
            nc.scalar.mul(m.A[:, :, :], m.A[:, :, :], -1.0).then_inc(a, 1)
            act.wait_ge(rr_in, 1)
            nc.scalar.activation(rr[:, :, :], rr[:, :, :], ACT.Sqrt).then_inc(rr_sqrt, 1)
            for blk in range(4):
                for c in range(2):
                    act.wait_ge(zx_mm, 4 * blk + c + 1)
                    b, t0 = blk // 2, (blk % 2) * BLK
                    nc.scalar.copy(XP[:, c * B + b, KW - 1 + t0:KW - 1 + t0 + BLK], ps[4 + c][:, :]).then_inc(xc_in, 1)
                for c in range(2):
                    act.wait_ge(zx_mm, 4 * blk + 2 + c + 1)
                    nc.scalar.activation(sz[:, c, blk * BLK:(blk + 1) * BLK], ps[6 + c][:, :], ACT.Silu).then_inc(z_done, 1)
            for c in range(DH):
                for b in range(B):
                    i = c * B + b
                    act.wait_ge(cv_ready, i + 1)
                    nc.scalar.activation(xc[:, c, b * S:(b + 1) * S], cv[:, i % 2, :], ACT.Silu).then_inc(xc_done, 1)
            act.wait_ge(rt_dif, 1)
            nc.scalar.activation(dif[:, :], dif[:, :], ACT.Exp).then_inc(rt_exp, 1)
            i = 0
            for blk in range(4):
                act.wait_ge(mm_bc, blk + 1)
                nc.scalar.copy(bc_p[0][:, blk * BLK:(blk + 1) * BLK], ps[6 + blk % 2][:, :]).then_inc(bc_hi, 1)
                for o in range(DH):
                    act.wait_ge(mm_dt, i + 1)
                    if i >= 2:
                        act.wait_ge(dt_done, i - 1)
                    nc.scalar.activation(ab[:, i % 2, :], ps[4 + i % 2][:, :], ACT.Abs, bias=dt_b[:, o:o + 1]).then_inc(sp_abs, 1)
                    act.wait_ge(sp_abs, i + 1)
                    own += 1
                    nc.scalar.activation(ab[:, i % 2, :], ab[:, i % 2, :], ACT.Exp, scale=-1.0).then_inc(a, 1)
                    act.wait_ge(a, 2 + own)
                    nc.scalar.activation(ab[:, i % 2, :], ab[:, i % 2, :], ACT.Ln, bias=m.one[:, 0:1]).then_inc(sp_ln, 1)
                    i += 1

        @block.vector
        def _(dve):
            cnt = [0]

            def link(ins):
                cnt[0] += 1
                ins.then_inc(v, 1)
                dve.wait_ge(v, cnt[0])

            link(nc.vector.memset(m.one[:, :], 1.0))
            for t in range(NT):
                if t % 4 == 0:
                    dve.wait_ge(ld_x, 16 * 4)
                ins = nc.vector.bn_stats(st6[:, t, :], X[:, t, :])
            link(ins)
            for t in range(NT):
                ins = nc.vector.bn_aggr(mv[:, t, :], st6[:, t, :])
            link(ins)
            link(nc.vector.tensor_scalar(rr[:, 0, :], mv[:, :, 1], EPS_LN, None, ALU.add))
            link(nc.vector.reciprocal(rr[:, 1, :], rr[:, 0, :]))
            link(nc.vector.tensor_tensor(rr[:, 1, :], rr[:, 1, :], mv[:, :, 1], ALU.mult))
            nc.vector.tensor_scalar(rr[:, 1, :], rr[:, 1, :], EPS_RMS, None, ALU.add).then_inc(rr_in, 1)
            dve.wait_ge(rr_sqrt, 1)
            link(nc.vector.reciprocal(rr[:, :, :], rr[:, :, :]))
            for t in range(NT):
                ins = nc.vector.tensor_scalar(xn[:, t, :], X[:, t, :], mv[:, t, 0:1], rstd[:, t:t + 1], ALU.subtract, ALU.mult)
            link(ins)
            for t in range(NT):
                nc.vector.tensor_scalar(XR[:, t, :], xn[:, t, :], rms[:, t:t + 1], None, ALU.mult).then_inc(ln_done, 1)
            dve.wait_ge(ld_s, 16)
            nc.vector.tensor_copy(m.Dp[:, :], vec[:, V_D:V_D + DH])
            for q in range(4):
                dve.wait_ge(xn_T, 2 * q + 1)
                nc.vector.tensor_copy(m.xnT[:, q * BLK:(q + 1) * BLK], ps[4 + 2 * (q % 2)][:, :]).then_inc(tok_T, 1)
                dve.wait_ge(xn_T, 2 * q + 2)
                nc.vector.tensor_scalar(xrT[:, q * BLK:(q + 1) * BLK], ps[5 + 2 * (q % 2)][:, :], norm_w[:, 0:1], None, ALU.mult).then_inc(tok_T, 1)
            nc.vector.tensor_tensor(m.acc[:, :, :], X[:, :, :], xn[:, :, :], ALU.add).then_inc(lg, 1)
            dve.wait_ge(ld_w, 80)
            dve.wait_ge(rt_mm, 1)
            link(nc.vector.tensor_copy(L[:, :, :].rearrange("p a e -> p (a e)"), ps[3][:, 0:NT * 2 * E]))
            for r in range(NT * 2):
                ins = nc.vector.max(top[:, r, :], L[:, r, :])
            link(ins)
            nc.vector.tensor_tensor(dif[:, :], top[:, :, 1], top[:, :, 0], ALU.subtract).then_inc(rt_dif, 1)
            for r in range(NT * 2):
                ins = nc.vector.max_index(idx[:, r, :], top[:, r, :], L[:, r, :])
            link(ins)
            link(nc.vector.tensor_copy(idf[:, :, :], idx[:, :, 0:2]))
            for j in range(2):
                ins = nc.vector.tensor_tensor(oh[:, j, :, :], m.iota8[:, :].unsqueeze(1).to_broadcast([P, NT * 2, E]),
                                              idf[:, :, j:j + 1].to_broadcast([P, NT * 2, E]), ALU.is_equal)
            link(ins)
            n_x = 0
            for c in range(DH):
                for b in range(B):
                    i = c * B + b
                    dve.wait_ge(consts, 1)
                    dve.wait_ge(xc_in, 4 * b + 4)
                    if i >= 2:
                        dve.wait_ge(xc_done, i - 1)
                    link(nc.vector.tensor_scalar(cv[:, i % 2, :], XP[:, i, 0:S], conv_w[:, c, 0:1], conv_b[:, c:c + 1], ALU.mult, ALU.add))
                    for k in range(1, KW):
                        ins = nc.vector.scalar_tensor_tensor(cv[:, i % 2, :], XP[:, i, k:k + S], conv_w[:, c, k:k + 1], cv[:, i % 2, :], ALU.mult, ALU.add)
                        if k < KW - 1:
                            link(ins)
                    ins.then_inc(cv_ready, 1)
            dve.wait_ge(rt_exp, 1)
            link(nc.vector.tensor_scalar(pr[:, :, 0], dif[:, :], 1.0, None, ALU.add))
            link(nc.vector.reciprocal(pr[:, :, 0], pr[:, :, 0]))
            link(nc.vector.tensor_tensor(pr[:, :, 1], pr[:, :, 0], dif[:, :], ALU.mult))
            for j in range(2):
                link(nc.vector.tensor_tensor(oh[:, j, :, :], oh[:, j, :, :], pr[:, :, j:j + 1].to_broadcast([P, NT * 2, E]), ALU.mult))
            nc.vector.tensor_tensor(oh[:, 0, :, :], oh[:, 0, :, :], oh[:, 1, :, :], ALU.add).then_inc(cb_done, 1)
            dve.wait_ge(cb_T, 1)
            nc.vector.tensor_copy(cT[:, :, :].rearrange("p a n -> p (a n)"), ps[3][:, 0:2 * P]).then_inc(cb_cp, 1)
            i = 0
            for blk in range(4):
                c0 = slice(blk * BLK, (blk + 1) * BLK)
                dve.wait_ge(bc_hi, blk + 1)
                link(nc.vector.tensor_tensor(res[:, blk % 2, :], ps[6 + blk % 2][:, :], bc_p[0][:, c0], ALU.subtract))
                link(nc.vector.tensor_copy(bc_p[1][:, c0], res[:, blk % 2, :]))
                nc.vector.tensor_tensor(bc_p[2][:, c0], res[:, blk % 2, :], bc_p[1][:, c0], ALU.subtract).then_inc(bc_done, 1)
                for o in range(DH):
                    dve.wait_ge(sp_abs, i + 1)
                    link(nc.vector.tensor_scalar(rl[:, i % 2, :], ps[4 + i % 2][:, :], dt_b[:, o:o + 1], 0.0, ALU.add, ALU.max))
                    dve.wait_ge(sp_ln, i + 1)
                    nc.vector.scalar_tensor_tensor(m.dt[:, o, c0], ab[:, i % 2, :], 1e-4, rl[:, i % 2, :], ALU.add, ALU.add).then_inc(dt_done, 1)
                    dve.wait_ge(dt_done, i + 1)
                    dve.wait_ge(xc_done, 4)
                    nc.vector.tensor_tensor(m.u[:, o, c0], m.dt[:, o, c0], xc[:, o, c0], ALU.mult)
                    i += 1

        @block.tensor
        def _(pe):
            pe.wait_ge(ld_c, 16)
            for q in range(4):
                pe.wait_ge(ln_done, 4 * q + 4)
                for k, src in enumerate((xn, XR)):
                    if q >= 2:
                        pe.wait_ge(tok_T, 2 * (q - 2) + k + 1)
                    for j in range(4):
                        ins = nc.tensor.transpose(ps[4 + 2 * (q % 2) + k][:, j * P:(j + 1) * P], src[:, 4 * q + j, :], m.ident[:, :])
                    ins.then_inc(xn_T, 1)
            pe.wait_ge(ld_w, 80)
            pe.wait_ge(tok_T, 8)
            for blk in range(4):
                for c in range(4):
                    if blk:
                        pe.wait_ge(xc_in if c < 2 else z_done, 2 * (blk - 1) + c % 2 + 1)
                    nc.tensor.matmul(ps[4 + c][:, :], lhsT=w_inT[:, c * P:(c + 1) * P], rhs=xrT[:, blk * BLK:(blk + 1) * BLK],
                                     start=True, stop=True).then_inc(zx_mm, 1)
            for t in range(NT):
                ins = nc.tensor.matmul(ps[3][:, t * 2 * E:(t + 1) * 2 * E], lhsT=m.xnT[:, t * P:(t + 1) * P], rhs=w_rT[:, :],
                                       start=True, stop=True)
            ins.then_inc(rt_mm, 1)
            pe.wait_ge(cb_done, 1)
            for g in range(2):
                ins = nc.tensor.transpose(ps[3][:, g * P:(g + 1) * P],
                                          oh[:, 0, :, :].rearrange("p a e -> p (a e)")[:, g * P:(g + 1) * P], m.ident[:, :])
            ins.then_inc(cb_T, 1)
            pe.wait_ge(xc_done, 4)
            pe.wait_ge(z_done, 8)
            i = 0
            for blk in range(4):
                if blk >= 2:
                    pe.wait_ge(bc_done, blk - 1)
                for k in range(DH):
                    ins = nc.tensor.matmul(ps[6 + blk % 2][:, :], lhsT=w_bcT[:, k, :], rhs=xc[:, k, blk * BLK:(blk + 1) * BLK],
                                           start=(k == 0), stop=(k == DH - 1))
                ins.then_inc(mm_bc, 1)
                for o in range(DH):
                    if i >= 2:
                        pe.wait_ge(dt_done, i - 1)
                    for k in range(DH):
                        ins = nc.tensor.matmul(ps[4 + i % 2][:, :], lhsT=w_dtT[:, k, o * P:(o + 1) * P], rhs=xc[:, k, blk * BLK:(blk + 1) * BLK],
                                               start=(k == 0), stop=(k == DH - 1))
                    ins.then_inc(mm_dt, 1)
                    i += 1


def scan_and_experts(nc, d, m, ps):
    with ExitStack() as ctx:
        sb = lambda n, s, t=FP32: ctx.enter_context(nc.sbuf_tensor(n, s, t))
        sem = lambda n: ctx.enter_context(nc.semaphore(n))
        RA, RD, RH, RB = 4, 4, 4, 2
        AHEAD = 3
        Bs = sb("Bs", [P, RB, BLK])
        dA = sb("dA", [P, RA, DH, BLK])
        dBx = sb("dBx", [P, RD, DH, BLK])
        hh = dBx
        hC = sb("hC", [P, RH, DH, BLK])
        carry = sb("carry", [P, STATE, DH])
        cbb = sb("cbb", [P, 2 * E, P])
        xs = sb("xs", [P, 2 * E, P])
        yb = sb("yb", [P, 2, BLK])
        act_mem = sb("gate_act", [P, 2, FF])
        sg, gg = act_mem[:, 0, :], act_mem[:, 1, :]
        eo = act_mem[:, :, :].rearrange("p a n -> p (a n)")
        inter = sb("inter", [P, FF])
        interT = sb("interT", [P, KC, P])
        Ld = sb("Ld", [P, E])
        top = sb("topd", [P, E])
        idx = sb("idxd", [P, E], U32)
        idf = sb("idfd", [P, 2])
        dif = sb("difd", [P, 1])
        edif = sb("edif", [P, 1])
        pr = sb("prd", [P, 2])
        cd = sb("cd", [P, 2, E])

        psB, psC, psY, G, U = ps[0:2], ps[2:4], ps[4:6], ps[6], ps[7]
        s_psB, s_Bs, s_dA, s_dBx, s_psC, s_scan, s_hC, s_y, s_carry = [sem(n) for n in (
            "psB_full", "Bs_full", "dA_full", "dBx_full", "psC_full", "scanned", "hC_full", "y_added", "carried")]
        s_cbb, s_xs, s_gate, s_up, s_tanh, s_gg, s_int, s_intT, s_intE, s_lg, s_lgc, s_dif, s_exp, s_dn0, s_dn1, s_cd, s_cmb, s_sum, s_out, s_q = [
            sem(n) for n in ("cbb_full", "xs_full", "gate_done", "up_done", "tanh_done", "gg_done",
                             "inter_done", "interT_mm", "interT_done", "logits_mm", "logits_out", "dif_done", "exp_done", "down0", "down1",
                             "weights_done", "weighted", "summed", "tile_out", "dve_own")]
        s_zero, s_yst, s_at, s_yout, s_init = sem("carry_zero"), sem("y_stored"), sem("reached"), sem("y_out"), sem("first_set")
        OFF = 4

        block = ctx.enter_context(nc.Block())

        def loops(eng, body, start_block, end_block):
            with eng.Fori(0, B, 1) as b:
                cb = b * (2 * STATE)
                with eng.Fori(0, 2, 1) as tc:
                    ct = tc * STATE
                    start_block(cb, ct)
                    with eng.Fori(0, UNITS, 1) as ic:
                        body(cb, ct, ic * UN)
                    end_block(cb, ct)

        nothing = lambda cb, ct: None

        @block.sync
        def _(sp):
            rows = m.comb_dram.rearrange("t e n -> t (e n)")
            sp.dma_start(cbb[:, :, :].rearrange("p e n -> p (e n)"), rows[0:1, :].to_broadcast([P, 2 * E * P])).then_inc(s_cbb, 16)

            def body(cb, ct, n0):
                q = (cb + ct + n0) // UN
                sp.wait_ge(s_xs, 2 * q + 2)
                sp.dma_start(cbb[:, :, :].rearrange("p e n -> p (e n)"),
                             rows[bass.ds(q + 1, 1), :].to_broadcast([P, 2 * E * P])).then_inc(s_cbb, 16)

            def end_block(cb, ct):
                blk = (cb + ct) // STATE
                sp.wait_ge(s_yout, blk + 1)
                sp.dma_start(m.y_dram[bass.ds(blk, 1), :, :].rearrange("a p c -> p (a c)"), yb[:, :, :].rearrange("p j c -> p (j c)")).then_inc(s_yst, 16)

            loops(sp, body, nothing, end_block)
            sp.wait_ge(s_yst, 16 * (2 * B + 1))
            sp.wait_ge(s_cbb, 16 * (NT + 1))

        @block.scalar
        def _(act):
            act.sem_inc(s_Bs, OFF)
            act.sem_inc(s_dA, OFF)

            def copy_B(N, s):
                act.wait_ge(s_psB, N + (s + 1))
                act.wait_ge(s_dBx, N + (OFF + s - RB + 1))
                nc.scalar.copy(Bs[:, s % RB, :], psB[s % 2][:, :]).then_inc(s_Bs, 1)

            def turned(q):
                act.wait_ge(s_intT, q + 1)
                nc.scalar.copy(interT[:, :, :].rearrange("p k n -> p (k n)"), G[:, :]).then_inc(s_intE, 1)

            def exp_dif(q):
                act.wait_ge(s_dif, q + 1)
                nc.scalar.activation(edif[:, :], dif[:, :], ACT.Exp).then_inc(s_exp, 1)

            def weigh(q, half):
                if half:
                    act.wait_ge(s_cd, q + 1)
                act.wait_ge((s_dn0, s_dn1)[half], q + 1)
                for j in range(4):
                    e = 4 * half + j
                    ins = nc.scalar.mul(eo[:, e * P:(e + 1) * P], (U, G)[half][:, j * P:(j + 1) * P], cd[:, 0, e:e + 1])
                ins.then_inc(s_cmb, 1)

            def body(cb, ct, n0):
                N = cb + ct + n0
                t0 = (cb + ct) * 8
                q = N // UN
                for s in range(UN):
                    copy_B(N, s)
                    act.wait_ge(s_scan, N + (OFF + s - RA + 1))
                    nc.scalar.activation(dA[:, s % RA, 0, :], m.dt[:, 0, bass.ds(t0, BLK)], ACT.Exp, scale=m.A[:, 0, bass.ds(n0 + s, 1)])
                    nc.scalar.activation(dA[:, s % RA, 1, :], m.dt[:, 1, bass.ds(t0, BLK)], ACT.Exp, scale=m.A[:, 1, bass.ds(n0 + s, 1)]).then_inc(s_dA, 1)
                    if s == 2:
                        turned(q)
                    if s == 5:
                        exp_dif(q)
                    if s == 7:
                        weigh(q, 1)
                    if s == 8:
                        weigh(q, 0)
                    if s == 13:
                        act.wait_ge(s_gate, q + 2)
                        act.wait_ge(s_out, q + 1)
                        nc.scalar.activation(sg, G[:, :], ACT.Tanh, scale=0.5).then_inc(s_tanh, 1)

            loops(act, body, nothing, nothing)
            copy_B(B * 2 * STATE, 0)
            turned(NT)
            exp_dif(NT)
            weigh(NT, 1)
            weigh(NT, 0)

        @block.gpsimd
        def _(pool):
            nc.gpsimd.memset(inter[:, :], 0.0).then_inc(s_int, 1)
            nc.gpsimd.memset(m.accx[:, 0, :], 0.0).then_inc(s_init, 1)
            pool.wait_ge(s_init, 1)
            pool.sem_inc(s_dBx, OFF)

            def add_up(q, sq):
                pool.wait_ge(s_cmb, 2 * q + 2)
                n = E * P
                for step in range(3):
                    n //= 2
                    if step:
                        pool.wait_ge(s_sum, sq + step)
                    nc.gpsimd.tensor_tensor(eo[:, 0:n], eo[:, 0:n], eo[:, n:2 * n], ALU.add).then_inc(s_sum, 1)
                pool.wait_ge(s_sum, sq + 3)
                pool.sem_inc(s_at, 1)
                a = m.accx[:, bass.ds(q, 1), :].rearrange("p a h -> p (a h)") if not isinstance(q, int) else m.accx[:, q, :]
                nc.gpsimd.tensor_tensor(a, a, eo[:, 0:P], ALU.add).then_inc(s_out, 1)

            def body(cb, ct, n0):
                N = cb + ct + n0
                t0 = (cb + ct) * 8
                q = N // UN
                for s in range(UN):
                    pool.wait_ge(s_Bs, N + (OFF + s + 1))
                    pool.wait_ge(s_hC, N + (OFF + s - RD + 1))
                    pool.sem_inc(s_at, 1)
                    nc.gpsimd.tensor_tensor(dBx[:, s % RD, :, :], m.u[:, :, bass.ds(t0, BLK)],
                                            Bs[:, s % RB, :].unsqueeze(1).to_broadcast([P, DH, BLK]), ALU.mult).then_inc(s_dBx, 1)
                    if s in (3, 6):
                        gu = s // 6
                        pool.wait_ge(s_cbb, q * 16 + 16)
                        pool.wait_ge((s_gate, s_up)[gu], q + 1)
                        pool.sem_inc(s_at, 1)
                        nc.gpsimd.tensor_tensor(xs[:, gu * E:(gu + 1) * E, :], cbb[:, gu * E:(gu + 1) * E, :],
                                                m.xnT[:, bass.ds(N * 8, P)].unsqueeze(1).to_broadcast([P, E, P]), ALU.mult).then_inc(s_xs, 1)
                    if s == 10:
                        add_up(q, 3 * q)

            loops(pool, body, nothing, nothing)
            add_up(NT, 3 * NT)

        @block.vector
        def _(dve):
            dve.sem_inc(s_scan, OFF)
            dve.sem_inc(s_hC, OFF)
            dve.sem_inc(s_yst, 16)

            OWN = 7

            def link(ins):
                ins.then_inc(s_q, 1)

            def router(q, step):
                own = q * OWN
                if step == 0:
                    dve.wait_ge(s_lg, q + 1)
                    nc.vector.tensor_copy(Ld[:, :], G[:, 0:E]).then_inc(s_lgc, 1)
                if step == 1:
                    dve.wait_ge(s_init, 1)
                    dve.wait_ge(s_lgc, q + 1)
                    link(nc.vector.max(top[:, :], Ld[:, :]))
                if step == 2:
                    dve.wait_ge(s_q, own + 1)
                    nc.vector.tensor_tensor(dif[:, :], top[:, 1:2], top[:, 0:1], ALU.subtract).then_inc(s_dif, 1)
                    link(nc.vector.max_index(idx[:, :], top[:, :], Ld[:, :]))
                if step == 3:
                    dve.wait_ge(s_q, own + 2)
                    link(nc.vector.tensor_copy(idf[:, :], idx[:, 0:2]))
                if step == 4:
                    dve.wait_ge(s_exp, q + 1)
                    link(nc.vector.tensor_scalar(pr[:, 0:1], edif[:, :], 1.0, None, ALU.add))
                if step == 5:
                    dve.wait_ge(s_q, own + 4)
                    link(nc.vector.reciprocal(pr[:, 0:1], pr[:, 0:1]))
                    dve.wait_ge(s_q, own + 5)
                    link(nc.vector.tensor_tensor(pr[:, 1:2], pr[:, 0:1], edif[:, :], ALU.mult))
                if step == 6:
                    nc.vector.tensor_scalar(cd[:, 0, :], m.iota8[:, :], idf[:, 0:1], pr[:, 0:1], ALU.is_equal, ALU.mult)
                    dve.wait_ge(s_q, own + 6)
                    link(nc.vector.tensor_scalar(cd[:, 1, :], m.iota8[:, :], idf[:, 1:2], pr[:, 1:2], ALU.is_equal, ALU.mult))
                if step == 7:
                    dve.wait_ge(s_q, own + 7)
                    nc.vector.tensor_tensor(cd[:, 0, :], cd[:, 0, :], cd[:, 1, :], ALU.add).then_inc(s_cd, 1)

            def times_C(N, s):
                dve.wait_ge(s_psC, N + (s + 1))
                dve.wait_ge(s_y, N + (OFF + s - RH + 1))
                nc.vector.tensor_tensor(hC[:, s % RH, :, :], hh[:, s % RD, :, :],
                                        psC[s % 2][:, :].unsqueeze(1).to_broadcast([P, DH, BLK]), ALU.mult).then_inc(s_hC, 1)

            def body(cb, ct, n0):
                N = cb + ct + n0
                q = N // UN
                for s in range(UN):
                    dve.wait_ge(s_dA, N + (OFF + s + 1))
                    dve.wait_ge(s_dBx, N + (OFF + s + 1))
                    for h in range(DH):
                        ins = nc.vector.tensor_tensor_scan(hh[:, s % RD, h, :], dA[:, s % RA, h, :], dBx[:, s % RD, h, :],
                                                           carry[:, bass.ds(n0 + s, 1), h], ALU.mult, ALU.add)
                    ins.then_inc(s_scan, 1)
                    if 2 <= s < 6:
                        router(q, 2 * s - 4)
                    if s:
                        times_C(N, s - 1)
                    if 2 <= s < 6:
                        router(q, 2 * s - 3)
                    if s == 12:
                        dve.wait_ge(s_tanh, q + 1)
                        nc.vector.scalar_tensor_tensor(gg, sg, 1.0, G[:, :], ALU.add, ALU.mult).then_inc(s_gg, 1)
                    if s == 15:
                        dve.wait_ge(s_gg, q + 1)
                        dve.wait_ge(s_up, q + 2)
                        nc.vector.scalar_tensor_tensor(inter[:, :], gg, 0.5, U[:, :], ALU.mult, ALU.mult).then_inc(s_int, 1)
                    dve.wait_ge(s_scan, N + (OFF + s + 1))
                    nc.vector.tensor_scalar(carry[:, bass.ds(n0 + s, 1), :].rearrange("p n h -> p (n h)"), hh[:, s % RD, :, BLK - 1],
                                            1.0, None, ALU.mult).then_inc(s_carry, 1)
                times_C(N, UN - 1)

            with dve.Fori(0, B, 1) as b:
                cb = b * (2 * STATE)
                nc.vector.memset(carry[:, :, :], 0.0).then_inc(s_zero, 1)
                with dve.Fori(0, 2, 1) as tc:
                    ct = tc * STATE
                    dve.wait_ge(s_zero, b + 1)
                    dve.wait_ge(s_carry, cb + ct)
                    dve.sem_inc(s_at, 1)
                    with dve.Fori(0, UNITS, 1) as ic:
                        body(cb, ct, ic * UN)
                    blk = (cb + ct) // STATE
                    dve.wait_ge(s_y, cb + ct + (OFF + STATE))
                    dve.wait_ge(s_yst, blk * 16 + 16)
                    for j in range(2):
                        ins = nc.vector.tensor_copy(yb[:, j, :], psY[j][:, :])
                    ins.then_inc(s_yout, 1)
            for step in range(8):
                router(NT, step)

        @block.tensor
        def _(pe):
            pe.sem_inc(s_y, OFF)
            pe.sem_inc(s_gate, 1)
            pe.sem_inc(s_up, 1)
            gate = [(0, e) for e in range(E)]
            up = [(1, e) for e in range(E)]
            plan = {6: gate[0:2], 7: gate[2:4], 8: gate[4:6], 9: gate[6:8],
                    10: up[0:2], 11: up[2:4], 12: up[4:5], 13: up[5:7], 14: up[7:8]}
            down = {1: [(0, 0), (0, 1)], 2: [(0, 2), (0, 3)], 3: [(1, 0), (1, 1)], 4: [(1, 2), (1, 3)]}

            def units(q, s):
                return m.PT[0:96, bass.ds(q + s // UN, 1), :].rearrange("p a t -> p (a t)")

            def bcast_B(N, q, s):
                if s >= 2 or not isinstance(N, int):
                    pe.wait_ge(s_Bs, N + (OFF + s - 2 + 1))
                nc.tensor.matmul(psB[s % 2][:, :], lhsT=m.sel[:, 0, s % UN, :], rhs=units(q, s), start=True, stop=True).then_inc(s_psB, 1)

            def bcast_C(N, q, s):
                pe.wait_ge(s_hC, N + (OFF + s - 2 + 1))
                nc.tensor.matmul(psC[s % 2][:, :], lhsT=m.sel[:, 1, s % UN, :], rhs=units(q, s), start=True, stop=True).then_inc(s_psC, 1)

            def add_y(N, s):
                pe.wait_ge(s_hC, N + (OFF + s + 1))
                for t in range(4):
                    for h in range(DH):
                        j = t * DH + h
                        ins = nc.tensor.matmul(psY[j // 4][:, (j % 4) * P:(j % 4 + 1) * P], lhsT=hC[:, s % RH, h, t * P:(t + 1) * P],
                                               rhs=m.ident[:, :], is_transpose=True, start=False, stop=False, skip_group_check=True)
                ins.then_inc(s_y, 1)

            def inter_T(q):
                pe.wait_ge(s_int, q + 1)
                for k in range(KC):
                    ins = nc.tensor.transpose(G[:, k * P:(k + 1) * P], inter[:, k * P:(k + 1) * P], m.ident[:, :])
                ins.then_inc(s_intT, 1)

            def down_products(q, s):
                if s == 1:
                    pe.wait_ge(s_intE, q + 1)
                    for k in range(KC):
                        ins = nc.tensor.matmul(G[:, 0:E], lhsT=interT[:, k, :], rhs=m.w_rdT[:, k, :], start=(k == 0), stop=(k == KC - 1))
                    ins.then_inc(s_lg, 1)
                for half, k in down.get(s, []):
                    if half and k == 0:
                        pe.wait_ge(s_lgc, q + 1)
                    ins = nc.tensor.matmul((U, G)[half][:, :], lhsT=interT[:, k, :],
                                           rhs=m.w_dnT[:, k, 4 * half:4 * half + 4, :].rearrange("p e h -> p (e h)"),
                                           start=(k == 0), stop=(k == KC - 1))
                    if k == KC - 1:
                        ins.then_inc((s_dn0, s_dn1)[half], 1)

            def body(cb, ct, n0):
                N = cb + ct + n0
                q = N // UN
                for s in range(UN):
                    bcast_B(N, q, s + AHEAD)
                    if s == 0:
                        inter_T(q)
                    down_products(q, s)
                    for gu, e in plan.get(s, []):
                        if e == 0:
                            pe.wait_ge(s_xs, 2 * q + (1 + gu))
                            pe.wait_ge(s_cmb, 2 * q + (1 + gu))
                        ins = nc.tensor.matmul((G, U)[gu][:, :], lhsT=xs[:, gu * E + e, :], rhs=m.wT[gu][:, e, :], start=(e == 0), stop=(e == E - 1))
                        if e == E - 1:
                            ins.then_inc((s_gate, s_up)[gu], 1)
                    bcast_C(N, q, s + 1)
                    if s:
                        add_y(N, s - 1)
                add_y(N, UN - 1)

            def start_block(cb, ct):
                for j in range(2):
                    nc.tensor.matmul(psY[j][:, :], lhsT=m.zeros[:, 0:P], rhs=m.zeros[:, :], start=True, stop=False, skip_group_check=True)

            def end_block(cb, ct):
                pe.wait_ge(s_yout, (cb + ct) // STATE + 1)

            for s in range(AHEAD):
                bcast_B(0, 0, s)
            bcast_C(0, 0, 0)
            loops(pe, body, start_block, end_block)
            inter_T(NT)
            for s in range(1, 5):
                down_products(NT, s)


def gate_and_project(nc, d, m, ps):
    with ExitStack() as ctx:
        sb = lambda n, s, t=FP32: ctx.enter_context(nc.sbuf_tensor(n, s, t))
        sem = lambda n: ctx.enter_context(nc.semaphore(n))
        yg = sb("yg", [P, 2, DH, BLK])
        w_oT = sb("w_oT", [P, DH, D])
        y = sb("y", [P, T // BLK, 2 * BLK])
        xc = sb("xc2", [P, DH, T])
        sz = sb("sz2", [P, DH, T])
        ld = sem("y_loaded")
        y_T, y_dx, y_gated, y_mm, y_acc = [sem(n) for n in ("y_T", "y_dx", "y_gated", "y_mm", "y_acc")]
        block = ctx.enter_context(nc.Block())
        NB4 = T // BLK

        @block.sync
        def _(sp):
            sp.dma_start(w_oT[:, :, :], d.w_oT).then_inc(ld, 16)
            sp.dma_start(y[:, :, :], m.y_dram.rearrange("k p c -> p k c")).then_inc(ld, 16)
            sp.dma_start(xc[:, :, :], m.xc_dram).then_inc(ld, 16)
            sp.dma_start(sz[:, :, :], m.sz_dram).then_inc(ld, 16)

        @block.tensor
        def _(pe):
            pe.wait_ge(ld, 64)
            for i in range(NB4 + 1):
                if i < NB4:
                    for h in range(DH):
                        if i >= 2:
                            pe.wait_ge(y_dx, 2 * (i - 2) + h + 1)
                        for t in range(4):
                            ins = nc.tensor.transpose(ps[2 * (i % 2) + h][:, t * P:(t + 1) * P], y[:, i, (t * DH + h) * P:(t * DH + h + 1) * P], m.ident[:, :])
                        ins.then_inc(y_T, 1)
                if i >= 1:
                    k = i - 1
                    pe.wait_ge(y_gated, 2 * k + 2)
                    if k >= 2:
                        pe.wait_ge(y_acc, k - 1)
                    for t in range(4):
                        for h in range(DH):
                            ins = nc.tensor.matmul(ps[4 + k % 2][:, t * P:(t + 1) * P], lhsT=yg[:, k % 2, h, t * P:(t + 1) * P], rhs=w_oT[:, h, :],
                                                   start=(h == 0), stop=(h == DH - 1))
                    ins.then_inc(y_mm, 1)

        @block.vector
        def _(dve):
            dve.wait_ge(ld, 64)
            for i in range(NB4 + 1):
                if i < NB4:
                    for h in range(DH):
                        c = slice(i * BLK, (i + 1) * BLK)
                        dve.wait_ge(y_T, 2 * i + h + 1)
                        if i >= 2:
                            dve.wait_ge(y_mm, i - 1)
                        nc.vector.scalar_tensor_tensor(yg[:, i % 2, h, :], xc[:, h, c], m.Dp[:, h:h + 1], ps[2 * (i % 2) + h][:, :],
                                                       ALU.mult, ALU.add).then_inc(y_dx, 1)
                        dve.wait_ge(y_dx, 2 * i + h + 1)
                        nc.vector.tensor_tensor(yg[:, i % 2, h, :], yg[:, i % 2, h, :], sz[:, h, c], ALU.mult).then_inc(y_gated, 1)
                if i >= 1:
                    k = i - 1
                    dve.wait_ge(y_mm, k + 1)
                    a = m.accx[:, 1 + 4 * k:5 + 4 * k, :].rearrange("p t h -> p (t h)")
                    nc.vector.tensor_tensor(a, ps[4 + k % 2][:, :], a, ALU.add).then_inc(y_acc, 1)



def second_norm(nc, d, m, ps):
    with ExitStack() as ctx:
        sb = lambda n, s, t=FP32: ctx.enter_context(nc.sbuf_tensor(n, s, t))
        sem = lambda n: ctx.enter_context(nc.semaphore(n))
        st6, mv, r1 = sb("n_st6", [P, NT, 6]), sb("n_mv", [P, NT, 2]), sb("n_r", [P, NT])
        v, n_in, n_sqrt, n_done, n_mm, n_cp = [sem(n) for n in ("n_dve", "n_in", "n_sqrt", "n_done", "n_mm", "n_cp")]
        block = ctx.enter_context(nc.Block())

        @block.vector
        def _(dve):
            cnt = [0]

            def link(ins):
                cnt[0] += 1
                ins.then_inc(v, 1)
                dve.wait_ge(v, cnt[0])

            for t in range(NT):
                ins = nc.vector.bn_stats(st6[:, t, :], m.acc[:, t, :])
            link(ins)
            for t in range(NT):
                ins = nc.vector.bn_aggr(mv[:, t, :], st6[:, t, :])
            link(ins)
            nc.vector.tensor_scalar(r1[:, :], mv[:, :, 1], EPS_LN, None, ALU.add).then_inc(n_in, 1)
            dve.wait_ge(n_sqrt, 1)
            link(nc.vector.reciprocal(r1[:, :], r1[:, :]))
            for t in range(NT):
                nc.vector.tensor_scalar(m.xn2[:, t, :], m.acc[:, t, :], mv[:, t, 0:1], r1[:, t:t + 1], ALU.subtract, ALU.mult).then_inc(n_done, 1)
            for q in range(4):
                dve.wait_ge(n_mm, q + 1)
                nc.vector.tensor_copy(m.xn2T[:, q * BLK:(q + 1) * BLK], ps[q][:, :]).then_inc(n_cp, 1)
            dve.wait_ge(n_done, NT)
            nc.vector.tensor_copy(m.yatt[:, :, :], m.xn2[:, :, :])

        @block.scalar
        def _(act):
            act.wait_ge(n_in, 1)
            nc.scalar.activation(r1[:, :], r1[:, :], ACT.Sqrt).then_inc(n_sqrt, 1)

        @block.tensor
        def _(pe):
            for q in range(4):
                pe.wait_ge(n_done, 4 * q + 4)
                for j in range(4):
                    ins = nc.tensor.transpose(ps[q][:, j * P:(j + 1) * P], m.xn2[:, 4 * q + j, :], m.ident[:, :])
                ins.then_inc(n_mm, 1)


def attention(nc, d, m, psum):
    ORDER = [7, 0, 6, 1, 5, 2, 4, 3]
    items = []
    entries = []
    for b in range(B):
        mine = [("s", b, qt, h) for qt in ORDER for h in range(2)]
        for at, w in ((3, 0), (7, 1), (11, 2)):
            mine.insert(at + w, ("p", 1 - b, w, 0))
        entries += mine
    items = [e for e in entries if e[0] == "s"]
    NE, NI, NP = len(entries), len(items), len(items) // 2
    entry_of = [i for i, e in enumerate(entries) if e[0] == "s"]
    last_w = max(i for i, e in enumerate(entries) if e[0] == "p" and e[1] == 1)
    PRO = 3
    LT, LV, LP = 2, 4, 3
    entry = lambda k: entry_of[k % NI] + (k // NI) * NE

    with ExitStack() as ctx:
        sb = lambda n, s, t=FP32: ctx.enter_context(nc.sbuf_tensor(n, s, t))
        sem = lambda n: ctx.enter_context(nc.semaphore(n))
        wqkv = sb("wqkv", [P, 3, P])
        wo = sb("wo", [P, HP + 1, D])
        identb = sb("identb", [P, P], BF16)
        maskb = sb("maskb", [P, P], BF16)
        qT = sb("qT", [P, B, S])
        kT = sb("kT", [P, B, S])
        V = sb("V", [P, B, QT, P])
        Pr = sb("Pr", [P, 4, S])
        PT = sb("PTs", [P, 4, S])
        nmax = sb("nmax", [P, 2])
        rsum = sb("rsum", [P, 8])
        rinv = sb("rinv", [P, 8])
        O = sb("O", [P, 2, P])
        OT = sb("OT", [P, 2, P])

        slot = [psum[:, 0:2, :].rearrange("p a t -> p (a t)"), psum[:, 2:4, :].rearrange("p a t -> p (a t)")]
        pPT = psum[:, 4:6, :].rearrange("p a t -> p (a t)")
        pO, pW = psum[:, 6, :], psum[:, 7, :]

        a_ld, a_w, a_z = sem("a_ld"), sem("a_w"), sem("a_zero")
        s_full, s_free, s_max, s_T, s_ev, s_PV, s_norm, s_oT, s_oTs, s_Wo, s_add = [sem("a_" + n) for n in (
            "slot_full", "slot_free", "max", "PT_mm", "PT_out", "O_mm", "O_out", "OT_mm", "OT_out", "Wo_mm", "added")]
        OFF = 8
        block = ctx.enter_context(nc.Block())

        @block.sync
        def _(sp):
            sp.dma_start(wqkv[:, :, :], d.wqkv[0]).then_inc(a_w, 16)
            sp.dma_start(wo[:, 1:HP + 1, :], d.wo).then_inc(a_ld, 16)
            sp.dma_start(identb[:, :], d.identb).then_inc(a_ld, 16)
            sp.dma_start(maskb[:, :], d.maskb).then_inc(a_ld, 16)
            with sp.Fori(0, HP, 1) as hp:
                sp.wait_ge(s_full, hp * NE + (PRO + last_w + 1))
                sp.dma_start(wqkv[:, :, :].rearrange("p a e -> p (a e)"),
                             d.wqkv.rearrange("n p a e -> n p (a e)")[bass.ds(hp + 1, 1)].rearrange("n p e -> (n p) e")).then_inc(a_w, 16)

        @block.gpsimd
        def _(pool):
            nc.gpsimd.memset(wo[:, 0, :], 0.0).then_inc(a_z, 1)
            nc.gpsimd.memset(V[:, 1, :, :], 0.0).then_inc(a_z, 1)
            nc.gpsimd.memset(Pr[:, :, :], 0.0).then_inc(a_z, 1)
            nc.gpsimd.memset(PT[:, :, :], 0.0).then_inc(a_z, 1)
            nc.gpsimd.memset(rsum[:, :], 1.0)
            nc.gpsimd.memset(rinv[:, :], 1.0).then_inc(a_z, 1)
            nc.gpsimd.memset(O[:, :, :], 0.0).then_inc(a_z, 1)

        @block.tensor
        def _(pe):
            pe.sem_inc(s_T, OFF - LT)
            pe.sem_inc(s_PV, OFF - LV)
            pe.sem_inc(s_oT, OFF - LP)
            pe.sem_inc(s_Wo, OFF - LP)
            pe.wait_ge(a_ld, 48)
            pe.wait_ge(a_z, 6)

            def project(base, i, e, wbase):
                _, b, w, _ = e
                pe.wait_ge(s_free, base + (OFF + i - 1))
                pe.wait_ge(a_w, wbase)
                if w < 2:
                    for c in range(2):
                        ins = nc.tensor.matmul(slot[i % 2][:, c * BLK:(c + 1) * BLK], lhsT=wqkv[:, w, :],
                                               rhs=m.xn2T[:, b * S + c * BLK:b * S + (c + 1) * BLK], start=True, stop=True)
                else:
                    for t in range(QT):
                        ins = nc.tensor.matmul(slot[i % 2][:, t * P:(t + 1) * P], lhsT=m.xn2T[:, b * S + t * P:b * S + (t + 1) * P],
                                               rhs=wqkv[:, 2, :], start=True, stop=True)
                ins.then_inc(s_full, 1)

            def scores(base, i, e):
                _, b, qt, h = e
                n = (qt + 1) * P
                r = slice(h * HS, (h + 1) * HS)
                pe.wait_ge(s_free, base + (OFF + i - 1))
                for c in range(0, n, BLK):
                    w = min(BLK, n - c)
                    last = c + w == n
                    if last:
                        nc.tensor.matmul(slot[i % 2][:, n - P:n], lhsT=identb[:, :], rhs=maskb[:, :], start=True, stop=False, skip_group_check=True)
                    ins = nc.tensor.matmul(slot[i % 2][:, c:c + w], lhsT=qT[r, b, qt * P:(qt + 1) * P], rhs=kT[r, b, c:c + w],
                                           start=not last, stop=True, skip_group_check=True)
                ins.then_inc(s_full, 1)

            def values(base, k):
                _, b, qt, h = items[k % NI]
                pe.wait_ge(s_ev, base + (OFF + k + 1))
                pe.wait_ge(s_norm, base + (OFF + k))
                for t in range(qt + 1):
                    ins = nc.tensor.matmul(pO[:, 0:HS], lhsT=PT[:, k % 4, t * P:(t + 1) * P], rhs=V[:, b, t, h * HS:(h + 1) * HS],
                                           start=(t == 0), stop=(t == qt))
                ins.then_inc(s_PV, 1)

            def turn(base, ebase, k):
                _, b, qt, h = items[k % NI]
                pe.wait_ge(s_free, ebase + (OFF + PRO + entry(k) + 1))
                pe.wait_ge(s_ev, base + (OFF + k))
                for t in range(qt + 1):
                    ins = nc.tensor.transpose(pPT[:, t * P:(t + 1) * P], Pr[:, k % 4, t * P:(t + 1) * P], m.ident[:, :])
                ins.then_inc(s_T, 1)

            def pair_turn(pbase, kbase, p):
                pe.wait_ge(s_norm, kbase + (OFF + 2 * p + 2))
                pe.wait_ge(s_add, pbase + (OFF + p))
                nc.tensor.transpose(pW[:, 0:P], O[:, p % 2, :], m.ident[:, :]).then_inc(s_oT, 1)

            def pair_out(pbase, p, w):
                pe.wait_ge(s_oTs, pbase + (OFF + p + 1))
                nc.tensor.matmul(pW[:, 0:D], lhsT=OT[:, p % 2, :], rhs=w, start=True, stop=True).then_inc(s_Wo, 1)

            for w in range(3):
                project(0, w, ("p", 0, w, 0), 16)
            with pe.Fori(0, HP, 1) as hp:
                kb, eb, pb = hp * NI, hp * NE, hp * NP
                wo_of = lambda p: wo[:, bass.ds(hp + (0 if p < 0 else 1), 1), :].rearrange("p a e -> p (a e)")
                k = 0
                for i, e in enumerate(entries):
                    if e[0] == "p":
                        project(eb, PRO + i, e, hp * 16 + (16 if e[1] == 1 else 32))
                        continue
                    scores(eb, PRO + i, e)
                    values(kb, k - LV)
                    turn(kb, eb, k - LT)
                    if k % 2 == 0:
                        pair_turn(pb, kb, k // 2 - LP)
                    else:
                        pair_out(pb, k // 2 - LP, wo_of(k // 2 - LP))
                    k += 1
            kb, pb = HP * NI, HP * NP
            for k in range(2 * LP):
                if k < LV:
                    values(kb, k - LV)
                if k < LT:
                    turn(kb, HP * NE, k - LT)
                if k % 2 == 0:
                    pair_turn(pb, kb, k // 2 - LP)
                else:
                    pair_out(pb, k // 2 - LP, wo[:, HP, :])

        @block.scalar
        def _(act):
            act.sem_inc(s_free, OFF)
            act.sem_inc(s_oTs, OFF - LP)
            act.wait_ge(a_z, 6)

            def projected(base, kbase, i, e, k):
                _, b, w, _ = e
                act.wait_ge(s_full, base + (i + 1))
                if w == 0:
                    ins = nc.scalar.mul(qT[:, b, :], slot[i % 2], HS ** -0.5)
                elif w == 1:
                    ins = nc.scalar.copy(kT[:, b, :], slot[i % 2])
                else:
                    if k is not None:
                        act.wait_ge(s_PV, kbase + (OFF + k))
                    ins = nc.scalar.copy(V[:, b, :, :].rearrange("p t e -> p (t e)"), slot[i % 2])
                ins.then_inc(s_free, 1)

            def pair_copy(pbase, p):
                act.wait_ge(s_oT, pbase + (OFF + p + 1))
                act.wait_ge(s_Wo, pbase + (OFF + p - 1))
                nc.scalar.copy(OT[:, p % 2, :], pW[:, 0:P]).then_inc(s_oTs, 1)

            for w in range(3):
                projected(0, 0, w, ("p", 0, w, 0), None)
            with act.Fori(0, HP, 1) as hp:
                kb, eb, pb = hp * NI, hp * NE, hp * NP
                k = 0
                for i, e in enumerate(entries):
                    if e[0] == "p":
                        projected(eb, kb, PRO + i, e, 0 if e[1] == 1 else NI // 2)
                        continue
                    n = (e[2] + 1) * P
                    act.wait_ge(s_max, kb + (OFF + k + 1))
                    act.wait_ge(s_T, kb + (OFF + k - 3))
                    nc.scalar.activation(Pr[:, k % 4, 0:n], slot[(PRO + i) % 2][:, 0:n], ACT.Exp, bias=nmax[:, k % 2:k % 2 + 1],
                                         accum_out=rsum[:, k % 8:k % 8 + 1]).then_inc(s_free, 1)
                    if k % 2 == 0:
                        pair_copy(pb, k // 2 - LP)
                    k += 1
            for p in range(LP):
                pair_copy(HP * NP, p - LP)

        @block.vector
        def _(dve):
            dve.sem_inc(s_max, OFF)
            dve.sem_inc(s_ev, OFF - LT)
            dve.sem_inc(s_norm, OFF - LV)
            dve.sem_inc(s_add, OFF - LP)
            dve.wait_ge(a_z, 6)

            def normalise(base, pbase, k):
                _, b, qt, h = items[k % NI]
                p = k // 2
                dve.wait_ge(s_PV, base + (OFF + k + 1))
                dve.wait_ge(s_ev, base + (OFF + k + 1))
                if h == 0:
                    dve.wait_ge(s_oT, pbase + (OFF + p - 1))
                nc.vector.tensor_scalar(O[:, p % 2, h * HS:(h + 1) * HS], pO[:, 0:HS], rinv[:, k % 8:k % 8 + 1], None, ALU.mult).then_inc(s_norm, 1)

            def evacuate(base, k):
                n = (items[k % NI][2] + 1) * P
                dve.wait_ge(s_T, base + (OFF + k + 1))
                dve.wait_ge(s_PV, base + (OFF + k - 3))
                nc.vector.reciprocal(rinv[:, k % 8:k % 8 + 1], rsum[:, k % 8:k % 8 + 1])
                nc.vector.tensor_copy(PT[:, k % 4, 0:n], pPT[:, 0:n]).then_inc(s_ev, 1)

            def add(pbase, p):
                _, b, qt, _ = items[(2 * p) % NI]
                dve.wait_ge(s_Wo, pbase + (OFF + p + 1))
                y = m.yatt[:, b * QT + qt, :]
                nc.vector.tensor_tensor(y, y, pW[:, 0:D], ALU.add).then_inc(s_add, 1)

            with dve.Fori(0, HP, 1) as hp:
                kb, eb, pb = hp * NI, hp * NE, hp * NP
                k = 0
                for i, e in enumerate(entries):
                    if e[0] == "p":
                        continue
                    n = (e[2] + 1) * P
                    dve.wait_ge(s_full, eb + (PRO + i + 1))
                    dve.wait_ge(s_free, eb + (OFF + PRO + entry(k - 2) + 1))
                    nc.vector.tensor_reduce(nmax[:, k % 2:k % 2 + 1], slot[(PRO + i) % 2][:, 0:n], AX.X, ALU.max, negate=True).then_inc(s_max, 1)
                    normalise(kb, pb, k - LV)
                    evacuate(kb, k - LT)
                    if k % 2:
                        add(pb, k // 2 - LP)
                    k += 1
            kb, pb = HP * NI, HP * NP
            for k in range(2 * LP):
                if k < LV:
                    normalise(kb, pb, k - LV)
                if k < LT:
                    evacuate(kb, k - LT)
                if k % 2:
                    add(pb, k // 2 - LP)


def ternary_and_last(nc, d, m, psum):
    with ExitStack() as ctx:
        sb = lambda n, s, t=FP32: ctx.enter_context(nc.sbuf_tensor(n, s, t))
        sem = lambda n: ctx.enter_context(nc.semaphore(n))
        w = [sb("t_wu", [P, FF]), sb("t_wd", [P, FF])]
        wt = [sb("t_tu", [P, FF]), sb("t_td", [P, FF])]
        asum = sb("t_as", [P, 2])
        thr = sb("t_thr", [P, 4])
        cst = sb("t_cst", [P, P])
        gb = sb("t_gb", [P, 2, D])
        hh = sb("t_h", [P, 3, FF])
        hT = sb("t_hT", [P, 2, KC, P])
        sq = sb("t_sq", [P, FF])
        sqx = sb("t_sqx", [P, NT, D])
        ssx = sb("t_ssx", [P, NT])
        ssh = sb("t_ssh", [P, NT])
        rx = sb("t_rx", [P, NT])
        rh = sb("t_rh", [P, NT])
        st6, mv, r1 = sb("l_st6", [P, NT, 6]), sb("l_mv", [P, NT, 2]), sb("l_r", [P, NT])
        dn = sb("t_dn", [P, NT, D])
        t_ld, t_v, t_as, t_sgn, t_thr, t_wq, t_x, t_xs, t_up, t_gelu, t_hT, t_hTs, t_dn, t_dns, t_sq, t_sqr, l_in, l_sqrt, t_out, t_f = [sem("t_" + n) for n in (
            "ld", "v", "as", "sgn", "thr", "wq", "x", "xs", "up", "gelu", "hT", "hTs", "dn", "dns", "sq", "sqr", "lin", "lsq", "out", "fin")]
        ps = [psum[:, i, :] for i in range(8)]
        block = ctx.enter_context(nc.Block())

        @block.sync
        def _(sp):
            sp.dma_start(w[0][:, :], d.t_upT).then_inc(t_ld, 16)
            sp.dma_start(w[1][:, :], d.t_dnT).then_inc(t_ld, 16)
            sp.dma_start(cst[:, :], d.half_mean).then_inc(t_ld, 16)
            sp.dma_start(gb[:, 0, :], d.gamma.to_broadcast([P, D])).then_inc(t_ld, 16)
            sp.dma_start(gb[:, 1, :], d.beta.to_broadcast([P, D])).then_inc(t_ld, 16)
            sp.wait_ge(t_f, 1)
            sp.dma_start(m.out, m.acc).then_inc(t_out, 16)
            sp.wait_ge(t_out, 16)

        @block.tensor
        def _(pe):
            pe.wait_ge(t_as, 1)
            nc.tensor.matmul(ps[7][:, 0:2], lhsT=cst[:, :], rhs=asum[:, :], start=True, stop=True).then_inc(t_thr, 1)
            pe.wait_ge(t_wq, 1)
            for t in range(NT + 2):
                if t < NT:
                    if t >= 2:
                        pe.wait_ge(t_gelu, t - 1)
                    nc.tensor.matmul(ps[t % 2], lhsT=m.xn2T[:, t * P:(t + 1) * P], rhs=w[0][:, :], start=True, stop=True).then_inc(t_up, 1)
                if 1 <= t <= NT:
                    j = t - 1
                    pe.wait_ge(t_gelu, j + 1)
                    if j >= 2:
                        pe.wait_ge(t_hTs, j - 1)
                    for k in range(KC):
                        ins = nc.tensor.transpose(ps[2 + j % 2][:, k * P:(k + 1) * P], hh[:, j % 3, k * P:(k + 1) * P], m.ident[:, :])
                    ins.then_inc(t_hT, 1)
                if t >= 2:
                    j = t - 2
                    pe.wait_ge(t_hTs, j + 1)
                    if j >= 2:
                        pe.wait_ge(t_dns, j - 1)
                    for k in range(KC):
                        ins = nc.tensor.matmul(ps[4 + j % 2][:, 0:D], lhsT=hT[:, j % 2, k, :], rhs=w[1][:, k * P:(k + 1) * P], start=(k == 0), stop=(k == KC - 1))
                    ins.then_inc(t_dn, 1)

        @block.scalar
        def _(act):
            act.wait_ge(t_x, 1)
            nc.scalar.activation(rx[:, :], ssx[:, :], ACT.Sqrt, scale=1.0 / D).then_inc(t_xs, 1)
            act.wait_ge(l_in, 1)
            nc.scalar.activation(r1[:, :], r1[:, :], ACT.Sqrt).then_inc(l_sqrt, 1)
            act.wait_ge(t_xs, 2)
            for t in range(NT):
                act.wait_ge(t_up, t + 1)
                if t >= 3:
                    act.wait_ge(t_hT, t - 2)
                    act.wait_ge(t_sq, t - 2)
                nc.scalar.activation(hh[:, t % 3, :], ps[t % 2], ACT.Gelu, scale=rx[:, t:t + 1]).then_inc(t_gelu, 1)
            act.wait_ge(t_sq, NT)
            nc.scalar.activation(rh[:, :], ssh[:, :], ACT.Sqrt, scale=1.0 / FF).then_inc(t_sqr, 1)

        @block.vector
        def _(dve):
            cnt = [0]

            def link(ins):
                cnt[0] += 1
                ins.then_inc(t_v, 1)
                dve.wait_ge(t_v, cnt[0])

            dve.wait_ge(t_ld, 80)
            nc.vector.tensor_reduce(asum[:, 0:1], w[0][:, :], AX.X, ALU.add, apply_absolute_value=True)
            nc.vector.tensor_reduce(asum[:, 1:2], w[1][:, :], AX.X, ALU.add, apply_absolute_value=True).then_inc(t_as, 1)
            for t in range(NT):
                ins = nc.vector.tensor_tensor_reduce(out=sqx[:, t, :], in0=m.xn2[:, t, :], in1=m.xn2[:, t, :], scale=1.0, scalar=0.0,
                                                     op0=ALU.mult, op1=ALU.add, accum_out=ssx[:, t:t + 1])
            ins.then_inc(t_x, 1)
            dve.wait_ge(t_thr, 1)
            nc.vector.tensor_scalar(thr[:, 0:2], ps[7][:, 0:2], 1.0, None, ALU.mult)
            link(nc.vector.tensor_scalar(thr[:, 2:4], ps[7][:, 0:2], -1.0, None, ALU.mult))
            for i in range(2):
                link(nc.vector.tensor_scalar(wt[i][:, :], w[i][:, :], thr[:, i:i + 1], None, ALU.is_gt))
                link(nc.vector.scalar_tensor_tensor(wt[i][:, :], w[i][:, :], thr[:, 2 + i:3 + i], wt[i][:, :], ALU.is_lt, ALU.subtract))
                link(nc.vector.tensor_tensor(wt[i][:, :], wt[i][:, :], w[i][:, :], ALU.add))
                ins = nc.vector.tensor_tensor(w[i][:, :], w[i][:, :], wt[i][:, :], ALU.subtract)
            ins.then_inc(t_wq, 1)
            for t in range(NT):
                ins = nc.vector.bn_stats(st6[:, t, :], m.yatt[:, t, :])
            link(ins)
            for t in range(NT):
                ins = nc.vector.bn_aggr(mv[:, t, :], st6[:, t, :])
            link(ins)
            nc.vector.tensor_scalar(r1[:, :], mv[:, :, 1], EPS_LN2, None, ALU.add).then_inc(l_in, 1)
            dve.wait_ge(t_xs, 1)
            link(nc.vector.tensor_scalar(rx[:, :], rx[:, :], EPS_T, None, ALU.add))
            nc.vector.reciprocal(rx[:, :], rx[:, :]).then_inc(t_xs, 1)
            dve.wait_ge(l_sqrt, 1)
            link(nc.vector.reciprocal(r1[:, :], r1[:, :]))
            for t in range(NT):
                ins = nc.vector.tensor_scalar(m.yatt[:, t, :], m.yatt[:, t, :], mv[:, t, 0:1], r1[:, t:t + 1], ALU.subtract, ALU.mult)
            link(ins)
            gam, bet = [gb[:, i, :].unsqueeze(1).to_broadcast([P, NT, D]) for i in range(2)]
            for t in range(NT + 1):
                if t == 1:
                    link(nc.vector.tensor_tensor(m.yatt[:, :, :], m.yatt[:, :, :], gam, ALU.mult))
                if t == 3:
                    link(nc.vector.tensor_tensor(m.yatt[:, :, :], m.yatt[:, :, :], bet, ALU.add))
                if t == 5:
                    link(nc.vector.tensor_tensor(m.acc, m.acc, m.yatt[:, :, :], ALU.add))
                if t < NT:
                    dve.wait_ge(t_gelu, t + 1)
                    if t:
                        dve.wait_ge(t_sq, t)
                    nc.vector.tensor_tensor_reduce(out=sq[:, :], in0=hh[:, t % 3, :], in1=hh[:, t % 3, :], scale=1.0, scalar=0.0,
                                                   op0=ALU.mult, op1=ALU.add, accum_out=ssh[:, t:t + 1]).then_inc(t_sq, 1)
                    dve.wait_ge(t_hT, t + 1)
                    if t >= 2:
                        dve.wait_ge(t_dn, t - 1)
                    nc.vector.tensor_copy(hT[:, t % 2, :, :].rearrange("p k n -> p (k n)"), ps[2 + t % 2]).then_inc(t_hTs, 1)
                if t:
                    dve.wait_ge(t_dn, t)
                    nc.vector.tensor_copy(dn[:, t - 1, :], ps[4 + (t - 1) % 2][:, 0:D]).then_inc(t_dns, 1)
            dve.wait_ge(t_dns, NT)
            dve.wait_ge(t_sqr, 1)
            link(nc.vector.tensor_scalar(rh[:, :], rh[:, :], EPS_T, None, ALU.add))
            link(nc.vector.reciprocal(rh[:, :], rh[:, :]))
            for t in range(NT):
                ins = nc.vector.scalar_tensor_tensor(m.acc[:, t, :], dn[:, t, :], rh[:, t:t + 1], m.acc[:, t, :], ALU.mult, ALU.add)
            ins.then_inc(t_f, 1)


def both_layers(nc, d, out, stage=3):
    with ExitStack() as ctx:
        sb = lambda n, s, t=FP32: ctx.enter_context(nc.sbuf_tensor(n, s, t))
        psum = ctx.enter_context(nc.psum_tensor("psum", [P, 8, BLK], FP32))
        ps = [psum[:, i, :] for i in range(8)]
        m = Memory()
        m.out = out
        m.ident = sb("ident", [P, P])
        m.accx = sb("accx", [P, NT + 1, D])
        m.acc = m.accx[:, 1:NT + 1, :]
        m.one = sb("one", [P, 1])
        m.iota8 = sb("iota8", [P, E])
        with ExitStack() as c1:
            sb = lambda n, s, t=FP32: c1.enter_context(nc.sbuf_tensor(n, s, t))
            dram = lambda n, s: nc.dram_tensor(n, s, FP32, kind="Internal").ap()
            m.Dp = sb("Dp", [P, DH])
            with ExitStack() as c2:
                sb = lambda n, s, t=FP32: c2.enter_context(nc.sbuf_tensor(n, s, t))
                m.A = sb("A", [P, DH, STATE])
                m.dt = sb("dt", [P, DH, T])
                m.u_mem = sb("u", [P, DH * B * (KW - 1 + S)])
                m.u = m.u_mem[:, 0:DH * T].rearrange("p (h t) -> p h t", h=DH)
                m.PT = sb("PT", [P, UNITS * B * 2 + 1, BLK], BF16)
                m.sel = sb("sel", [96, 2, UN, P], BF16)
                m.zeros = sb("zeros", [P, BLK], BF16)
                m.xnT = sb("xnT", [P, T])
                m.wT = [sb("w_gT", [P, E, FF]), sb("w_uT", [P, E, FF])]
                m.w_dnT = sb("w_dnT", [P, KC, E, D])
                m.w_rdT = sb("w_rdT", [P, KC, E])
                m.xc_dram, m.sz_dram = dram("xc_dram", (P, DH, T)), dram("sz_dram", (P, DH, T))
                m.y_dram = dram("y_dram", (T // BLK, P, 2 * BLK))
                m.comb_dram = dram("comb_dram", (NT + 1, 2 * E, P))
                prepare(nc, d, m, ps)
                scan_and_experts(nc, d, m, ps)
            gate_and_project(nc, d, m, ps)
        m.xn2 = ctx.enter_context(nc.sbuf_tensor("xn2", [P, NT, D], FP32))
        m.xn2T = ctx.enter_context(nc.sbuf_tensor("xn2T", [P, T], FP32))
        m.yatt = ctx.enter_context(nc.sbuf_tensor("yatt", [P, NT, D], FP32))
        second_norm(nc, d, m, ps)
        attention(nc, d, m, psum)
        ternary_and_last(nc, d, m, psum)


def layout(i):
    bf16 = mybir.dt.np(BF16)
    c = np.ascontiguousarray
    half = lambda w: w.reshape(DH, P, -1).transpose(1, 0, 2)
    o = {}
    o["x"] = c(i["L0_attn_x"].reshape(NT, P, D).transpose(1, 0, 2))
    o["vec"] = c(np.concatenate([i["L0_attn_norm_w"].reshape(P, 1), half(i["L0_attn_conv_b"].reshape(INNER, 1)).reshape(P, -1),
                                 half(i["L0_attn_dt_b"].reshape(INNER, 1)).reshape(P, -1), half(i["L0_attn_D_param"].reshape(INNER, 1)).reshape(P, -1),
                                 half(i["L0_attn_conv_w"].reshape(INNER, KW)).reshape(P, -1), half(i["L0_attn_A_log"]).reshape(P, -1)], axis=1))
    o["w_inT"] = c(i["L0_attn_in_proj_w"].T)
    o["w_bcT"] = c(half(np.concatenate([i["L0_attn_B_w"], i["L0_attn_C_w"]], axis=0).T))
    o["w_dtT"] = c(half(i["L0_attn_dt_w"].T))
    o["w_oT"] = c(half(i["L0_attn_out_proj_w"].T))
    o["w_rT"] = c(np.concatenate([i["L0_ffn_router_gate"], i["L0_ffn_router_up"]], axis=0).T)
    o["w_rdT"] = c(i["L0_ffn_router_down"].T.reshape(KC, P, E).transpose(1, 0, 2))
    o["w_gT"] = c(i["L0_ffn_w_gate"].transpose(2, 0, 1))
    o["w_uT"] = c(i["L0_ffn_w_up"].transpose(2, 0, 1))
    o["w_dnT"] = c(i["L0_ffn_w_down"].transpose(2, 0, 1).reshape(KC, P, E, D).transpose(1, 0, 2, 3))
    pairs = lambda w: w.reshape(HP, 2, D, HS).transpose(0, 2, 1, 3).reshape(HP, D, P)
    w = np.stack([pairs(i["L1_attn_" + n]) for n in ("Wq", "Wk", "Wv")], axis=2)
    o["wqkv"] = c(np.concatenate([w, np.zeros_like(w[:1])], axis=0))
    o["wo"] = c(i["L1_attn_Wo"].reshape(HP, P, D).transpose(1, 0, 2))
    o["gamma"], o["beta"] = i["L1_attn_gamma"].reshape(1, D), i["L1_attn_beta"].reshape(1, D)
    o["t_upT"] = c(i["L1_ffn_w_up"].T)
    o["t_dnT"] = c(i["L1_ffn_w_down"].T.reshape(KC, P, D).transpose(1, 0, 2).reshape(P, FF))
    o["half_mean"] = np.full((P, P), 0.5 / (FF * D), np.float32)
    o["identb"] = np.eye(P).astype(bf16)
    o["maskb"] = np.where(np.tril(np.ones((P, P))) > 0, 0.0, NEG).astype(bf16)
    o["ident"] = np.eye(P, dtype=np.float32)
    o["iota8"] = c(np.broadcast_to(np.arange(E, dtype=np.float32), (P, E)))
    sel = np.zeros((2, 3, UN, 2, UN, P), np.float32)
    for q in range(2):
        for s in range(UN):
            sel[q, :, s, q, s, :] = 1.0
    o["sel"] = sel.reshape(96, 2, UN, P).astype(bf16)
    return o


INPUTS = ["x", "vec", "w_inT", "w_bcT", "w_dtT", "w_oT", "w_rT", "w_rdT", "w_gT", "w_uT", "w_dnT", "wqkv", "wo", "gamma", "beta",
          "t_upT", "t_dnT", "half_mean", "identb", "maskb", "ident", "iota8", "sel"]


def kernel(**inputs):
    import concourse.bacc as bacc
    from concourse.bass_utils import run_bass_kernel_spmd

    arrays = layout({k: np.asarray(v) for k, v in inputs.items()})
    nc = bacc.Bacc("TRN2", target_bir_lowering=False, num_devices=1)
    d = namedtuple("Inputs", INPUTS)(*[nc.dram_tensor("in_" + n, arrays[n].shape, mybir.dt.from_np(arrays[n].dtype), kind="ExternalInput").ap()
                                       for n in INPUTS])
    out = nc.dram_tensor("out", (P, NT, D), FP32, kind="ExternalOutput").ap()
    both_layers(nc, d, out)
    r = run_bass_kernel_spmd(nc, [{"in_" + n: arrays[n] for n in INPUTS}], core_ids=[0])
    return r.results[0]["out"].transpose(1, 0, 2).reshape(B, S, D)
```

```python
import numpy as np
import concourse.bass as bass
from concourse import mybir
from collections import namedtuple
from contextlib import ExitStack

FP32 = mybir.dt.float32
BF16 = mybir.dt.bfloat16
FP32R = mybir.dt.float32r
U32 = mybir.dt.uint32
ALU = mybir.AluOpType
ACT = mybir.ActivationFunctionType
AX = mybir.AxisListType

P = 128
B, S, D = 2, 1024, 128
T = B * S
NT = T // P
BLK = 512
INNER, STATE, KW = 256, 64, 4
DH = INNER // P
E, FF = 8, 512
KC = FF // P
H, HS = 16, 64
HP = H // 2
QT = S // P
EPS_LN, EPS_RMS, EPS_LN2, EPS_T = 1e-5, 1e-6, 1e-3, 1e-8
UN = 16
UNITS = STATE // UN
PER = BLK // P
NB = T // BLK
NEG = -1.0e30
V_NORM, V_CB, V_DTB, V_D = 0, 1, 1 + DH, 1 + 2 * DH
V_CW = 1 + 3 * DH
V_A = V_CW + DH * KW
VECS = V_A + DH * STATE


class Memory:
    pass


def prepare(nc, d, m, ps):
    with ExitStack() as ctx:
        sb = lambda n, s, t=FP32: ctx.enter_context(nc.sbuf_tensor(n, s, t))
        sem = lambda n: ctx.enter_context(nc.semaphore(n))
        X = sb("X", [P, NT, D])
        XR = sb("XR", [P, NT, D])
        xrT = m.dt[:, 0, :]
        XP = m.u_mem[:, :].rearrange("p (a s) -> p a s", s=KW - 1 + S)
        bc_p = [XR[:, 8 * i:8 * i + 8, :].rearrange("p a h -> p (a h)").bitcast(BF16) for i in range(2)] + \
               [X[:, 0:8, :].rearrange("p a h -> p (a h)").bitcast(BF16)]
        xc = sb("xc", [P, DH, T])
        sz = sb("sz", [P, DH, T])
        mv = sb("mv", [P, NT, 2])
        st6 = sb("st6", [P, NT, 6])
        rr = sb("rr", [P, 2, NT])
        rstd, rms = rr[:, 0, :], rr[:, 1, :]
        w_inT = sb("w_inT", [P, 4 * P])
        w_bcT = sb("w_bcT", [P, DH, P])
        w_dtT = sb("w_dtT", [P, DH, INNER])
        w_rT = sb("w_rT", [P, 2 * E])
        vec = sb("vec", [P, VECS])
        norm_w, conv_b, dt_b = vec[:, V_NORM:V_NORM + 1], vec[:, V_CB:V_CB + DH], vec[:, V_DTB:V_DTB + DH]
        conv_w = vec[:, V_CW:V_CW + DH * KW].rearrange("p (c k) -> p c k", c=DH)
        xn = sb("xn", [P, NT, D])
        rl_mem = m.dA[:, 0:2, :, :].rearrange("p a h t -> p (a h t)").rearrange("p (c s) -> p c s", c=DH)
        rl = [xn[:, :, :].rearrange("p a h -> p (a h)").rearrange("p (c s) -> p c s", c=DH), rl_mem]
        cv = [rl[0][:, 0, :], rl[0][:, 1, :], rl[0][:, 0, :], rl_mem[:, 0, :]]
        res = X[:, 8:16, :].rearrange("p a h -> p (a h)").rearrange("p (r t) -> p r t", r=2)
        idx = sb("idx", [P, NT * 2, E], U32)
        idf = sb("idf", [P, NT * 2, 2])
        dif = sb("dif", [P, NT * 2])
        pr = sb("pr", [P, NT * 2, 2])
        spare = m.dA[:, 2:4, :, :].rearrange("p a h t -> p (a h t)")
        oh = spare[:, 0:4 * NT * E].rearrange("p (j r e) -> p j r e", j=2, e=E)
        L, top = [spare[:, 4 * P * i:4 * P * i + 2 * NT * E].rearrange("p (r e) -> p r e", e=E) for i in (2, 3)]
        cT = spare[:, BLK:BLK + 2 * P].rearrange("p (g n) -> p g n", g=2)

        ld_x, ld_w, ld_e, ld_s, ld_c = sem("ld_x"), sem("ld_w"), sem("ld_e"), sem("ld_s"), sem("ld_c")
        consts = sem("p_consts")
        rr_in, rr_sqrt, rr_done, xr_done, xr_out = sem("rr_in"), sem("rr_sqrt"), sem("rr_done"), sem("xr_done"), sem("xr_out")
        v = sem("p_dve")
        a = sem("p_act")
        ln_done, xn_T, tok_T = sem("ln_done"), sem("xn_T"), sem("tok_T")
        zx_mm, zx_out, xc_done = sem("zx_mm"), sem("zx_out"), sem("xc_done")
        cv_ready, mm_dt, mm_bc, sp_abs, sp_exp, sp_relu, sp_ln, dt_done = [sem(n) for n in (
            "cv_ready", "mm_dt", "mm_bc", "sp_abs", "sp_exp", "sp_relu", "sp_ln", "dt_done")]
        bc_hi, bc_done, rt_mm, rt_dif, rt_exp, cb_done, cb_T, cb_cp, cb_out, pt_out, lg = [sem(n) for n in (
            "bc_hi", "bc_done", "rt_mm", "rt_dif", "rt_exp", "cb_done", "cb_T", "cb_cp", "cb_out", "pt_out", "lg")]

        chunks = [(blk, c) for blk in range(4) for c in range(2)] + [(blk, 2 + c) for blk in range(4) for c in range(2)]
        dt_bank = [4, 5, 6, 7, 2, 0, 1, 3]
        tile_of = lambda x, i: x[:, i % 2, (i // 2) * BLK:(i // 2 + 1) * BLK]
        batch_of = lambda x, b: x[:, :, b * S:(b + 1) * S]

        block = ctx.enter_context(nc.Block())

        @block.sync
        def _(sp):
            for h in range(4):
                sp.dma_start(X[:, 4 * h:4 * h + 4, :], d.x[:, 4 * h:4 * h + 4, :]).then_inc(ld_x, 16)
            sp.dma_start(m.ident[:, :], d.ident).then_inc(ld_c, 16)
            sp.dma_start(vec[:, :], d.vec).then_inc(ld_s, 16)
            sp.dma_start(w_inT[:, :], d.w_inT).then_inc(ld_w, 16)
            sp.dma_start(w_rT[:, :], d.w_rT).then_inc(ld_w, 16)
            sp.dma_start(w_bcT[:, :, :], d.w_bcT).then_inc(ld_w, 16)
            sp.dma_start(w_dtT[:, :, :], d.w_dtT).then_inc(ld_w, 16)
            sp.dma_start(m.iota8[:, :], d.iota8).then_inc(ld_w, 16)
            sp.dma_start(m.w_rdT[:, :, :], d.w_rdT).then_inc(ld_e, 16)
            sp.dma_start(m.w_oT[:, :, :], d.w_oT).then_inc(ld_e, 16)
            sp.dma_start(m.sel[:, :, :, :], d.sel).then_inc(ld_e, 16)
            for g in range(2):
                sp.dma_start(m.wT[g][:, :, :], (d.w_gT, d.w_uT)[g]).then_inc(ld_e, 16)
            sp.dma_start(m.w_dnT[:, :, :, :], d.w_dnT).then_inc(ld_e, 16)
            sp.wait_ge(xc_done, 4)
            sp.dma_start(m.xc_dram, xc[:, :, :]).then_inc(cb_out, 16)
            sp.wait_ge(zx_out, 16)
            sp.dma_start(m.sz_dram, sz[:, :, :]).then_inc(cb_out, 16)
            for b in range(B):
                sp.wait_ge(bc_done, 2 * b + 2)
                for q in range(2):
                    for part in range(3):
                        for ic in range(UNITS):
                            r0 = q * STATE + ic * UN
                            o0 = q * 48 + part * UN
                            k0 = 2 * UNITS * b + ic
                            sp.dma_start(m.PT[o0:o0 + UN, k0:k0 + UNITS + 1:UNITS, :],
                                         bc_p[part][r0:r0 + UN, b * S:(b + 1) * S].rearrange("p (k t) -> p k t", t=BLK)).then_inc(pt_out, 16)
            sp.wait_ge(pt_out, 16 * 6 * UNITS * B)
            sp.wait_ge(cb_out, 64)
            sp.wait_ge(ld_e, 96)

        @block.gpsimd
        def _(pool):
            nc.gpsimd.memset(XP[:, :, 0:KW - 1], 0.0).then_inc(consts, 1)
            nc.gpsimd.memset(m.zeros[:, :], 0.0)
            nc.gpsimd.memset(m.PT[:, UNITS * B * 2, :], 0.0)
            pool.wait_ge(ln_done, NT)
            nc.gpsimd.tensor_tensor(m.acc[:, :, :], X[:, :, :], xn[:, :, :], ALU.add).then_inc(lg, 1)
            pool.wait_ge(xc_done, 4)
            pool.wait_ge(dt_done, 1)
            nc.gpsimd.tensor_tensor(m.u[:, 1, 0:S], m.dt[:, 1, 0:S], xc[:, 1, 0:S], ALU.mult)
            pool.wait_ge(dt_done, 2)
            nc.gpsimd.tensor_tensor(m.u[:, 1, S:T], m.dt[:, 1, S:T], xc[:, 1, S:T], ALU.mult)

        @block.scalar
        def _(act):
            act.wait_ge(ld_s, 16)
            A_log = vec[:, V_A:V_A + DH * STATE].rearrange("p (c n) -> p c n", c=DH)
            nc.scalar.activation(m.A[:, :, :], A_log, ACT.Exp).then_inc(a, 1)
            act.wait_ge(a, 1)
            nc.scalar.mul(m.A[:, :, :], m.A[:, :, :], -1.0).then_inc(a, 1)
            act.wait_ge(rr_in, 1)
            nc.scalar.activation(rr[:, :, :], rr[:, :, :], ACT.Sqrt).then_inc(rr_sqrt, 1)
            act.wait_ge(rr_done, 1)
            for t in range(NT):
                act.wait_ge(ln_done, t + 1)
                nc.scalar.mul(XR[:, t, :], xn[:, t, :], rms[:, t:t + 1]).then_inc(xr_done, 1)
            for q in range(4):
                act.wait_ge(xn_T, 2 * q + 1)
                nc.scalar.copy(m.xnT[:, q * BLK:(q + 1) * BLK], ps[4 + 2 * (q % 2)][:, :]).then_inc(tok_T, 1)
            for n, (blk, c) in enumerate(chunks):
                act.wait_ge(zx_mm, n + 1)
                if c < 2:
                    b, t0 = blk // 2, (blk % 2) * BLK
                    nc.scalar.copy(XP[:, c * B + b, KW - 1 + t0:KW - 1 + t0 + BLK], ps[4 + n % 4][:, :]).then_inc(zx_out, 1)
                else:
                    nc.scalar.activation(sz[:, c - 2, blk * BLK:(blk + 1) * BLK], ps[4 + n % 4][:, :], ACT.Silu).then_inc(zx_out, 1)

            def silu_xc(b):
                for c in range(DH):
                    i = b * DH + c
                    act.wait_ge(cv_ready, i + 1)
                    nc.scalar.activation(xc[:, c, b * S:(b + 1) * S], cv[i], ACT.Silu).then_inc(xc_done, 1)

            def high_parts(b):
                for blk in (2 * b, 2 * b + 1):
                    act.wait_ge(mm_bc, blk + 1)
                    nc.scalar.copy(bc_p[0][:, blk * BLK:(blk + 1) * BLK], ps[blk % 2][:, :]).then_inc(bc_hi, 1)

            def absolutes(b):
                for i in range(4 * b, 4 * b + 4):
                    act.wait_ge(mm_dt, i + 1)
                    nc.scalar.activation(tile_of(m.dt, i), ps[dt_bank[i]][:, :], ACT.Abs, bias=dt_b[:, i % 2:i % 2 + 1]).then_inc(sp_abs, 1)

            silu_xc(0)
            high_parts(0)
            silu_xc(1)
            absolutes(0)
            act.wait_ge(rt_dif, 1)
            nc.scalar.activation(dif[:, :], dif[:, :], ACT.Exp).then_inc(rt_exp, 1)
            for b in range(B):
                if b:
                    high_parts(b)
                    absolutes(b)
                act.wait_ge(sp_abs, 4 * b + 4)
                nc.scalar.activation(batch_of(m.dt, b), batch_of(m.dt, b), ACT.Exp, scale=-1.0).then_inc(sp_exp, 1)
            act.wait_ge(cb_cp, 1)
            act.dma_start(m.comb_dram[0:NT].rearrange("(g t) e n -> (t e) g n", g=2), cT[:, :, :]).then_inc(cb_out, 16)
            act.dma_start(m.comb_dram[NT], cT[0:2 * E, 0, :]).then_inc(cb_out, 16)
            for b in range(B):
                act.wait_ge(sp_exp, b + 1)
                nc.scalar.activation(batch_of(m.dt, b), batch_of(m.dt, b), ACT.Ln, bias=m.one[:, 0:1]).then_inc(sp_ln, 1)

        @block.vector
        def _(dve):
            cnt = [0]

            def link(ins):
                cnt[0] += 1
                ins.then_inc(v, 1)
                dve.wait_ge(v, cnt[0])

            link(nc.vector.memset(m.one[:, :], 1.0))
            for t in range(NT):
                if t % 4 == 0:
                    dve.wait_ge(ld_x, 16 * 4)
                ins = nc.vector.bn_stats(st6[:, t, :], X[:, t, :])
            link(ins)
            for t in range(NT):
                ins = nc.vector.bn_aggr(mv[:, t, :], st6[:, t, :])
            link(ins)
            link(nc.vector.tensor_scalar(rr[:, 0, :], mv[:, :, 1], EPS_LN, None, ALU.add))
            link(nc.vector.reciprocal(rr[:, 1, :], rr[:, 0, :]))
            link(nc.vector.tensor_tensor(rr[:, 1, :], rr[:, 1, :], mv[:, :, 1], ALU.mult))
            nc.vector.tensor_scalar(rr[:, 1, :], rr[:, 1, :], EPS_RMS, None, ALU.add).then_inc(rr_in, 1)
            dve.wait_ge(rr_sqrt, 1)
            link(nc.vector.reciprocal(rr[:, :, :], rr[:, :, :]))
            dve.sem_inc(rr_done, 1)
            for t in range(NT):
                nc.vector.tensor_scalar(xn[:, t, :], X[:, t, :], mv[:, t, 0:1], rstd[:, t:t + 1], ALU.subtract, ALU.mult).then_inc(ln_done, 1)
            dve.wait_ge(ld_s, 16)
            nc.vector.tensor_copy(m.Dp[:, :], vec[:, V_D:V_D + DH])
            for q in range(4):
                dve.wait_ge(xn_T, 2 * q + 2)
                nc.vector.tensor_scalar(xrT[:, q * BLK:(q + 1) * BLK], ps[5 + 2 * (q % 2)][:, :], norm_w[:, 0:1], None, ALU.mult).then_inc(xr_out, 1)
            dve.wait_ge(ld_w, 80)
            dve.wait_ge(consts, 1)
            dve.wait_ge(lg, 1)
            dve.wait_ge(xr_done, NT)
            for i in range(B * DH):
                b, c = i // DH, i % DH
                row = c * B + b
                dve.wait_ge(zx_out, 4 * b + 4)
                if i == 2:
                    dve.wait_ge(xc_done, 1)
                link(nc.vector.tensor_scalar(cv[i], XP[:, row, 0:S], conv_w[:, c, 0:1], conv_b[:, c:c + 1], ALU.mult, ALU.add))
                for k in range(1, KW):
                    ins = nc.vector.scalar_tensor_tensor(cv[i], XP[:, row, k:k + S], conv_w[:, c, k:k + 1], cv[i], ALU.mult, ALU.add)
                    if k < KW - 1:
                        link(ins)
                ins.then_inc(cv_ready, 1)

            def split(blk):
                c0 = slice(blk * BLK, (blk + 1) * BLK)
                dve.wait_ge(bc_hi, blk + 1)
                link(nc.vector.tensor_tensor(res[:, blk % 2, :], ps[blk % 2][:, :], bc_p[0][:, c0], ALU.subtract))
                link(nc.vector.tensor_copy(bc_p[1][:, c0], res[:, blk % 2, :]))
                nc.vector.tensor_tensor(bc_p[2][:, c0], res[:, blk % 2, :], bc_p[1][:, c0], ALU.subtract).then_inc(bc_done, 1)

            def relu(i):
                b = i // 4
                dve.wait_ge(sp_abs, i + 1)
                if i % 4 == 0:
                    dve.wait_ge(xc_done, 3 + b)
                nc.vector.tensor_scalar(rl[b][:, i % 2, (i // 2 % 2) * BLK:(i // 2 % 2 + 1) * BLK], ps[dt_bank[i]][:, :],
                                        dt_b[:, i % 2:i % 2 + 1], 0.0, ALU.add, ALU.max).then_inc(sp_relu, 1)

            dve.wait_ge(rt_mm, 1)
            link(nc.vector.tensor_copy(L[:, :, :].rearrange("p a e -> p (a e)"), ps[3][:, 0:NT * 2 * E]))
            for r in range(NT * 2):
                ins = nc.vector.max(top[:, r, :], L[:, r, :])
            link(ins)
            nc.vector.tensor_tensor(dif[:, :], top[:, :, 1], top[:, :, 0], ALU.subtract).then_inc(rt_dif, 1)
            split(0)
            split(1)
            for r in range(NT * 2):
                ins = nc.vector.max_index(idx[:, r, :], top[:, r, :], L[:, r, :])
            link(ins)
            link(nc.vector.tensor_copy(idf[:, :, :], idx[:, :, 0:2]))
            split(2)
            split(3)
            for j in range(2):
                ins = nc.vector.tensor_tensor(oh[:, j, :, :], m.iota8[:, :].unsqueeze(1).to_broadcast([P, NT * 2, E]),
                                              idf[:, :, j:j + 1].to_broadcast([P, NT * 2, E]), ALU.is_equal)
            link(ins)
            dve.wait_ge(rt_exp, 1)
            link(nc.vector.tensor_scalar(pr[:, :, 0], dif[:, :], 1.0, None, ALU.add))
            link(nc.vector.reciprocal(pr[:, :, 0], pr[:, :, 0]))
            link(nc.vector.tensor_tensor(pr[:, :, 1], pr[:, :, 0], dif[:, :], ALU.mult))
            for j in range(2):
                link(nc.vector.tensor_tensor(oh[:, j, :, :], oh[:, j, :, :], pr[:, :, j:j + 1].to_broadcast([P, NT * 2, E]), ALU.mult))
            nc.vector.tensor_tensor(oh[:, 0, :, :], oh[:, 0, :, :], oh[:, 1, :, :], ALU.add).then_inc(cb_done, 1)
            for i in range(8):
                if i == 1:
                    dve.wait_ge(cb_T, 1)
                    nc.vector.tensor_copy(cT[:, :, :].rearrange("p a n -> p (a n)"), ps[3][:, 0:2 * P]).then_inc(cb_cp, 1)
                relu(i)
            for b in range(B):
                dve.wait_ge(sp_relu, 4 * b + 4)
                dve.wait_ge(sp_ln, b + 1)
                nc.vector.scalar_tensor_tensor(batch_of(m.dt, b), batch_of(m.dt, b), 1e-4, rl[b][:, :, :], ALU.add, ALU.add).then_inc(dt_done, 1)
            dve.wait_ge(dt_done, 2)
            dve.wait_ge(xc_done, 4)
            nc.vector.tensor_tensor(m.u[:, 0, :], m.dt[:, 0, :], xc[:, 0, :], ALU.mult)

        @block.tensor
        def _(pe):
            pe.wait_ge(ld_c, 16)
            for q in range(4):
                for k, src in enumerate((xn, XR)):
                    pe.wait_ge((ln_done, xr_done)[k], 4 * q + 4)
                    if q >= 2:
                        pe.wait_ge((tok_T, xr_out)[k], q - 1)
                    for j in range(4):
                        ins = nc.tensor.transpose(ps[4 + 2 * (q % 2) + k][:, j * P:(j + 1) * P], src[:, 4 * q + j, :], m.ident[:, :])
                    ins.then_inc(xn_T, 1)
            pe.wait_ge(ld_w, 80)
            pe.wait_ge(xr_out, 4)
            pe.wait_ge(tok_T, 4)
            for n, (blk, c) in enumerate(chunks):
                if n >= 4:
                    pe.wait_ge(zx_out, n - 3)
                nc.tensor.matmul(ps[4 + n % 4][:, :], lhsT=w_inT[:, c * P:(c + 1) * P], rhs=xrT[:, blk * BLK:(blk + 1) * BLK],
                                 start=True, stop=True).then_inc(zx_mm, 1)
            for t in range(NT):
                ins = nc.tensor.matmul(ps[3][:, t * 2 * E:(t + 1) * 2 * E], lhsT=m.xnT[:, t * P:(t + 1) * P], rhs=w_rT[:, :],
                                       start=True, stop=True)
            ins.then_inc(rt_mm, 1)

            def product(bank, w, blk):
                for k in range(DH):
                    ins = nc.tensor.matmul(ps[bank][:, :], lhsT=w(k), rhs=xc[:, k, blk * BLK:(blk + 1) * BLK], start=(k == 0), stop=(k == DH - 1))
                return ins

            for b in range(B):
                pe.wait_ge(xc_done, DH * (b + 1))
                for blk in (2 * b, 2 * b + 1):
                    if b:
                        pe.wait_ge(bc_done, blk - 1)
                    product(blk % 2, lambda k: w_bcT[:, k, :], blk).then_inc(mm_bc, 1)
                pe.wait_ge(zx_out, 16)
                for i in range(4 * b, 4 * b + 4):
                    if i in (5, 6):
                        pe.wait_ge(bc_done, i - 2)
                    if i == 7:
                        pe.wait_ge(cb_done, 1)
                        for g in range(2):
                            ins = nc.tensor.transpose(ps[3][:, g * P:(g + 1) * P],
                                                      oh[:, 0, :, :].rearrange("p a e -> p (a e)")[:, g * P:(g + 1) * P], m.ident[:, :])
                        ins.then_inc(cb_T, 1)
                        pe.wait_ge(cb_cp, 1)
                    product(dt_bank[i], lambda k: w_dtT[:, k, (i % 2) * P:(i % 2 + 1) * P], i // 2).then_inc(mm_dt, 1)


class GateProjectNorm:

    def __init__(self, nc, m, ps, ctx, yg):
        sb = lambda n, s, t=FP32: ctx.enter_context(nc.sbuf_tensor(n, s, t))
        sem = lambda n: ctx.enter_context(nc.semaphore(n))
        self.nc, self.m, self.ps, self.yg = nc, m, ps, yg
        self.st6, self.mv, self.r1 = sb("n_st6", [P, NT, 6]), sb("n_mv", [P, NT, 2]), sb("n_r", [P, NT])
        self.y_T, self.y_dx, self.y_gated, self.y_mm, self.y_acc = [sem(n) for n in ("y_T", "y_dx", "y_gated", "y_mm", "y_acc")]
        self.n_st, self.n_in, self.n_sqrt, self.n_rec, self.n_done, self.n_mm, self.n_cp = [sem(n) for n in (
            "n_stats", "n_in", "n_sqrt", "n_rec", "n_done", "n_mm", "n_cp")]

    def tiles(self, x, k):
        return x[:, PER * k:PER * (k + 1), :].rearrange("p t h -> p (t h)")


    def y_transposes(self, pe, i):
        nc, m, ps = self.nc, self.m, self.ps
        for h in range(DH):
            if i >= 2:
                pe.wait_ge(self.y_dx, 2 * (i - 2) + h + 1)
            for t in range(PER):
                j, c = divmod(t * DH + h, 4)
                ins = nc.tensor.transpose(ps[2 * (i % 2) + h][:, t * P:(t + 1) * P], m.u[:, j, i * BLK + c * P:i * BLK + (c + 1) * P], m.ident[:, :])
            ins.then_inc(self.y_T, 1)

    def project(self, pe, k):
        nc, m, ps, yg = self.nc, self.m, self.ps, self.yg
        pe.wait_ge(self.y_gated, 2 * k + 2)
        if k >= 2:
            pe.wait_ge(self.y_acc, k - 1)
        for t in range(PER):
            for h in range(DH):
                ins = nc.tensor.matmul(ps[4 + k % 2][:, t * P:(t + 1) * P], lhsT=yg[:, k % 2, h, t * P:(t + 1) * P], rhs=m.w_oT[:, h, :],
                                       start=(h == 0), stop=(h == DH - 1))
        ins.then_inc(self.y_mm, 1)

    def norm_transposes(self, pe, k):
        nc, m, ps = self.nc, self.m, self.ps
        pe.wait_ge(self.n_done, k + 1)
        if k >= 2:
            pe.wait_ge(self.n_cp, k - 1)
        for j in range(PER):
            ins = nc.tensor.transpose(ps[6 + k % 2][:, j * P:(j + 1) * P], m.xn2[:, PER * k + j, :], m.ident[:, :])
        ins.then_inc(self.n_mm, 1)


    def gate(self, pool, k):
        for h in range(DH):
            pool.wait_ge(self.y_dx, 2 * k + h + 1)
            y = self.yg[:, k % 2, h, :]
            self.nc.gpsimd.tensor_tensor(y, y, self.m.sz_back[:, h, k * BLK:(k + 1) * BLK], ALU.mult).then_inc(self.y_gated, 1)


    def norm_copies(self, act, k):
        nc, m, ps, r1 = self.nc, self.m, self.ps, self.r1
        c = slice(PER * k, PER * (k + 1))
        act.wait_ge(self.n_in, k + 1)
        nc.scalar.activation(r1[:, c], r1[:, c], ACT.Sqrt).then_inc(self.n_sqrt, 1)
        act.wait_ge(self.n_done, k + 1)
        nc.scalar.copy(self.tiles(m.yatt, k), self.tiles(m.xn2, k))
        act.wait_ge(self.n_mm, k + 1)
        nc.scalar.copy(m.xn2T[:, k * BLK:(k + 1) * BLK], ps[6 + k % 2][:, :]).then_inc(self.n_cp, 1)


    def add_D(self, dve, i):
        nc, m, ps = self.nc, self.m, self.ps
        for h in range(DH):
            dve.wait_ge(self.y_T, 2 * i + h + 1)
            if i >= 2:
                dve.wait_ge(self.y_mm, i - 1)
            nc.vector.scalar_tensor_tensor(self.yg[:, i % 2, h, :], m.xc_back[:, h, i * BLK:(i + 1) * BLK], m.Dp[:, h:h + 1],
                                           ps[2 * (i % 2) + h][:, :], ALU.mult, ALU.add).then_inc(self.y_dx, 1)

    def norm(self, dve, k):
        nc, m, ps, st6, mv, r1 = self.nc, self.m, self.ps, self.st6, self.mv, self.r1
        c = slice(PER * k, PER * (k + 1))
        dve.wait_ge(self.y_mm, k + 1)
        nc.vector.tensor_tensor(self.tiles(m.acc, k), ps[4 + k % 2][:, :], self.tiles(m.acc, k), ALU.add).then_inc(self.y_acc, 1)
        dve.wait_ge(self.y_acc, k + 1)
        for t in range(PER * k, PER * (k + 1)):
            ins = nc.vector.bn_stats(st6[:, t, :], m.acc[:, t, :])
        ins.then_inc(self.n_st, 1)
        dve.wait_ge(self.n_st, 2 * k + 1)
        for t in range(PER * k, PER * (k + 1)):
            ins = nc.vector.bn_aggr(mv[:, t, :], st6[:, t, :])
        ins.then_inc(self.n_st, 1)
        dve.wait_ge(self.n_st, 2 * k + 2)
        nc.vector.tensor_scalar(r1[:, c], mv[:, c, 1], EPS_LN, None, ALU.add).then_inc(self.n_in, 1)
        dve.wait_ge(self.n_sqrt, k + 1)
        nc.vector.reciprocal(r1[:, c], r1[:, c]).then_inc(self.n_rec, 1)
        dve.wait_ge(self.n_rec, k + 1)
        for t in range(PER * k, PER * (k + 1)):
            ins = nc.vector.tensor_scalar(m.xn2[:, t, :], m.acc[:, t, :], mv[:, t, 0:1], r1[:, t:t + 1], ALU.subtract, ALU.mult)
        ins.then_inc(self.n_done, 1)


def scan_and_experts(nc, d, m, ps):
    with ExitStack() as ctx:
        sb = lambda n, s, t=FP32: ctx.enter_context(nc.sbuf_tensor(n, s, t))
        sem = lambda n: ctx.enter_context(nc.semaphore(n))
        RA, RD, RH, RB = 4, 4, 2, 4
        AHEAD = 4
        Bs = sb("Bs", [P, RB, BLK])
        dA = m.dA
        dBx = sb("dBx", [P, RD, DH, BLK])
        hh = dBx
        hC = sb("hC", [P, RH, DH, BLK])
        carry = sb("carry", [P, STATE, DH])
        cbb = sb("cbb", [P, 2 * E, P])
        xs = sb("xs", [P, 2 * E, P])
        act_mem = sb("gate_act", [P, 2, FF])
        sg, gg = act_mem[:, 0, :], act_mem[:, 1, :]
        eo = act_mem[:, :, :].rearrange("p a n -> p (a n)")
        inter = sb("inter", [P, FF])
        interT = sb("interT", [P, KC, P])
        Ld = sb("Ld", [P, E])
        top = sb("topd", [P, E])
        idx = sb("idxd", [P, E], U32)
        idf = sb("idfd", [P, 2])
        dif = sb("difd", [P, 1])
        edif = sb("edif", [P, 1])
        pr = sb("prd", [P, 2])
        cd = sb("cd", [P, 2, E])

        psB, psC, psY, G, U = ps[0:2], ps[2:4], ps[4:6], ps[6], ps[7]
        s_psB, s_Bs, s_dA, s_dBx, s_psC, s_scan, s_hC, s_y, s_carry = [sem(n) for n in (
            "psB_full", "Bs_full", "dA_full", "dBx_full", "psC_full", "scanned", "hC_full", "y_added", "carried")]
        s_cbb, s_xs, s_gate, s_up, s_tanh, s_gg, s_int, s_intT, s_intE, s_lg, s_lgc, s_dif, s_exp, s_dn0, s_dn1, s_cd, s_cmb, s_sum, s_out, s_q = [
            sem(n) for n in ("cbb_full", "xs_full", "gate_done", "up_done", "tanh_done", "gg_done",
                             "inter_done", "interT_mm", "interT_done", "logits_mm", "logits_out", "dif_done", "exp_done", "down0", "down1",
                             "weights_done", "weighted", "summed", "tile_out", "dve_own")]
        s_zero, s_at, s_yout, s_init = sem("carry_zero"), sem("reached"), sem("y_out"), sem("first_set")
        s_back = [sem("loaded_back0"), sem("loaded_back1")]
        OFF = 4
        ALL = B * 2 * STATE
        behind = GateProjectNorm(nc, m, ps, ctx, hC)

        block = ctx.enter_context(nc.Block())

        def loops(eng, body, start_block, end_block):
            with eng.Fori(0, B, 1) as b:
                cb = b * (2 * STATE)
                with eng.Fori(0, 2, 1) as tc:
                    ct = tc * STATE
                    start_block(cb, ct)
                    with eng.Fori(0, UNITS, 1) as ic:
                        body(cb, ct, ic * UN)
                    end_block(cb, ct)

        nothing = lambda cb, ct: None

        @block.sync
        def _(sp):
            rows = m.comb_dram.rearrange("t e n -> t (e n)")
            sp.dma_start(cbb[:, :, :].rearrange("p e n -> p (e n)"), rows[0:1, :].to_broadcast([P, 2 * E * P])).then_inc(s_cbb, 16)

            def body(cb, ct, n0):
                q = (cb + ct + n0) // UN
                sp.wait_ge(s_xs, 2 * q + 2)
                sp.dma_start(cbb[:, :, :].rearrange("p e n -> p (e n)"),
                             rows[bass.ds(q + 1, 1), :].to_broadcast([P, 2 * E * P])).then_inc(s_cbb, 16)

            loops(sp, body, nothing, nothing)
            sp.wait_ge(s_cbb, 16 * (NT + 1))
            sp.dma_start(m.wqkv[:, :, :], d.wqkv[0]).then_inc(s_cbb, 16)
            sp.wait_ge(s_cbb, 16 * (NT + 2))

        @block.scalar
        def _(act):
            act.sem_inc(s_Bs, OFF)
            act.sem_inc(s_dA, OFF)

            def copy_B(N, s):
                act.wait_ge(s_psB, N + (s + 1))
                act.wait_ge(s_dBx, N + (OFF + s - RB + 1))
                nc.scalar.copy(Bs[:, s % RB, :], psB[s % 2][:, :]).then_inc(s_Bs, 1)

            def turned(q):
                act.wait_ge(s_intT, q + 1)
                nc.scalar.copy(interT[:, :, :].rearrange("p k n -> p (k n)"), G[:, :]).then_inc(s_intE, 1)

            def exp_dif(q):
                act.wait_ge(s_dif, q + 1)
                nc.scalar.activation(edif[:, :], dif[:, :], ACT.Exp).then_inc(s_exp, 1)

            def weigh(q, half):
                if half:
                    act.wait_ge(s_cd, q + 1)
                act.wait_ge((s_dn0, s_dn1)[half], q + 1)
                for j in range(4):
                    e = 4 * half + j
                    ins = nc.scalar.mul(eo[:, e * P:(e + 1) * P], (U, G)[half][:, j * P:(j + 1) * P], cd[:, 0, e:e + 1])
                ins.then_inc(s_cmb, 1)

            def body(cb, ct, n0):
                N = cb + ct + n0
                t0 = (cb + ct) * 8
                q = N // UN
                for s in range(UN):
                    copy_B(N, s)
                    act.wait_ge(s_scan, N + (OFF + s - RA + 1))
                    nc.scalar.activation(dA[:, s % RA, 0, :], m.dt[:, 0, bass.ds(t0, BLK)], ACT.Exp, scale=m.A[:, 0, bass.ds(n0 + s, 1)])
                    nc.scalar.activation(dA[:, s % RA, 1, :], m.dt[:, 1, bass.ds(t0, BLK)], ACT.Exp, scale=m.A[:, 1, bass.ds(n0 + s, 1)]).then_inc(s_dA, 1)
                    if s == 3:
                        turned(q)
                    if s == 5:
                        exp_dif(q)
                    if s == 7:
                        weigh(q, 1)
                    if s == 8:
                        weigh(q, 0)
                    if s == 13:
                        act.wait_ge(s_gate, q + 2)
                        act.wait_ge(s_out, q + 1)
                        nc.scalar.activation(sg, G[:, :], ACT.Tanh, scale=0.5).then_inc(s_tanh, 1)

            loops(act, body, nothing, nothing)
            act.wait_ge(s_gate, NT + 1)
            act.wait_ge(s_up, NT + 1)
            for b in range(B):
                act.dma_start(m.xc_back[:, :, b * S:(b + 1) * S], m.xc_dram[:, :, b * S:(b + 1) * S]).then_inc(s_back[b], 16)
                act.dma_start(m.sz_back[:, :, b * S:(b + 1) * S], m.sz_dram[:, :, b * S:(b + 1) * S]).then_inc(s_back[b], 16)
            for s in range(AHEAD - 2):
                copy_B(B * 2 * STATE, s)
            turned(NT)
            exp_dif(NT)
            weigh(NT, 1)
            weigh(NT, 0)
            for k in range(NB):
                behind.norm_copies(act, k)

        @block.gpsimd
        def _(pool):
            nc.gpsimd.memset(inter[:, :], 0.0).then_inc(s_int, 1)
            nc.gpsimd.memset(m.accx[:, 0, :], 0.0).then_inc(s_init, 1)
            pool.wait_ge(s_init, 1)
            pool.sem_inc(s_dBx, OFF)

            def add_up(q, sq):
                pool.wait_ge(s_cmb, 2 * q + 2)
                n = E * P
                for step in range(3):
                    n //= 2
                    if step:
                        pool.wait_ge(s_sum, sq + step)
                    nc.gpsimd.tensor_tensor(eo[:, 0:n], eo[:, 0:n], eo[:, n:2 * n], ALU.add).then_inc(s_sum, 1)
                pool.wait_ge(s_sum, sq + 3)
                pool.sem_inc(s_at, 1)
                a = m.accx[:, bass.ds(q, 1), :].rearrange("p a h -> p (a h)") if not isinstance(q, int) else m.accx[:, q, :]
                nc.gpsimd.tensor_tensor(a, a, eo[:, 0:P], ALU.add).then_inc(s_out, 1)

            def body(cb, ct, n0):
                N = cb + ct + n0
                t0 = (cb + ct) * 8
                q = N // UN
                for s in range(UN):
                    pool.wait_ge(s_Bs, N + (OFF + s + 1))
                    pool.wait_ge(s_hC, N + (OFF + s - RD + 1))
                    pool.sem_inc(s_at, 1)
                    nc.gpsimd.tensor_tensor(dBx[:, s % RD, :, :], m.u[:, :, bass.ds(t0, BLK)],
                                            Bs[:, s % RB, :].unsqueeze(1).to_broadcast([P, DH, BLK]), ALU.mult).then_inc(s_dBx, 1)
                    if s in (2, 7):
                        gu = s // 7
                        pool.wait_ge(s_cbb, q * 16 + 16)
                        pool.wait_ge((s_gate, s_up)[gu], q + 1)
                        pool.sem_inc(s_at, 1)
                        nc.gpsimd.tensor_tensor(xs[:, gu * E:(gu + 1) * E, :], cbb[:, gu * E:(gu + 1) * E, :],
                                                m.xnT[:, bass.ds(N * 8, P)].unsqueeze(1).to_broadcast([P, E, P]), ALU.mult).then_inc(s_xs, 1)
                    if s == 12:
                        add_up(q, 3 * q)

            loops(pool, body, nothing, nothing)
            pool.wait_ge(s_back[0], 32)
            behind.gate(pool, 0)
            behind.gate(pool, 1)
            add_up(NT, 3 * NT)
            pool.wait_ge(s_back[1], 32)
            behind.gate(pool, 2)
            behind.gate(pool, 3)

        @block.vector
        def _(dve):
            dve.sem_inc(s_scan, OFF)
            dve.sem_inc(s_hC, OFF)

            OWN = 7

            def link(ins):
                ins.then_inc(s_q, 1)

            def router(q, step):
                own = q * OWN
                if step == 0:
                    dve.wait_ge(s_lg, q + 1)
                    nc.vector.tensor_copy(Ld[:, :], G[:, 0:E]).then_inc(s_lgc, 1)
                if step == 1:
                    dve.wait_ge(s_init, 1)
                    dve.wait_ge(s_lgc, q + 1)
                    link(nc.vector.max(top[:, :], Ld[:, :]))
                if step == 2:
                    dve.wait_ge(s_q, own + 1)
                    nc.vector.tensor_tensor(dif[:, :], top[:, 1:2], top[:, 0:1], ALU.subtract).then_inc(s_dif, 1)
                    link(nc.vector.max_index(idx[:, :], top[:, :], Ld[:, :]))
                if step == 3:
                    dve.wait_ge(s_q, own + 2)
                    link(nc.vector.tensor_copy(idf[:, :], idx[:, 0:2]))
                if step == 4:
                    dve.wait_ge(s_exp, q + 1)
                    link(nc.vector.tensor_scalar(pr[:, 0:1], edif[:, :], 1.0, None, ALU.add))
                if step == 5:
                    dve.wait_ge(s_q, own + 4)
                    link(nc.vector.reciprocal(pr[:, 0:1], pr[:, 0:1]))
                    dve.wait_ge(s_q, own + 5)
                    link(nc.vector.tensor_tensor(pr[:, 1:2], pr[:, 0:1], edif[:, :], ALU.mult))
                if step == 6:
                    nc.vector.tensor_scalar(cd[:, 0, :], m.iota8[:, :], idf[:, 0:1], pr[:, 0:1], ALU.is_equal, ALU.mult)
                    dve.wait_ge(s_q, own + 6)
                    link(nc.vector.tensor_scalar(cd[:, 1, :], m.iota8[:, :], idf[:, 1:2], pr[:, 1:2], ALU.is_equal, ALU.mult))
                if step == 7:
                    dve.wait_ge(s_q, own + 7)
                    nc.vector.tensor_tensor(cd[:, 0, :], cd[:, 0, :], cd[:, 1, :], ALU.add).then_inc(s_cd, 1)

            def times_C(N, s):
                dve.wait_ge(s_psC, N + (s + 1))
                dve.wait_ge(s_y, N + (OFF + s - RH + 1))
                nc.vector.tensor_tensor(hC[:, s % RH, :, :], hh[:, s % RD, :, :],
                                        psC[s % 2][:, :].unsqueeze(1).to_broadcast([P, DH, BLK]), ALU.mult).then_inc(s_hC, 1)

            def body(cb, ct, n0):
                N = cb + ct + n0
                q = N // UN
                for s in range(UN):
                    dve.wait_ge(s_dA, N + (OFF + s + 1))
                    dve.wait_ge(s_dBx, N + (OFF + s + 1))
                    for h in range(DH):
                        ins = nc.vector.tensor_tensor_scan(hh[:, s % RD, h, :], dA[:, s % RA, h, :], dBx[:, s % RD, h, :],
                                                           carry[:, bass.ds(n0 + s, 1), h], ALU.mult, ALU.add)
                    ins.then_inc(s_scan, 1)
                    if 2 <= s < 6:
                        router(q, 2 * s - 4)
                    if s:
                        times_C(N, s - 1)
                    if 2 <= s < 6:
                        router(q, 2 * s - 3)
                    if s == 12:
                        dve.wait_ge(s_tanh, q + 1)
                        nc.vector.scalar_tensor_tensor(gg, sg, 1.0, G[:, :], ALU.add, ALU.mult).then_inc(s_gg, 1)
                    if s == 15:
                        dve.wait_ge(s_gg, q + 1)
                        dve.wait_ge(s_up, q + 2)
                        nc.vector.scalar_tensor_tensor(inter[:, :], gg, 0.5, U[:, :], ALU.mult, ALU.mult).then_inc(s_int, 1)
                    dve.wait_ge(s_scan, N + (OFF + s + 1))
                    nc.vector.tensor_scalar(carry[:, bass.ds(n0 + s, 1), :].rearrange("p n h -> p (n h)"), hh[:, s % RD, :, BLK - 1],
                                            1.0, None, ALU.mult).then_inc(s_carry, 1)
                times_C(N, UN - 1)

            with dve.Fori(0, B, 1) as b:
                cb = b * (2 * STATE)
                nc.vector.memset(carry[:, :, :], 0.0).then_inc(s_zero, 1)
                with dve.Fori(0, 2, 1) as tc:
                    ct = tc * STATE
                    dve.wait_ge(s_zero, b + 1)
                    dve.wait_ge(s_carry, cb + ct)
                    dve.sem_inc(s_at, 1)
                    with dve.Fori(0, UNITS, 1) as ic:
                        body(cb, ct, ic * UN)
                    dve.wait_ge(s_y, cb + ct + (OFF + STATE))
                    for j in range(2):
                        ins = nc.vector.tensor_scalar(m.u[:, j, bass.ds((cb + ct) * 8, BLK)], psY[j][:, :], 1.0, None, ALU.mult)
                    ins.then_inc(s_yout, 1)
            dve.wait_ge(s_back[0], 32)
            behind.add_D(dve, 0)
            for step in range(8):
                router(NT, step)
            for i in range(1, NB + 1):
                if i == NB // B:
                    dve.wait_ge(s_back[1], 32)
                if i < NB:
                    behind.add_D(dve, i)
                if i == NB:
                    dve.wait_ge(s_out, NT + 1)
                behind.norm(dve, i - 1)

        @block.tensor
        def _(pe):
            pe.sem_inc(s_y, OFF)
            pe.sem_inc(s_gate, 1)
            pe.sem_inc(s_up, 1)
            gate = [(0, e) for e in range(E)]
            up = [(1, e) for e in range(E)]
            plan = {6: gate[0:2], 7: gate[2:4], 8: gate[4:6], 9: gate[6:8],
                    10: up[0:2], 11: up[2:4], 12: up[4:5], 13: up[5:7], 14: up[7:8]}
            down = {1: [(0, 0), (0, 1)], 2: [(0, 2), (0, 3)], 3: [(1, 0), (1, 1)], 4: [(1, 2), (1, 3)]}

            def units(q, s):
                return m.PT[0:96, bass.ds(q + s // UN, 1), :].rearrange("p a t -> p (a t)")

            def bcast_B(N, q, s):
                if s >= 2 or not isinstance(N, int):
                    pe.wait_ge(s_Bs, N + (OFF + s - 2 + 1))
                nc.tensor.matmul(psB[s % 2][:, :], lhsT=m.sel[:, 0, s % UN, :], rhs=units(q, s), start=True, stop=True).then_inc(s_psB, 1)

            def bcast_C(N, q, s):
                pe.wait_ge(s_hC, N + (OFF + s - 2 + 1))
                nc.tensor.matmul(psC[s % 2][:, :], lhsT=m.sel[:, 1, s % UN, :], rhs=units(q, s), start=True, stop=True).then_inc(s_psC, 1)

            def add_y(N, s):
                pe.wait_ge(s_hC, N + (OFF + s + 1))
                for t in range(4):
                    for h in range(DH):
                        j = t * DH + h
                        ins = nc.tensor.matmul(psY[j // 4][:, (j % 4) * P:(j % 4 + 1) * P], lhsT=hC[:, s % RH, h, t * P:(t + 1) * P],
                                               rhs=m.ident[:, :], is_transpose=True, start=False, stop=False, skip_group_check=True)
                ins.then_inc(s_y, 1)

            def inter_T(q):
                pe.wait_ge(s_int, q + 1)
                for k in range(KC):
                    ins = nc.tensor.transpose(G[:, k * P:(k + 1) * P], inter[:, k * P:(k + 1) * P], m.ident[:, :])
                ins.then_inc(s_intT, 1)

            def down_products(q, s):
                if s == 1:
                    pe.wait_ge(s_intE, q + 1)
                    for k in range(KC):
                        ins = nc.tensor.matmul(G[:, 0:E], lhsT=interT[:, k, :], rhs=m.w_rdT[:, k, :], start=(k == 0), stop=(k == KC - 1))
                    ins.then_inc(s_lg, 1)
                for half, k in down.get(s, []):
                    if half and k == 0:
                        pe.wait_ge(s_lgc, q + 1)
                    ins = nc.tensor.matmul((U, G)[half][:, :], lhsT=interT[:, k, :],
                                           rhs=m.w_dnT[:, k, 4 * half:4 * half + 4, :].rearrange("p e h -> p (e h)"),
                                           start=(k == 0), stop=(k == KC - 1))
                    if k == KC - 1:
                        ins.then_inc((s_dn0, s_dn1)[half], 1)

            def body(cb, ct, n0):
                N = cb + ct + n0
                q = N // UN
                for s in range(UN):
                    if s == 0:
                        inter_T(q)
                    down_products(q, s)
                    for gu, e in plan.get(s, []):
                        if e == 0:
                            pe.wait_ge(s_xs, 2 * q + (1 + gu))
                            pe.wait_ge(s_cmb, 2 * q + (1 + gu))
                        ins = nc.tensor.matmul((G, U)[gu][:, :], lhsT=xs[:, gu * E + e, :], rhs=m.wT[gu][:, e, :], start=(e == 0), stop=(e == E - 1))
                        if e == E - 1:
                            ins.then_inc((s_gate, s_up)[gu], 1)
                    bcast_C(N, q, s + 1)
                    if s:
                        add_y(N, s - 1)
                    bcast_B(N, q, s + AHEAD)
                add_y(N, UN - 1)

            def start_block(cb, ct):
                for j in range(2):
                    nc.tensor.matmul(psY[j][:, :], lhsT=m.zeros[:, 0:P], rhs=m.zeros[:, :], start=True, stop=False, skip_group_check=True)

            def end_block(cb, ct):
                pe.wait_ge(s_yout, (cb + ct) // STATE + 1)

            for s in range(AHEAD):
                bcast_B(0, 0, s)
            bcast_C(0, 0, 0)
            loops(pe, body, start_block, end_block)
            inter_T(NT)
            pe.wait_ge(s_Bs, ALL + OFF + AHEAD - 2)
            behind.y_transposes(pe, 0)
            down_products(NT, 1)
            down_products(NT, 2)
            behind.y_transposes(pe, 1)
            down_products(NT, 3)
            down_products(NT, 4)
            behind.project(pe, 0)
            for i in range(2, NB + 2):
                if i < NB:
                    behind.y_transposes(pe, i)
                if i <= NB:
                    behind.project(pe, i - 1)
                if i == 2:
                    pe.wait_ge(s_cmb, 2 * NT + 2)
                behind.norm_transposes(pe, i - 2)


def attention(nc, d, m, psum):
    ORDER = [7, 0, 6, 1, 5, 2, 4, 3]
    items = []
    entries = []
    for b in range(B):
        mine = [("s", b, qt, h) for qt in ORDER for h in range(2)]
        for at, w in ((3, 0), (7, 1), (11, 2)):
            mine.insert(at + w, ("p", 1 - b, w, 0))
        entries += mine
    items = [e for e in entries if e[0] == "s"]
    NE, NI, NP = len(entries), len(items), len(items) // 2
    entry_of = [i for i, e in enumerate(entries) if e[0] == "s"]
    last_w = max(i for i, e in enumerate(entries) if e[0] == "p" and e[1] == 1)
    PRO = 3
    LT, LV, LP = 2, 4, 3
    entry = lambda k: entry_of[k % NI] + (k // NI) * NE

    with ExitStack() as ctx:
        sb = lambda n, s, t=FP32: ctx.enter_context(nc.sbuf_tensor(n, s, t))
        sem = lambda n: ctx.enter_context(nc.semaphore(n))
        wqkv = m.wqkv
        wo = sb("wo", [P, HP + 1, D])
        maskb = sb("maskb", [P, P], BF16)
        qs = [[sb(f"q{b}{h}", [P, S], FP32R) for h in range(2)] for b in range(B)]
        k_hi = [[sb(f"k_hi{b}{h}", [P, S], FP32R) for h in range(2)] for b in range(B)]
        k_lo = [[sb(f"k_lo{b}{h}", [P, S], FP32R) for h in range(2)] for b in range(B)]
        x_qk = sb("x_qk", [P, 2, S])
        q_lo = sb("q_lo", [P, S], FP32R)
        own = [slice(0, HS), slice(HS, P)]
        V = sb("V", [P, B, QT, P])
        Pr = sb("Pr", [P, 4, S])
        PT = sb("PTs", [P, 4, S])
        nmax = sb("nmax", [P, 2])
        rsum = sb("rsum", [P, 8])
        rinv = sb("rinv", [P, 8])
        cst = sb("t_cst", [P, P])
        asum = sb("t_as", [P, 2])
        thrs = sb("t_thr", [P, 4])
        wts = [sb("t_tu", [P, FF]), sb("t_td", [P, FF])]
        low = sb("t_low", [P, FF])
        sqx = sb("t_sqx", [P, NT, D])
        t_ld, t_as, t_thr, t_p = sem("t_ld"), sem("t_as"), sem("t_thr"), sem("t_pool")
        GHOST = BLK + P
        O = sb("O", [P, 2, P])
        OT = sb("OT", [P, 2, P])

        slot = [psum[:, 0:2, :].rearrange("p a t -> p (a t)"), psum[:, 2:4, :].rearrange("p a t -> p (a t)")]
        pPT = psum[:, 4:6, :].rearrange("p a t -> p (a t)")
        pO, pW = psum[:, 6, :], psum[:, 7, :]

        a_ld, a_w, a_z = sem("a_ld"), sem("a_w"), sem("a_zero")
        s_hi, s_lo, s_stk, s_mask = sem("a_high"), sem("a_low"), sem("a_stacked"), sem("a_masked")
        STK = 6 * 16
        s_full, s_free, s_max, s_T, s_ev, s_PV, s_norm, s_oT, s_oTs, s_Wo, s_add = [sem("a_" + n) for n in (
            "slot_full", "slot_free", "max", "PT_mm", "PT_out", "O_mm", "O_out", "OT_mm", "OT_out", "Wo_mm", "added")]
        OFF = 8
        block = ctx.enter_context(nc.Block())

        @block.sync
        def _(sp):
            sp.dma_start(wo[:, 1:HP + 1, :], d.wo).then_inc(a_ld, 16)
            sp.dma_start(maskb[:, :], d.maskb).then_inc(a_ld, 16)
            sp.dma_start(m.tw[0][:, :], d.t_upT).then_inc(t_ld, 16)
            sp.dma_start(m.tw[1][:, :], d.t_dnT).then_inc(t_ld, 16)
            sp.dma_start(cst[:, :], d.half_mean).then_inc(t_ld, 16)
            sp.dma_start(m.gb[:, 0, :], d.gamma.to_broadcast([P, D])).then_inc(t_ld, 16)
            sp.dma_start(m.gb[:, 1, :], d.beta.to_broadcast([P, D])).then_inc(t_ld, 16)

            def stack(g, b):
                def copy(to, src, h):
                    sp.dma_start(to[own[1 - h], :].bitcast(FP32), src[own[h], :].bitcast(FP32)).then_inc(s_stk, 16)

                sp.wait_ge(s_lo, 4 * g + 2)
                for h in range(2):
                    copy(qs[b][h], q_lo, h)
                sp.wait_ge(s_hi, 2 * g + 2)
                for h in range(2):
                    copy(k_hi[b][h], k_hi[b][h], h)
                sp.wait_ge(s_lo, 4 * g + 4)
                for h in range(2):
                    copy(k_lo[b][h], k_lo[b][h], h)

            stack(0, 0)
            with sp.Fori(0, HP, 1) as hp:
                stack(2 * hp + 1, 1)
                sp.wait_ge(s_full, hp * NE + (PRO + last_w + 1))
                sp.dma_start(wqkv[:, :, :].rearrange("p a e -> p (a e)"),
                             d.wqkv.rearrange("n p a e -> n p (a e)")[bass.ds(hp + 1, 1)].rearrange("n p e -> (n p) e")).then_inc(a_w, 16)
                stack(2 * hp + 2, 0)
            sp.wait_ge(s_stk, STK * (2 * HP + 1))

        @block.gpsimd
        def _(pool):
            nc.gpsimd.memset(V[:, 1, :, :], 0.0).then_inc(a_z, 1)
            nc.gpsimd.memset(Pr[:, 4 - LT:4, 0:GHOST], 0.0).then_inc(a_z, 1)
            nc.gpsimd.memset(wo[:, 0, :], 0.0).then_inc(a_z, 1)
            nc.gpsimd.memset(rsum[:, :], 1.0).then_inc(a_z, 1)

            def low_parts(g, b):
                for n in range(4):
                    w, h = n // 2, n % 2
                    pool.wait_ge(s_lo, 4 * g + n)
                    if h == 0:
                        pool.wait_ge(s_hi, 2 * g + 1 + w)
                    if n == 0:
                        pool.wait_ge(s_stk, g * STK)
                    low, high = (q_lo, k_lo[b][h])[w], (qs, k_hi)[w][b][h]
                    nc.gpsimd.tensor_tensor(low[own[h], :], x_qk[own[h], w, :], high[own[h], :].bitcast(FP32), ALU.subtract).then_inc(s_lo, 1)

            pool.wait_ge(a_z, 7)
            nc.gpsimd.tensor_tensor(sqx[:, :, :], m.xn2, m.xn2, ALU.mult).then_inc(t_p, 1)
            pool.wait_ge(t_p, 1)
            n = D
            while n > 1:
                n //= 2
                nc.gpsimd.tensor_tensor(sqx[:, :, 0:n] if n > 1 else m.ssx[:, :].unsqueeze(2), sqx[:, :, 0:n], sqx[:, :, n:2 * n], ALU.add).then_inc(t_p, 1)
                pool.wait_ge(t_p, D.bit_length() - n.bit_length() + 1)
            pool.wait_ge(t_thr, 2)
            done = D.bit_length()
            for i in range(2):
                wi, wt, thr = m.tw[i], wts[i], thrs
                nc.gpsimd.tensor_scalar(wt[:, :], wi[:, :], thr[:, i:i + 1], None, ALU.is_gt).then_inc(t_p, 1)
                pool.wait_ge(t_p, done + 1)
                nc.gpsimd.tensor_scalar(low[:, :], wi[:, :], thr[:, 2 + i:3 + i], None, ALU.is_lt).then_inc(t_p, 1)
                pool.wait_ge(t_p, done + 2)
                nc.gpsimd.tensor_tensor(wt[:, :], low[:, :], wt[:, :], ALU.subtract).then_inc(t_p, 1)
                pool.wait_ge(t_p, done + 3)
                nc.gpsimd.tensor_tensor(wt[:, :], wt[:, :], wi[:, :], ALU.add).then_inc(t_p, 1)
                pool.wait_ge(t_p, done + 4)
                nc.gpsimd.tensor_tensor(wi[:, :], wi[:, :], wt[:, :], ALU.subtract).then_inc(t_p, 1)
                done += 5
            pool.wait_ge(t_p, done)
            with pool.Fori(0, HP, 1) as hp:
                low_parts(2 * hp + 1, 1)
                low_parts(2 * hp + 2, 0)

        @block.tensor
        def _(pe):
            pe.sem_inc(s_T, OFF - LT)
            pe.sem_inc(s_PV, OFF - LV)
            pe.sem_inc(s_oT, OFF - LP)
            pe.sem_inc(s_Wo, OFF - LP)

            def project(base, i, e, wbase):
                _, b, w, _ = e
                pe.wait_ge(s_free, base + (OFF + i - 1))
                if wbase is not None:
                    pe.wait_ge(a_w, wbase)
                if w < 2:
                    for c in range(2):
                        ins = nc.tensor.matmul(slot[i % 2][:, c * BLK:(c + 1) * BLK], lhsT=wqkv[:, w, :],
                                               rhs=m.xn2T[:, b * S + c * BLK:b * S + (c + 1) * BLK], start=True, stop=True)
                else:
                    for t in range(QT):
                        ins = nc.tensor.matmul(slot[i % 2][:, t * P:(t + 1) * P], lhsT=m.xn2T[:, b * S + t * P:b * S + (t + 1) * P],
                                               rhs=wqkv[:, 2, :], start=True, stop=True)
                ins.then_inc(s_full, 1)

            def scores(base, i, e):
                _, b, qt, h = e
                n = (qt + 1) * P
                pe.wait_ge(s_free, base + (OFF + i - 1))
                for c in range(0, n, BLK):
                    w = min(BLK, n - c)
                    for part in range(2):
                        ins = nc.tensor.matmul(slot[i % 2][:, c:c + w], lhsT=qs[b][h][:, qt * P:(qt + 1) * P], rhs=(k_hi, k_lo)[part][b][h][:, c:c + w],
                                               start=(part == 0), stop=(part == 1))
                ins.then_inc(s_full, 1)

            def values(base, k):
                _, b, qt, h = items[k % NI]
                pe.wait_ge(s_ev, base + (OFF + k + 1))
                pe.wait_ge(s_norm, base + (OFF + k))
                for t in range(qt + 1):
                    ins = nc.tensor.matmul(pO[:, 0:HS], lhsT=PT[:, k % 4, t * P:(t + 1) * P], rhs=V[:, b, t, h * HS:(h + 1) * HS],
                                           start=(t == 0), stop=(t == qt))
                ins.then_inc(s_PV, 1)

            def turn(base, ebase, k):
                _, b, qt, h = items[k % NI]
                pe.wait_ge(s_free, ebase + (OFF + PRO + entry(k) + 1))
                pe.wait_ge(s_ev, base + (OFF + k))
                for t in range(qt + 1):
                    ins = nc.tensor.transpose(pPT[:, t * P:(t + 1) * P], Pr[:, k % 4, t * P:(t + 1) * P], m.ident[:, :])
                ins.then_inc(s_T, 1)

            def pair_turn(pbase, kbase, p):
                pe.wait_ge(s_norm, kbase + (OFF + 2 * p + 2))
                pe.wait_ge(s_add, pbase + (OFF + p))
                nc.tensor.transpose(pW[:, 0:P], O[:, p % 2, :], m.ident[:, :]).then_inc(s_oT, 1)

            def pair_out(pbase, p, w):
                pe.wait_ge(s_oTs, pbase + (OFF + p + 1))
                nc.tensor.matmul(pW[:, 0:D], lhsT=OT[:, p % 2, :], rhs=w, start=True, stop=True).then_inc(s_Wo, 1)

            for w in range(3):
                project(0, w, ("p", 0, w, 0), None)
            pe.wait_ge(t_as, 1)
            nc.tensor.matmul(pW[:, 0:2], lhsT=cst[:, :], rhs=asum[:, :], start=True, stop=True).then_inc(t_thr, 1)
            pe.wait_ge(a_ld, 32)
            pe.wait_ge(a_z, 7)
            pe.wait_ge(t_thr, 2)
            with pe.Fori(0, HP, 1) as hp:
                kb, eb, pb = hp * NI, hp * NE, hp * NP
                wo_of = lambda p: wo[:, bass.ds(hp + (0 if p < 0 else 1), 1), :].rearrange("p a e -> p (a e)")
                k = 0
                for i, e in enumerate(entries):
                    if e[0] == "p":
                        project(eb, PRO + i, e, None if e[1] == 1 else hp * 16 + 16)
                        continue
                    if k % (NI // B) == 0:
                        pe.wait_ge(s_stk, hp * (STK * B) + STK * (e[1] + 1))
                    scores(eb, PRO + i, e)
                    values(kb, k - LV)
                    turn(kb, eb, k - LT)
                    if k % 2 == 0:
                        pair_turn(pb, kb, k // 2 - LP)
                    else:
                        pair_out(pb, k // 2 - LP, wo_of(k // 2 - LP))
                    k += 1
            kb, pb = HP * NI, HP * NP
            for k in range(2 * LP):
                if k < LV:
                    values(kb, k - LV)
                if k < LT:
                    turn(kb, HP * NE, k - LT)
                if k % 2 == 0:
                    pair_turn(pb, kb, k // 2 - LP)
                else:
                    pair_out(pb, k // 2 - LP, wo[:, HP, :])

        @block.scalar
        def _(act):
            act.sem_inc(s_free, OFF)
            act.sem_inc(s_oTs, OFF - LP)

            def projected(base, kbase, i, e, k, g):
                _, b, w, _ = e
                act.wait_ge(s_full, base + (i + 1))
                if w < 2:
                    if not isinstance(g, int):
                        act.wait_ge(s_lo, 4 * g)
                    scale = (HS ** -0.5, 1.0)[w]
                    nc.scalar.mul(x_qk[:, w, :], slot[i % 2], scale).then_inc(s_free, 1)
                else:
                    if k is not None:
                        act.wait_ge(s_PV, kbase + (OFF + k))
                    nc.scalar.copy(V[:, b, :, :].rearrange("p t e -> p (t e)"), slot[i % 2]).then_inc(s_free, 1)

            def high_parts(base, i, e):
                _, b, w, _ = e
                act.wait_ge(s_free, base + (OFF + i + 1))
                for h in range(2):
                    ins = nc.scalar.copy((qs, k_hi)[w][b][h][own[h], :], x_qk[own[h], w, :])
                ins.then_inc(s_hi, 1)

            def pair_copy(pbase, p):
                act.wait_ge(s_oT, pbase + (OFF + p + 1))
                act.wait_ge(s_Wo, pbase + (OFF + p - 1))
                nc.scalar.copy(OT[:, p % 2, :], pW[:, 0:P]).then_inc(s_oTs, 1)

            for w in range(3):
                projected(0, 0, w, ("p", 0, w, 0), None, 0)
                if w < 2:
                    high_parts(0, w, ("p", 0, w, 0))
            act.wait_ge(a_z, 7)
            with act.Fori(0, HP, 1) as hp:
                kb, eb, pb = hp * NI, hp * NE, hp * NP
                k = 0
                for i, e in enumerate(entries):
                    if e[0] == "p":
                        projected(eb, kb, PRO + i, e, 0 if e[1] == 1 else NI // 2, 2 * hp + (1 if e[1] == 1 else 2))
                        continue
                    n = (e[2] + 1) * P
                    act.wait_ge(s_max, kb + (OFF + k + 1))
                    act.wait_ge(s_T, kb + (OFF + k - 3))
                    nc.scalar.activation(Pr[:, k % 4, 0:n], slot[(PRO + i) % 2][:, 0:n], ACT.Exp, bias=nmax[:, k % 2:k % 2 + 1],
                                         accum_out=rsum[:, k % 8:k % 8 + 1]).then_inc(s_free, 1)
                    before = entries[i - 1]
                    if i and before[0] == "p" and before[2] < 2:
                        high_parts(eb, PRO + i - 1, before)
                    if k % 2 == 0:
                        pair_copy(pb, k // 2 - LP)
                    k += 1
            for p in range(LP):
                pair_copy(HP * NP, p - LP)

        @block.vector
        def _(dve):
            dve.sem_inc(s_max, OFF)
            dve.sem_inc(s_ev, OFF - LT)
            dve.sem_inc(s_norm, OFF - LV)
            dve.sem_inc(s_add, OFF - LP)
            nc.vector.memset(PT[:, :, 0:GHOST], 0.0).then_inc(a_z, 1)
            nc.vector.memset(rinv[:, :], 1.0).then_inc(a_z, 1)
            nc.vector.memset(O[:, :, :], 0.0).then_inc(a_z, 1)
            for n in range(4):
                w, h = n // 2, n % 2
                low, high = (q_lo, k_lo[0][h])[w], (qs, k_hi)[w][0][h]
                dve.wait_ge(s_hi, 1 + w)
                nc.vector.tensor_tensor(low[own[h], :], x_qk[own[h], w, :], high[own[h], :].bitcast(FP32), ALU.subtract).then_inc(s_lo, 1)
            dve.wait_ge(t_ld, 80)
            nc.vector.tensor_reduce(asum[:, 0:1], m.tw[0][:, :], AX.X, ALU.add, apply_absolute_value=True)
            nc.vector.tensor_reduce(asum[:, 1:2], m.tw[1][:, :], AX.X, ALU.add, apply_absolute_value=True).then_inc(t_as, 1)
            dve.wait_ge(t_thr, 1)
            nc.vector.tensor_scalar(thrs[:, 0:2], pW[:, 0:2], 1.0, None, ALU.mult)
            nc.vector.tensor_scalar(thrs[:, 2:4], pW[:, 0:2], -1.0, None, ALU.mult).then_inc(t_thr, 1)
            dve.wait_ge(a_z, 7)
            dve.wait_ge(a_ld, 32)

            def normalise(base, pbase, k):
                _, b, qt, h = items[k % NI]
                p = k // 2
                dve.wait_ge(s_PV, base + (OFF + k + 1))
                dve.wait_ge(s_ev, base + (OFF + k + 1))
                if h == 0:
                    dve.wait_ge(s_oT, pbase + (OFF + p - 1))
                nc.vector.tensor_scalar(O[:, p % 2, h * HS:(h + 1) * HS], pO[:, 0:HS], rinv[:, k % 8:k % 8 + 1], None, ALU.mult).then_inc(s_norm, 1)

            def evacuate(base, k):
                n = (items[k % NI][2] + 1) * P
                dve.wait_ge(s_T, base + (OFF + k + 1))
                dve.wait_ge(s_PV, base + (OFF + k - 3))
                nc.vector.reciprocal(rinv[:, k % 8:k % 8 + 1], rsum[:, k % 8:k % 8 + 1])
                nc.vector.tensor_copy(PT[:, k % 4, 0:n], pPT[:, 0:n]).then_inc(s_ev, 1)

            def add(pbase, p):
                _, b, qt, _ = items[(2 * p) % NI]
                dve.wait_ge(s_Wo, pbase + (OFF + p + 1))
                y = m.yatt[:, b * QT + qt, :]
                nc.vector.tensor_tensor(y, y, pW[:, 0:D], ALU.add).then_inc(s_add, 1)

            with dve.Fori(0, HP, 1) as hp:
                kb, eb, pb = hp * NI, hp * NE, hp * NP
                k = 0
                for i, e in enumerate(entries):
                    if e[0] == "p":
                        continue
                    n = (e[2] + 1) * P
                    dve.wait_ge(s_full, eb + (PRO + i + 1))
                    dve.wait_ge(s_free, eb + (OFF + PRO + entry(k - 2) + 1))
                    diagonal = slot[(PRO + i) % 2][:, n - P:n]
                    nc.vector.tensor_tensor(diagonal, diagonal, maskb[:, :], ALU.add).then_inc(s_mask, 1)
                    dve.wait_ge(s_mask, kb + (k + 1))
                    nc.vector.tensor_reduce(nmax[:, k % 2:k % 2 + 1], slot[(PRO + i) % 2][:, 0:n], AX.X, ALU.max, negate=True).then_inc(s_max, 1)
                    normalise(kb, pb, k - LV)
                    evacuate(kb, k - LT)
                    if k % 2:
                        add(pb, k // 2 - LP)
                    k += 1
            kb, pb = HP * NI, HP * NP
            for k in range(2 * LP):
                if k < LV:
                    normalise(kb, pb, k - LV)
                if k < LT:
                    evacuate(kb, k - LT)
                if k % 2:
                    add(pb, k // 2 - LP)


def ternary_and_last(nc, d, m, psum):
    with ExitStack() as ctx:
        sb = lambda n, s, t=FP32: ctx.enter_context(nc.sbuf_tensor(n, s, t))
        sem = lambda n: ctx.enter_context(nc.semaphore(n))
        w = m.tw
        hh = sb("t_h", [P, 4, FF])
        hT = sb("t_hT", [P, 2, KC, P])
        sq = sb("t_sq", [P, FF])
        ssh = sb("t_ssh", [P, NT])
        rx = sb("t_rx", [P, NT])
        rh = sb("t_rh", [P, NT])
        st6, mv, r1 = sb("l_st6", [P, NT, 6]), sb("l_mv", [P, NT, 2]), sb("l_r", [P, NT])
        dn = sb("t_dn", [P, NT, D])
        f_v, f_xs, f_up, f_gelu, f_hT, f_hTs, f_dn, f_dns, f_sq, f_sqr, l_in, l_sqrt, l_done, l_pool, f_out, f_fin = [sem("f_" + n) for n in (
            "v", "xs", "up", "gelu", "hT", "hTs", "dn", "dns", "sq", "sqr", "lin", "lsq", "ldone", "lpool", "out", "fin")]
        ps = [psum[:, i, :] for i in range(8)]
        LAG = 3
        block = ctx.enter_context(nc.Block())

        @block.sync
        def _(sp):
            for g in range(2):
                sp.wait_ge(f_fin, g + 1)
                c = slice(g * NT // 2, (g + 1) * NT // 2)
                sp.dma_start(m.out[:, c, :], m.acc[:, c, :]).then_inc(f_out, 16)
            sp.wait_ge(f_out, 32)

        @block.tensor
        def _(pe):
            for t in range(NT + 2):
                if t < NT:
                    if t >= 2:
                        pe.wait_ge(f_gelu, t - 1)
                    nc.tensor.matmul(ps[t % 2], lhsT=m.xn2T[:, t * P:(t + 1) * P], rhs=w[0][:, :], start=True, stop=True).then_inc(f_up, 1)
                if 1 <= t <= NT:
                    j = t - 1
                    pe.wait_ge(f_gelu, j + 1)
                    if j >= 2:
                        pe.wait_ge(f_hTs, j - 1)
                    for k in range(KC):
                        ins = nc.tensor.transpose(ps[2 + j % 2][:, k * P:(k + 1) * P], hh[:, j % 4, k * P:(k + 1) * P], m.ident[:, :])
                    ins.then_inc(f_hT, 1)
                if t >= 2:
                    j = t - 2
                    pe.wait_ge(f_hTs, j + 1)
                    if j >= 2:
                        pe.wait_ge(f_dns, j - 1)
                    for k in range(KC):
                        ins = nc.tensor.matmul(ps[4 + j % 2][:, 0:D], lhsT=hT[:, j % 2, k, :], rhs=w[1][:, k * P:(k + 1) * P], start=(k == 0), stop=(k == KC - 1))
                    ins.then_inc(f_dn, 1)

        @block.scalar
        def _(act):
            nc.scalar.activation(rx[:, :], m.ssx[:, :], ACT.Sqrt, scale=1.0 / D).then_inc(f_xs, 1)
            act.wait_ge(f_xs, 2)
            for t in range(NT + LAG):
                if t < NT:
                    act.wait_ge(f_up, t + 1)
                    if t >= 4:
                        act.wait_ge(f_hT, t - 3)
                        act.wait_ge(f_sq, t - 3)
                    nc.scalar.activation(hh[:, t % 4, :], ps[t % 2], ACT.Gelu, scale=rx[:, t:t + 1]).then_inc(f_gelu, 1)
                if t == 4:
                    act.wait_ge(l_in, 1)
                    nc.scalar.activation(r1[:, :], r1[:, :], ACT.Sqrt).then_inc(l_sqrt, 1)
                if t == NT:
                    act.wait_ge(f_sq, NT)
                    nc.scalar.activation(rh[:, :], ssh[:, :], ACT.Sqrt, scale=1.0 / FF).then_inc(f_sqr, 1)
                if t >= LAG:
                    act.wait_ge(f_dn, t - LAG + 1)
                    nc.scalar.copy(dn[:, t - LAG, :], ps[4 + (t - LAG) % 2][:, 0:D]).then_inc(f_dns, 1)

        @block.gpsimd
        def _(pool):
            for k, (a, b, op) in enumerate(((m.yatt, 0, ALU.mult), (m.yatt, 1, ALU.add))):
                pool.wait_ge(l_done, 1)
                if k:
                    pool.wait_ge(l_pool, k)
                nc.gpsimd.tensor_tensor(a, a, m.gb[:, b, :].unsqueeze(1).to_broadcast([P, NT, D]), op).then_inc(l_pool, 1)
            pool.wait_ge(l_pool, 2)
            nc.gpsimd.tensor_tensor(m.acc, m.acc, m.yatt, ALU.add).then_inc(l_pool, 1)

        @block.vector
        def _(dve):
            cnt = [0]

            def link(ins):
                cnt[0] += 1
                ins.then_inc(f_v, 1)
                dve.wait_ge(f_v, cnt[0])

            dve.wait_ge(f_xs, 1)
            link(nc.vector.tensor_scalar(rx[:, :], rx[:, :], EPS_T, None, ALU.add))
            nc.vector.reciprocal(rx[:, :], rx[:, :]).then_inc(f_xs, 1)
            for t in range(NT):
                ins = nc.vector.bn_stats(st6[:, t, :], m.yatt[:, t, :])
            link(ins)
            for t in range(NT):
                dve.wait_ge(f_hT, t + 1)
                if t >= 2:
                    dve.wait_ge(f_dn, t - 1)
                nc.vector.tensor_copy(hT[:, t % 2, :, :].rearrange("p k n -> p (k n)"), ps[2 + t % 2]).then_inc(f_hTs, 1)
                if t:
                    dve.wait_ge(f_sq, t)
                nc.vector.tensor_tensor_reduce(out=sq[:, :], in0=hh[:, t % 4, :], in1=hh[:, t % 4, :], scale=1.0, scalar=0.0,
                                               op0=ALU.mult, op1=ALU.add, accum_out=ssh[:, t:t + 1]).then_inc(f_sq, 1)
                if t == 1:
                    for u in range(NT):
                        ins = nc.vector.bn_aggr(mv[:, u, :], st6[:, u, :])
                    link(ins)
                    nc.vector.tensor_scalar(r1[:, :], mv[:, :, 1], EPS_LN2, None, ALU.add).then_inc(l_in, 1)
                if t == 5:
                    dve.wait_ge(l_sqrt, 1)
                    link(nc.vector.reciprocal(r1[:, :], r1[:, :]))
                if t in (6, 7, 8, 9):
                    for u in range(4 * (t - 6), 4 * (t - 5)):
                        ins = nc.vector.tensor_scalar(m.yatt[:, u, :], m.yatt[:, u, :], mv[:, u, 0:1], r1[:, u:u + 1], ALU.subtract, ALU.mult)
                    if t == 9:
                        ins.then_inc(l_done, 1)
            dve.wait_ge(f_sqr, 1)
            link(nc.vector.tensor_scalar(rh[:, :], rh[:, :], EPS_T, None, ALU.add))
            link(nc.vector.reciprocal(rh[:, :], rh[:, :]))
            dve.wait_ge(l_pool, 3)
            for t in range(NT):
                dve.wait_ge(f_dns, t + 1)
                ins = nc.vector.scalar_tensor_tensor(m.acc[:, t, :], dn[:, t, :], rh[:, t:t + 1], m.acc[:, t, :], ALU.mult, ALU.add)
                if t % (NT // 2) == NT // 2 - 1:
                    ins.then_inc(f_fin, 1)


def both_layers(nc, d, out):
    with ExitStack() as ctx:
        sb = lambda n, s, t=FP32: ctx.enter_context(nc.sbuf_tensor(n, s, t))
        psum = ctx.enter_context(nc.psum_tensor("psum", [P, 8, BLK], FP32))
        ps = [psum[:, i, :] for i in range(8)]
        m = Memory()
        m.out = out
        m.ident = sb("ident", [P, P])
        m.accx = sb("accx", [P, NT + 1, D])
        m.acc = m.accx[:, 1:NT + 1, :]
        m.one = sb("one", [P, 1])
        m.iota8 = sb("iota8", [P, E])
        m.wqkv = sb("wqkv", [P, 3, P])
        keep = sb("keep", [P, 3, T])
        m.xn2, m.yatt = [keep[:, i, :].rearrange("p (t h) -> p t h", h=D) for i in range(2)]
        m.xn2T = m.xnT = keep[:, 2, :]
        m.dA = keep[:, 0:2, :].rearrange("p a (b h t) -> p (a b) h t", h=DH, t=BLK)
        with ExitStack() as mamba:
            sb = lambda n, s, t=FP32: mamba.enter_context(nc.sbuf_tensor(n, s, t))
            dram = lambda n, s: nc.dram_tensor(n, s, FP32, kind="Internal").ap()
            m.Dp = sb("Dp", [P, DH])
            m.A = sb("A", [P, DH, STATE])
            m.dt = sb("dt", [P, DH, T])
            m.u_mem = sb("u", [P, DH * B * (KW - 1 + S)])
            m.u = m.u_mem[:, 0:DH * T].rearrange("p (h t) -> p h t", h=DH)
            m.PT = sb("PT", [P, UNITS * B * 2 + 1, BLK], BF16)
            m.sel = sb("sel", [96, 2, UN, P], BF16)
            m.zeros = sb("zeros", [P, BLK], BF16)
            m.wT = [sb("w_gT", [P, E, FF]), sb("w_uT", [P, E, FF])]
            m.w_dnT = sb("w_dnT", [P, KC, E, D])
            m.w_rdT = sb("w_rdT", [P, KC, E])
            m.w_oT = sb("w_oT", [P, DH, D])
            m.xc_dram, m.sz_dram = dram("xc_dram", (P, DH, T)), dram("sz_dram", (P, DH, T))
            m.comb_dram = dram("comb_dram", (NT + 1, 2 * E, P))
            prepare(nc, d, m, ps)
            m.xc_back, m.sz_back = [w[:, :, :].rearrange("p a n -> p (a n)").rearrange("p (h t) -> p h t", h=DH) for w in m.wT]
            scan_and_experts(nc, d, m, ps)
        sb = lambda n, s, t=FP32: ctx.enter_context(nc.sbuf_tensor(n, s, t))
        m.tw = [sb("t_wu", [P, FF]), sb("t_wd", [P, FF])]
        m.gb = sb("t_gb", [P, 2, D])
        m.ssx = sb("t_ssx", [P, NT])
        attention(nc, d, m, psum)
        ternary_and_last(nc, d, m, psum)


def layout(i):
    bf16 = mybir.dt.np(BF16)
    c = np.ascontiguousarray
    half = lambda w: w.reshape(DH, P, -1).transpose(1, 0, 2)
    o = {}
    o["x"] = c(i["L0_attn_x"].reshape(NT, P, D).transpose(1, 0, 2))
    o["vec"] = c(np.concatenate([i["L0_attn_norm_w"].reshape(P, 1), half(i["L0_attn_conv_b"].reshape(INNER, 1)).reshape(P, -1),
                                 half(i["L0_attn_dt_b"].reshape(INNER, 1)).reshape(P, -1), half(i["L0_attn_D_param"].reshape(INNER, 1)).reshape(P, -1),
                                 half(i["L0_attn_conv_w"].reshape(INNER, KW)).reshape(P, -1), half(i["L0_attn_A_log"]).reshape(P, -1)], axis=1))
    o["w_inT"] = c(i["L0_attn_in_proj_w"].T)
    o["w_bcT"] = c(half(np.concatenate([i["L0_attn_B_w"], i["L0_attn_C_w"]], axis=0).T))
    o["w_dtT"] = c(half(i["L0_attn_dt_w"].T))
    o["w_oT"] = c(half(i["L0_attn_out_proj_w"].T))
    o["w_rT"] = c(np.concatenate([i["L0_ffn_router_gate"], i["L0_ffn_router_up"]], axis=0).T)
    o["w_rdT"] = c(i["L0_ffn_router_down"].T.reshape(KC, P, E).transpose(1, 0, 2))
    o["w_gT"] = c(i["L0_ffn_w_gate"].transpose(2, 0, 1))
    o["w_uT"] = c(i["L0_ffn_w_up"].transpose(2, 0, 1))
    o["w_dnT"] = c(i["L0_ffn_w_down"].transpose(2, 0, 1).reshape(KC, P, E, D).transpose(1, 0, 2, 3))
    pairs = lambda w: w.reshape(HP, 2, D, HS).transpose(0, 2, 1, 3).reshape(HP, D, P)
    w = np.stack([pairs(i["L1_attn_" + n]) for n in ("Wq", "Wk", "Wv")], axis=2)
    o["wqkv"] = c(np.concatenate([w, np.zeros_like(w[:1])], axis=0))
    o["wo"] = c(i["L1_attn_Wo"].reshape(HP, P, D).transpose(1, 0, 2))
    o["gamma"], o["beta"] = i["L1_attn_gamma"].reshape(1, D), i["L1_attn_beta"].reshape(1, D)
    o["t_upT"] = c(i["L1_ffn_w_up"].T)
    o["t_dnT"] = c(i["L1_ffn_w_down"].T.reshape(KC, P, D).transpose(1, 0, 2).reshape(P, FF))
    o["half_mean"] = np.full((P, P), 0.5 / (FF * D), np.float32)
    o["maskb"] = np.where(np.tril(np.ones((P, P))) > 0, 0.0, NEG).astype(bf16)
    o["ident"] = np.eye(P, dtype=np.float32)
    o["iota8"] = c(np.broadcast_to(np.arange(E, dtype=np.float32), (P, E)))
    sel = np.zeros((2, 3, UN, 2, UN, P), np.float32)
    for q in range(2):
        for s in range(UN):
            sel[q, :, s, q, s, :] = 1.0
    o["sel"] = sel.reshape(96, 2, UN, P).astype(bf16)
    return o


INPUTS = ["x", "vec", "w_inT", "w_bcT", "w_dtT", "w_oT", "w_rT", "w_rdT", "w_gT", "w_uT", "w_dnT", "wqkv", "wo", "gamma", "beta",
          "t_upT", "t_dnT", "half_mean", "maskb", "ident", "iota8", "sel"]


def kernel(**inputs):
    import concourse.bacc as bacc
    from concourse.bass_utils import run_bass_kernel_spmd

    arrays = layout({k: np.asarray(v) for k, v in inputs.items()})
    nc = bacc.Bacc("TRN2", target_bir_lowering=False, num_devices=1)
    d = namedtuple("Inputs", INPUTS)(*[nc.dram_tensor("in_" + n, arrays[n].shape, mybir.dt.from_np(arrays[n].dtype), kind="ExternalInput").ap()
                                       for n in INPUTS])
    out = nc.dram_tensor("out", (P, NT, D), FP32, kind="ExternalOutput").ap()
    both_layers(nc, d, out)
    r = run_bass_kernel_spmd(nc, [{"in_" + n: arrays[n] for n in INPUTS}], core_ids=[0])
    return r.results[0]["out"].transpose(1, 0, 2).reshape(B, S, D)
```
